# Optimizing a Trainium2 kernel written in Bass

```python
import numpy as np
import jax
import jax.numpy as jnp

def _softmax(x, axis=-1):
    return jax.nn.softmax(x, axis=axis)

def _gelu(x):
    return jax.nn.gelu(x, approximate=True)

def _silu(x):
    return jax.nn.silu(x)

def _sigmoid(x):
    return jax.nn.sigmoid(x)

def _layernorm(x, axis=-1, eps=1e-05):
    m = jnp.mean(x, axis=axis, keepdims=True)
    v = jnp.var(x, axis=axis, keepdims=True)
    return (x - m) / jnp.sqrt(v + eps)

def _scatter_add(tgt, idx, src, axis=0):
    return tgt.at[idx].add(src)

def _segment_sum(src, seg, n):
    return jax.ops.segment_sum(src, seg, n)
kernel_name = 'mk_seq_preln_d1_jaxref_r8_117a78'

def setup_inputs(seed: int=0):
    np.random.seed(seed)
    _w = jnp.asarray

    def _L0_attn_setup():
        import jax, jax.numpy as jnp
        import numpy as np
        import math
        D_MODEL = 128
        D_STATE = 16
        EXPAND = 2
        D_CONV = 4
        D_INNER = EXPAND * D_MODEL
        DT_RANK = math.ceil(D_MODEL / 16)
        B_SZ, L_SEQ = (2, 256)

        def _layernorm(x, g, b, eps=1e-05):
            mu = jnp.mean(x, -1, keepdims=True)
            var = jnp.var(x, -1, keepdims=True)
            return (x - mu) * jax.lax.rsqrt(var + eps) * g + b

        def _causal_depthwise_conv(x, w, b):
            K = w.shape[1]
            xp = jnp.pad(x, ((0, 0), (K - 1, 0), (0, 0)))
            L = x.shape[1]
            y = sum((xp[:, k:k + L, :] * w[:, k] for k in range(K)))
            return y + b

        def _selective_scan(u, dt, A, Bm, Cm, D):
            dA = jnp.exp(dt[..., None] * A)
            dBu = (dt * u)[..., None] * Bm[:, :, None, :]

            def combine(e1, e2):
                a1, b1 = e1
                a2, b2 = e2
                return (a2 * a1, a2 * b1 + b2)
            _, h = jax.lax.associative_scan(combine, (dA, dBu), axis=1)
            y = jnp.einsum('blds,bls->bld', h, Cm)
            return y + u * D

        def _mamba(x, in_proj_w, conv_w, conv_b, x_proj_w, dt_proj_w, dt_proj_b, A_log, D, out_proj_w):
            xz = jnp.einsum('bld,ed->ble', x, in_proj_w)
            xin, z = jnp.split(xz, 2, axis=-1)
            xc = jax.nn.silu(_causal_depthwise_conv(xin, conv_w, conv_b))
            dbl = jnp.einsum('bld,ed->ble', xc, x_proj_w)
            dt, Bm, Cm = jnp.split(dbl, [DT_RANK, DT_RANK + D_STATE], axis=-1)
            dt = jax.nn.softplus(jnp.einsum('blr,dr->bld', dt, dt_proj_w) + dt_proj_b)
            A = -jnp.exp(A_log)
            y = _selective_scan(xc, dt, A, Bm, Cm, D)
            y = y * jax.nn.silu(z)
            return jnp.einsum('bld,ed->ble', y, out_proj_w)
        key = jax.random.key(seed)
        ks = jax.random.split(key, 10)
        s = 0.02
        inp = {'x': jax.random.normal(ks[0], (B_SZ, L_SEQ, D_MODEL), jnp.float32), 'ln_gamma': jnp.ones((D_MODEL,), jnp.float32), 'ln_beta': jnp.zeros((D_MODEL,), jnp.float32), 'in_proj_w': jax.random.normal(ks[1], (2 * D_INNER, D_MODEL), jnp.float32) * s, 'conv_w': jax.random.normal(ks[2], (D_INNER, D_CONV), jnp.float32) * s, 'conv_b': jnp.zeros((D_INNER,), jnp.float32), 'x_proj_w': jax.random.normal(ks[3], (DT_RANK + 2 * D_STATE, D_INNER), jnp.float32) * s, 'dt_proj_w': jax.random.normal(ks[4], (D_INNER, DT_RANK), jnp.float32) * DT_RANK ** (-0.5), 'dt_proj_b': jnp.full((D_INNER,), float(np.log(np.expm1(0.01))), jnp.float32), 'A_log': jnp.log(jnp.broadcast_to(jnp.arange(1, D_STATE + 1, dtype=jnp.float32), (D_INNER, D_STATE))), 'D': jnp.ones((D_INNER,), jnp.float32), 'out_proj_w': jax.random.normal(ks[5], (D_MODEL, D_INNER), jnp.float32) * s}
        return inp
    _L0_attn_in = _L0_attn_setup()

    def _L0_ffn_setup():
        import jax, jax.numpy as jnp
        import numpy as np
        E, D, F = (8, 128, 512)
        LN_EPS = 1e-05
        key = jax.random.key(seed)
        k = jax.random.split(key, 8)
        x = jax.random.normal(k[0], (4, 256, D), jnp.float32)
        centroids = jax.random.normal(k[1], (E, D), jnp.float32) * 0.1
        ln_g = jnp.ones((E, D), jnp.float32)
        ln_b = jnp.zeros((E, D), jnp.float32)
        w1 = jax.random.normal(k[2], (E, F, D), jnp.float32) * (1.0 / np.sqrt(D))
        b1 = jnp.zeros((E, F), jnp.float32)
        w2 = jax.random.normal(k[3], (E, D, F), jnp.float32) * (1.0 / np.sqrt(F))
        b2 = jnp.zeros((E, D), jnp.float32)
        return {'input_features': x, 'centroids': centroids, 'ln_g': ln_g, 'ln_b': ln_b, 'w1': w1, 'b1': b1, 'w2': w2, 'b2': b2}
    _L0_ffn_in = _L0_ffn_setup()
    _d = {'L0_attn_x': _L0_attn_in['x'], 'L0_attn_ln_gamma': _L0_attn_in['ln_gamma'], 'L0_attn_ln_beta': _L0_attn_in['ln_beta'], 'L0_attn_in_proj_w': _L0_attn_in['in_proj_w'], 'L0_attn_conv_w': _L0_attn_in['conv_w'], 'L0_attn_conv_b': _L0_attn_in['conv_b'], 'L0_attn_x_proj_w': _L0_attn_in['x_proj_w'], 'L0_attn_dt_proj_w': _L0_attn_in['dt_proj_w'], 'L0_attn_dt_proj_b': _L0_attn_in['dt_proj_b'], 'L0_attn_A_log': _L0_attn_in['A_log'], 'L0_attn_D': _L0_attn_in['D'], 'L0_attn_out_proj_w': _L0_attn_in['out_proj_w'], 'L0_ffn_centroids': _L0_ffn_in['centroids'], 'L0_ffn_ln_g': _L0_ffn_in['ln_g'], 'L0_ffn_ln_b': _L0_ffn_in['ln_b'], 'L0_ffn_w1': _L0_ffn_in['w1'], 'L0_ffn_b1': _L0_ffn_in['b1'], 'L0_ffn_w2': _L0_ffn_in['w2'], 'L0_ffn_b2': _L0_ffn_in['b2']}
    _x0 = _d['L0_attn_x']
    _d['L0_attn_x'] = jax.random.normal(jax.random.fold_in(jax.random.key(seed), 1), (4, 512, 128), dtype=_x0.dtype)
    del _x0
    return _d

def reference(L0_attn_x, L0_attn_ln_gamma, L0_attn_ln_beta, L0_attn_in_proj_w, L0_attn_conv_w, L0_attn_conv_b, L0_attn_x_proj_w, L0_attn_dt_proj_w, L0_attn_dt_proj_b, L0_attn_A_log, L0_attn_D, L0_attn_out_proj_w, L0_ffn_centroids, L0_ffn_ln_g, L0_ffn_ln_b, L0_ffn_w1, L0_ffn_b1, L0_ffn_w2, L0_ffn_b2):

    def _L0_attn_ref(x, ln_gamma, ln_beta, in_proj_w, conv_w, conv_b, x_proj_w, dt_proj_w, dt_proj_b, A_log, D, out_proj_w):
        import jax, jax.numpy as jnp
        import numpy as np
        import math
        D_MODEL = 128
        D_STATE = 16
        EXPAND = 2
        D_CONV = 4
        D_INNER = EXPAND * D_MODEL
        DT_RANK = math.ceil(D_MODEL / 16)
        B_SZ, L_SEQ = (2, 256)

        def _layernorm(x, g, b, eps=1e-05):
            mu = jnp.mean(x, -1, keepdims=True)
            var = jnp.var(x, -1, keepdims=True)
            return (x - mu) * jax.lax.rsqrt(var + eps) * g + b

        def _causal_depthwise_conv(x, w, b):
            K = w.shape[1]
            xp = jnp.pad(x, ((0, 0), (K - 1, 0), (0, 0)))
            L = x.shape[1]
            y = sum((xp[:, k:k + L, :] * w[:, k] for k in range(K)))
            return y + b

        def _selective_scan(u, dt, A, Bm, Cm, D):
            dA = jnp.exp(dt[..., None] * A)
            dBu = (dt * u)[..., None] * Bm[:, :, None, :]

            def combine(e1, e2):
                a1, b1 = e1
                a2, b2 = e2
                return (a2 * a1, a2 * b1 + b2)
            _, h = jax.lax.associative_scan(combine, (dA, dBu), axis=1)
            y = jnp.einsum('blds,bls->bld', h, Cm)
            return y + u * D

        def _mamba(x, in_proj_w, conv_w, conv_b, x_proj_w, dt_proj_w, dt_proj_b, A_log, D, out_proj_w):
            xz = jnp.einsum('bld,ed->ble', x, in_proj_w)
            xin, z = jnp.split(xz, 2, axis=-1)
            xc = jax.nn.silu(_causal_depthwise_conv(xin, conv_w, conv_b))
            dbl = jnp.einsum('bld,ed->ble', xc, x_proj_w)
            dt, Bm, Cm = jnp.split(dbl, [DT_RANK, DT_RANK + D_STATE], axis=-1)
            dt = jax.nn.softplus(jnp.einsum('blr,dr->bld', dt, dt_proj_w) + dt_proj_b)
            A = -jnp.exp(A_log)
            y = _selective_scan(xc, dt, A, Bm, Cm, D)
            y = y * jax.nn.silu(z)
            return jnp.einsum('bld,ed->ble', y, out_proj_w)
        h = _layernorm(x, ln_gamma, ln_beta)
        return x + _mamba(h, in_proj_w, conv_w, conv_b, x_proj_w, dt_proj_w, dt_proj_b, A_log, D, out_proj_w)

    def _L0_ffn_ref(input_features, centroids, ln_g, ln_b, w1, b1, w2, b2):
        import jax, jax.numpy as jnp
        import numpy as np
        E, D, F = (8, 128, 512)
        LN_EPS = 1e-05
        x = input_features.reshape(-1, D)
        aff = jax.lax.stop_gradient(x) @ centroids.T
        assign = jnp.argmax(aff, axis=1)
        onehot = jax.nn.one_hot(assign, E, dtype=x.dtype)
        mu = jnp.mean(x, axis=-1, keepdims=True)
        var = jnp.mean((x - mu) ** 2, axis=-1, keepdims=True)
        xhat = (x - mu) * jax.lax.rsqrt(var + LN_EPS)
        xn = xhat[None, :, :] * ln_g[:, None, :] + ln_b[:, None, :]
        h = jax.nn.relu(jnp.einsum('etd,efd->etf', xn, w1) + b1[:, None, :])
        y = x[None, :, :] + jnp.einsum('etf,edf->etd', h, w2) + b2[:, None, :]
        alpha = jax.nn.sigmoid(x @ centroids.T)
        a = alpha.T[:, :, None]
        gated = a * y + (1.0 - a) * x[None, :, :]
        out = jnp.einsum('te,etd->td', onehot, gated)
        return out.reshape(input_features.shape)
    x = L0_attn_x
    x = x + _L0_attn_ref(_layernorm(x, axis=-1), L0_attn_ln_gamma, L0_attn_ln_beta, L0_attn_in_proj_w, L0_attn_conv_w, L0_attn_conv_b, L0_attn_x_proj_w, L0_attn_dt_proj_w, L0_attn_dt_proj_b, L0_attn_A_log, L0_attn_D, L0_attn_out_proj_w)
    x = x + _L0_ffn_ref(_layernorm(x, axis=-1), L0_ffn_centroids, L0_ffn_ln_g, L0_ffn_ln_b, L0_ffn_w1, L0_ffn_b1, L0_ffn_w2, L0_ffn_b2)
    return x

_drawn_inputs = setup_inputs


def setup_inputs(seed=0):
    import zlib

    import numpy as np

    out = dict(_drawn_inputs(seed))
    spreads = {'L0_attn_ln_gamma': (1.0, 0.6),
     'L0_attn_ln_beta': (0.0, 0.8),
     'L0_attn_conv_b': (0.0, 0.8),
     'L0_attn_dt_proj_b': (-4.600165843963623, 0.6),
     'L0_attn_D': (1.0, 0.6),
     'L0_ffn_ln_g': (1.0, 0.6),
     'L0_ffn_ln_b': (0.0, 2.0),
     'L0_ffn_b1': (0.0, 2.0),
     'L0_ffn_b2': (0.0, 2.0)}
    factors = {'L0_attn_in_proj_w': 8.0,
     'L0_attn_conv_w': 8.0,
     'L0_attn_x_proj_w': 8.0,
     'L0_attn_dt_proj_w': 8.0,
     'L0_attn_A_log': 8.0,
     'L0_attn_out_proj_w': 8.0,
     'L0_ffn_centroids': 8.0,
     'L0_ffn_w1': 8.0,
     'L0_ffn_w2': 8.0}
    for name, (base, spread) in spreads.items():
        noise = np.random.default_rng([zlib.crc32(name.encode()), seed]).standard_normal(out[name].shape)
        drawn = base * np.exp(spread * noise) if base else spread * noise
        out[name] = jnp.asarray(drawn.astype(out[name].dtype))
    for name, factor in factors.items():
        out[name] = (out[name] * factor).astype(out[name].dtype)
    return out
```

```python
from contextlib import ExitStack

import concourse.bass as bass
from concourse import mybir

ALU = mybir.AluOpType
ACT = mybir.ActivationFunctionType
AX = mybir.AxisListType
F32 = mybir.dt.float32
BF16 = mybir.dt.bfloat16
EPS = 1e-5
P = 128


def build(nc, x, ln_gamma, ln_beta, in_proj_w, conv_w, conv_b, x_proj_w, dt_proj_w, dt_proj_b, A_log, D,
          out_proj_w, centroids, ln_g, ln_b, w1, b1, w2, b2, out):
    B, L, DM = x.shape
    DI, NS = A_log.shape
    R = dt_proj_w.shape[1]
    K = conv_w.shape[1]
    E, F, _ = w1.shape
    TB = L // P
    NC = DI // P
    NF = F // P
    BC = 2 * NS
    PADL = K - 1
    assert DM == P and L == 512 and NS == 16

    rows, n_rows = {}, 0
    for name, count in (("gamma", 1), ("beta", 1), ("conv_b", NC), ("dt_b", NC), ("D", NC), ("ln_g", E),
                        ("ln_b", E), ("b1", E * NF), ("cent", E)):
        rows[name] = n_rows
        n_rows += count

    ctx = ExitStack()
    with ctx:
        def sb(name, shape, dt=F32):
            return ctx.enter_context(nc.sbuf_tensor(name, shape, dt))

        def ps(name, shape, dt=F32):
            return ctx.enter_context(nc.psum_tensor(name, shape, dt))

        def sem(name):
            return ctx.enter_context(nc.semaphore(name))

        vec_rows = sb("vec_rows", [n_rows, P])
        win_raw = sb("win_raw", [P, 2 * NC, DM])
        xp_raw = sb("xp_raw", [R + BC, DI])
        dtw_raw = sb("dtw_raw", [P, NC, R])
        wo_raw = sb("wo_raw", [P, DI])
        w1_raw = sb("w1_raw", [P, E * NF, DM])
        w2_raw = sb("w2_raw", [P, E, F])
        convw = sb("convw", [P, NC, K])
        alog = sb("alog", [P, NC, NS])
        b2_sb = sb("b2_sb", [E, DM])
        ident = sb("ident", [P, P])
        pick32 = sb("pick32", [3 * BC, BC])
        pick = sb("pick", [3 * BC, BC, P], BF16)
        vec = sb("vec", [P, n_rows])
        nconvb = sb("nconvb", [P, NC])
        Aneg = sb("Aneg", [P, NC, NS])
        winT = sb("winT", [P, NC, K, P])
        wzT = sb("wzT", [P, DI])
        xpT = sb("xpT", [P, NC, 3 * BC + R])
        dtwT = sb("dtwT", [P, NC, P])
        woT = sb("woT", [P, NC, DM])
        w1T = w1_raw[:, :, :].rearrange("p (e j) d -> p e (j d)", e=E)
        w2T = w2_raw[:, :, :].rearrange("p e (j d) -> p e j d", j=NF)
        b1c = sb("b1c", [P, E * NF])
        firstw = sb("firstw", [P, TB, E])

        xt = [sb(f"xt{i}", [P, TB, DM]) for i in range(2)]
        bst = sb("bst", [P, TB, 6])
        mv = sb("mv", [P, TB, 2])
        vv = sb("vv", [P, 2, TB])
        rs = sb("rs", [P, 2, TB])
        lny = sb("lny", [P, 2, TB])
        yy = sb("yy", [P, 2, TB])
        sc1 = sb("sc1", [P, TB])
        sc2 = sb("sc2", [P, TB])
        xh = sb("xh", [P, TB, DM])
        xres = [sb(f"xres{i}", [P, TB, DM]) for i in range(2)]
        hT = sb("hT", [P, PADL + L])
        eu = sb("eu", [P, NC, L])
        u = sb("u", [P, NC, L])
        uD = [sb(f"uD{i}", [P, NC, L]) for i in range(2)]
        ez = sb("ez", [P, TB, DI])
        zs = [sb(f"zs{i}", [P, TB, DI]) for i in range(2)]
        parts = [sb(f"parts{i}", [3 * BC, L], BF16) for i in range(2)]
        rest = sb("rest", [3 * BC, L])
        dtlow = sb("dtlow", [P, L])
        av = sb("av", [P, NC, L])
        rv = sb("rv", [P, NC, L])
        zz = av
        ww = sb("ww", [P, NC, L])
        lw = sb("lw", [P, NC, L])
        sp = lw
        dt = [sb(f"dt{i}", [P, NC, L]) for i in range(2)]
        dtu = [sb(f"dtu{i}", [P, NC, L]) for i in range(2)]
        dA = [sb(f"dA{i}", [P, NC, L]) for i in range(2)]
        dBu = [sb(f"dBu{i}", [P, NC, L]) for i in range(2)]
        hs = [sb(f"hs{i}", [P, NC, L]) for i in range(2)]
        hC = [sb(f"hC{i}", [P, NC, L]) for i in range(2)]
        Cb = [sb(f"Cb{i}", [P, L]) for i in range(2)]
        yz = sb("yz", [P, TB, DI])
        win_tap = yz[:, :, :].rearrange("p j (a m) -> p (j a m)", m=P).rearrange("p (c k m) -> p c k m", c=NC, k=K)
        yzT = sb("yzT", [P, NC, L])
        x1 = sb("x1", [P, TB, DM])
        bst2 = sb("bst2", [P, TB, 6])
        mv2 = sb("mv2", [P, TB, 2])
        vv2 = sb("vv2", [P, 2, TB])
        rs2 = sb("rs2", [P, 2, TB])
        yy2 = sb("yy2", [P, 2, TB])
        nr = sb("nr", [P, 3, TB])
        xe = sb("xe", [P, TB, DM])
        xeT = sb("xeT", [P, L])
        base = [sb(f"base{i}", [P, TB, DM]) for i in range(2)]
        aff = sb("aff", [P, TB, E])
        score = sb("score", [P, TB, E])
        mx = sb("mx", [P, TB])
        mx2 = sb("mx2", [P, TB])
        gex = sb("gex", [P, TB])
        gate = sb("gate", [P, TB])
        hot = sb("hot", [P, TB, E])
        hotT = sb("hotT", [E, L])
        hid = sb("hid", [P, NF, L])
        acc = [sb(f"acc{i}", [P, TB, DM]) for i in range(2)]
        res = acc

        psB = ps("psB", [P, L])
        psC = ps("psC", [P, L])
        psY = ps("psY", [P, TB, DI])
        psF = [ps(f"psF{i}", [P, 512]) for i in range(2)]
        psU = ps("psU", [P, 512])
        psD = ps("psD", [P, 512])

        S = {}
        for name in """vec_in win_in convw_in xp_in dtw_in wo_in alog_in b2_in w1_in w2_in
                ident_ok pick_ok pads_ok firstw_ok vecT_mm vec_ok nconvb_ok tap_ok win_mm win_ok small_mm small_ok
                aexp_ok aneg_ok w1_mm w1_ok w2_mm w2_ok b1_mm b1_ok w1g_ok
                stat_ok xh_ok xres_ok hT_mm hT_ok conv_mm eu_ok u_ok uD_ok z_mm ez_ok zs_ok xp_mm parts_ok
                dtlow_ok dt_mm av_ok rv_ok zz_ok ww_ok lw_ok nc_ok sp_ok dt_ok dtu_ok
                Bb_mm dBu_ok Cb_mm Cb_ok dA_ok h_ok hC_ok sum_mm
                yz_ok yzT_mm yzT_ok op_mm x1_ok nr_ok xe_ok base_ok xeT_mm xeT_ok aff_mm mx_ok gex_ok hot_ok
                hotT_mm hotT_ok b2_mm acc0_ok up_mm hid_ok down_mm mix_ok res_ok
                vv_ok y_ok vv2_ok y2_ok lny_ok dve_chain""".split():
            S[name] = sem(name)

        x_in = [sem(f"x_in{b}") for b in range(B)]
        stored = [sem(f"stored{b}") for b in range(B)]

        def col(name, i=0):
            return vec[:, rows[name] + i:rows[name] + i + 1]

        HALVES = E * NF // 2 + 1

        def halves(s):
            at, slots = s - 5, NS - 5
            return range(HALVES * at // slots, HALVES * (at + 1) // slots) if at >= 0 else range(0)

        block = ctx.enter_context(nc.Block())

        @block.sync
        def _(sp_):
            def load_x(b):
                if b >= 2:
                    sp_.wait_ge(S["xh_ok"], b - 1)
                    sp_.wait_ge(S["xres_ok"], b - 1)
                sp_.dma_start(xt[b % 2][:, :, :], x[b].rearrange("(j p) d -> p j d", p=P)).then_inc(x_in[b], 16)

            load_x(0)
            one = [("gamma", ln_gamma), ("beta", ln_beta), ("conv_b", conv_b), ("dt_b", dt_proj_b), ("D", D)]
            for name, v in one:
                n = v.shape[0] // P
                sp_.dma_start(vec_rows[rows[name]:rows[name] + n, :], v.rearrange("(a n) -> a n", n=P))\
                   .then_inc(S["vec_in"], 16)
            for name, v in (("ln_g", ln_g), ("ln_b", ln_b), ("cent", centroids)):
                sp_.dma_start(vec_rows[rows[name]:rows[name] + E, :], v).then_inc(S["vec_in"], 16)
            sp_.dma_start(vec_rows[rows["b1"]:rows["b1"] + E * NF, :], b1.rearrange("e (j n) -> (e j) n", n=P))\
               .then_inc(S["vec_in"], 16)
            load_x(1)
            for e in range(E):
                sp_.dma_start(w1_raw[:, e * NF:(e + 1) * NF, :], w1[e].rearrange("(j p) d -> p j d", p=P))\
                   .then_inc(S["w1_in"], 16)
                sp_.dma_start(w2_raw[:, e, :], w2[e]).then_inc(S["w2_in"], 16)
            load_x(2)
            load_x(3)
            for b in range(B):
                sp_.wait_ge(S["res_ok"], b + 1)
                sp_.dma_start(out[b].rearrange("(j p) d -> p j d", p=P), res[b % 2][:, :, :])\
                   .then_inc(stored[b], 16)
            for b in range(B):
                sp_.wait_ge(stored[b], 16)

        @block.tensor
        def _(pe):
            def turn_weights_0():
                pe.wait_ge(S["ident_ok"], 2)
                pe.wait_ge(S["vec_in"], 16 * 9)
                pe.transpose(psF[0][:, 0:n_rows], vec_rows[:, :], ident[0:n_rows, 0:n_rows])\
                  .then_inc(S["vecT_mm"], 1)
                for c in range(NC):
                    pe.wait_ge(S["tap_ok"], K * (c + 1))
                    bank = (psU, psD)[c]
                    for k in range(K):
                        t = pe.transpose(bank[:, k * P:(k + 1) * P], win_tap[:, c, k, :], ident[:, :])
                    t.then_inc(S["win_mm"], 1)
                for c in range(NC):
                    t = pe.transpose(psF[1][:, c * P:(c + 1) * P], win_raw[:, NC + c, :], ident[:, :])
                t.then_inc(S["win_mm"], 1)
                pe.wait_ge(S["xp_in"], 16)
                pe.wait_ge(S["dtw_in"], 16)
                pe.wait_ge(S["wo_in"], 16)
                pe.wait_ge(S["vec_ok"], 1)
                pe.wait_ge(S["win_ok"], 1)
                for c in range(NC):
                    pe.transpose(psF[0][:, c * 64:c * 64 + R + BC], xp_raw[:, c * P:(c + 1) * P],
                                 ident[0:R + BC, 0:R + BC])
                    pe.transpose(psU[0:R, c * P:(c + 1) * P], dtw_raw[:, c, :], ident[:, :])
                for c in range(NC):
                    t = pe.transpose(psF[0][:, 128 + c * P:128 + (c + 1) * P], wo_raw[:, c * P:(c + 1) * P],
                                     ident[:, :])
                t.then_inc(S["small_mm"], 1)

            def turn_expert(e):
                pe.wait_ge(S["w1_in"], 16 * E)
                pe.wait_ge(S["w2_in"], 16 * E)
                if e == 0:
                    pe.wait_ge(S["small_ok"], 4)
                    pe.wait_ge(S["win_ok"], 2)
                else:
                    pe.wait_ge(S["w1_ok"], e)
                for j in range(NF):
                    t = pe.transpose(psU[:, j * P:(j + 1) * P], w1_raw[:, e * NF + j, :], ident[:, :])
                t.then_inc(S["w1_mm"], 1)
                if e:
                    pe.wait_ge(S["w2_ok"], e)
                for j in range(NF):
                    t = pe.transpose(psD[:, j * P:(j + 1) * P], w2_raw[:, e, j * P:(j + 1) * P], ident[:, :])
                t.then_inc(S["w2_mm"], 1)

            def b1_shift():
                pe.wait_ge(S["w1_ok"], E)
                for e in range(E):
                    for j in range(NF):
                        i = e * NF + j
                        t = pe.matmul(psU[:, i:i + 1], w1T[:, e, j * P:(j + 1) * P], col("ln_b", e),
                                      start=True, stop=True)
                t.then_inc(S["b1_mm"], 1)

            def front_turn(b):
                if b == 0:
                    pe.wait_ge(S["win_ok"], 3)
                else:
                    if b >= 2:
                        pe.wait_ge(S["hotT_ok"], b - 1)
                    else:
                        pe.wait_ge(S["rv_ok"], 2 * b)
                        pe.wait_ge(S["av_ok"], 2 * b)
                pe.wait_ge(S["xh_ok"], b + 1)
                for j in range(TB):
                    t = pe.transpose(psF[1][:, j * P:(j + 1) * P], xh[:, j, :], ident[:, :])
                t.then_inc(S["hT_mm"], 1)

            def front_conv(b):
                pe.wait_ge(S["hT_ok"], b + 1)
                if b == 0:
                    pe.wait_ge(S["small_ok"], 4)
                    pe.wait_ge(S["pads_ok"], 1)
                elif b >= 2:
                    pe.wait_ge(S["acc0_ok"], b - 1)
                else:
                    pe.wait_ge(S["rv_ok"], 2 * b)
                    pe.wait_ge(S["av_ok"], 2 * b)
                for c in range(NC):
                    for k in range(K):
                        t = pe.matmul(psF[c][:, :], winT[:, c, k, :], hT[:, k:k + L], start=(k == 0), stop=(k == K - 1))
                    t.then_inc(S["conv_mm"], 1)

            def front_z(b):
                for i in range(2):
                    pe.wait_ge(S["u_ok"], 2 * b + i + 1)
                    for j in range(2):
                        t = pe.matmul(psF[i][:, j * DI:(j + 1) * DI],
                                      hT[:, PADL + (2 * i + j) * P:PADL + (2 * i + j + 1) * P], wzT[:, :],
                                      start=True, stop=True)
                    t.then_inc(S["z_mm"], 1)

            def front_xproj(b):
                pe.wait_ge(S["zs_ok"], 2 * b + 1)
                for c in range(NC):
                    t = pe.matmul(psF[0][0:3 * BC + R, :], xpT[:, c, :], u[:, c, :], start=(c == 0), stop=(c == NC - 1))
                t.then_inc(S["xp_mm"], 1)

            def front_dt(b):
                pe.wait_ge(S["dtlow_ok"], b + 1)
                pe.wait_ge(S["parts_ok"], b + 1)
                pe.wait_ge(S["zs_ok"], 2 * b + 2)
                for c in range(NC):
                    pe.matmul(psF[c][:, :], dtwT[3 * BC:3 * BC + R, c, :], dtlow[3 * BC:3 * BC + R, :],
                              start=True, stop=True).then_inc(S["dt_mm"], 1)

            def spread_B(n):
                b, s = divmod(n, NS)
                pe.wait_ge(S["parts_ok"], b + 1)
                if n:
                    pe.wait_ge(S["dBu_ok"], n)
                pe.matmul(psB[:, :], pick[:, s, :], parts[b % 2][:, :], start=True, stop=True)\
                  .then_inc(S["Bb_mm"], 1)

            def spread_C(n):
                b, s = divmod(n, NS)
                if n:
                    pe.wait_ge(S["Cb_ok"], n)
                pe.matmul(psC[:, :], pick[:, NS + s, :], parts[b % 2][:, :], start=True, stop=True)\
                  .then_inc(S["Cb_mm"], 1)

            def add_up(src, first):
                for j in range(TB):
                    for c in range(NC):
                        t = pe.matmul(psY[:, j, c * P:(c + 1) * P], src[:, c, j * P:(j + 1) * P], ident[:, :],
                                      start=first and j % 2 == 0 and c == 0, stop=True, is_transpose=True,
                                      skip_group_check=True)
                return t

            def sum_state(n):
                b, s = divmod(n, NS)
                if s == 0:
                    if b:
                        pe.wait_ge(S["yz_ok"], b)
                    pe.wait_ge(S["uD_ok"], 2 * b + 2)
                    add_up(uD[b % 2], True)
                pe.wait_ge(S["hC_ok"], n + 1)
                add_up(hC[n % 2], False).then_inc(S["sum_mm"], 1)

            def tail_turn(b):
                pe.wait_ge(S["yz_ok"], b + 1)
                nb = min(b + 2, B)
                pe.wait_ge(S["rv_ok"], 2 * nb)
                pe.wait_ge(S["av_ok"], 2 * nb)
                for c in range(NC):
                    for j in range(TB):
                        t = pe.transpose(psF[c][:, j * P:(j + 1) * P], yz[:, j, c * P:(c + 1) * P], ident[:, :])
                    t.then_inc(S["yzT_mm"], 1)

            def tail_proj(b):
                pe.wait_ge(S["yzT_ok"], 2 * b + 2)
                for j in range(TB):
                    for c in range(NC):
                        t = pe.matmul(psF[0][:, j * DM:(j + 1) * DM], yzT[:, c, j * P:(j + 1) * P], woT[:, c, :],
                                      start=(c == 0), stop=(c == NC - 1))
                t.then_inc(S["op_mm"], 1)

            def tail_xeT(b):
                pe.wait_ge(S["xe_ok"], b + 1)
                for j in range(TB):
                    t = pe.transpose(psF[1][:, j * P:(j + 1) * P], xe[:, j, :], ident[:, :])
                t.then_inc(S["xeT_mm"], 1)

            def tail_aff(b):
                pe.wait_ge(S["xeT_ok"], b + 1)
                pe.wait_ge(S["x1_ok"], b + 1)
                for j in range(TB):
                    t = pe.matmul(psF[0][:, j * E:(j + 1) * E], xeT[:, j * P:(j + 1) * P],
                                  vec[:, rows["cent"]:rows["cent"] + E], start=True, stop=True)
                t.then_inc(S["aff_mm"], 1)

            def tail_hotT(b):
                pe.wait_ge(S["hot_ok"], b + 1)
                for j in range(TB):
                    t = pe.transpose(psF[1][0:E, j * P:(j + 1) * P], hot[:, j, :], ident[:, :])
                t.then_inc(S["hotT_mm"], 1)
                pe.wait_ge(S["hotT_ok"], b + 1)
                pe.wait_ge(S["b2_in"], 16)
                for j in range(TB):
                    t = pe.matmul(psF[0][:, j * DM:(j + 1) * DM], hotT[:, j * P:(j + 1) * P], b2_sb[:, :],
                                  start=True, stop=True)
                t.then_inc(S["b2_mm"], 1)

            def up(b, e, j):
                n = (b * E + e) * NF + j
                pe.wait_ge(S["hid_ok"], n) if n else pe.wait_ge(S["b1_ok"], 1)
                if e == 0 and j == 0:
                    pe.wait_ge(S["w1g_ok"], E)
                pe.matmul(psU[:, :], w1T[:, e, j * P:(j + 1) * P], xeT[:, :], start=True, stop=True)\
                  .then_inc(S["up_mm"], 1)

            def down(b, e, j):
                n = (b * E + e) * NF + j
                if j == 0:
                    pe.wait_ge(S["mix_ok"], b * E + e) if b or e else pe.wait_ge(S["w2_ok"], E)
                pe.wait_ge(S["hid_ok"], n + 1)
                for t_ in range(TB):
                    t = pe.matmul(psD[:, t_ * DM:(t_ + 1) * DM], hid[:, j, t_ * P:(t_ + 1) * P], w2T[:, e, j, :],
                                  start=(j == 0 and t_ == 0), stop=(j == NF - 1), skip_group_check=True)
                if j == NF - 1:
                    t.then_inc(S["down_mm"], 1)

            def expert_half(b, h):
                for i in range(2 * h, 2 * h + 2):
                    if i < E * NF:
                        up(b, i // NF, i % NF)
                    if 1 <= i <= E * NF:
                        down(b, (i - 1) // NF, (i - 1) % NF)

            TAIL_PE = ((1, tail_turn), (2, tail_proj), (4, tail_xeT), (4, tail_aff), (5, tail_hotT))
            FRONT_PE = ((6, front_turn), (7, front_conv), (9, front_z), (11, front_xproj), (12, front_dt))
            turn_weights_0()
            front_turn(0)
            front_conv(0)
            front_z(0)
            front_xproj(0)
            front_dt(0)
            spread_B(0)
            spread_C(0)
            for b in range(B):
                for s in range(NS):
                    n = b * NS + s
                    if n + 1 < B * NS:
                        spread_B(n + 1)
                        spread_C(n + 1)
                    if n >= 1:
                        sum_state(n - 1)
                    if b >= 1:
                        for at, step in TAIL_PE:
                            if s == at:
                                step(b - 1)
                        for h in halves(s):
                            expert_half(b - 1, h)
                    elif s < E:
                        turn_expert(s)
                    elif s == E:
                        b1_shift()
                    if b + 1 < B:
                        for at, step in FRONT_PE:
                            if s == at:
                                step(b + 1)
            sum_state(B * NS - 1)
            for step in (tail_turn, tail_proj, tail_xeT, tail_aff, tail_hotT):
                step(B - 1)
            for h in range(HALVES):
                expert_half(B - 1, h)

        @block.scalar
        def _(act):
            for dst, src, name in (
                    (win_raw[:, :, :], in_proj_w.rearrange("(j p) d -> p j d", p=P), "win_in"),
                    (convw[:, :, :], conv_w.rearrange("(c p) k -> p c k", p=P), "convw_in"),
                    (xp_raw[:, :], x_proj_w, "xp_in"),
                    (dtw_raw[:, :, :], dt_proj_w.rearrange("(c p) r -> p c r", p=P), "dtw_in"),
                    (wo_raw[:, :], out_proj_w, "wo_in"),
                    (alog[:, :, :], A_log.rearrange("(c p) s -> p c s", p=P), "alog_in"),
                    (b2_sb[:, :], b2, "b2_in")):
                act.dma_start(dst, src).then_inc(S[name], 16)

            def weights_0():
                act.wait_ge(S["vecT_mm"], 1)
                act.activation(vec[:, :], psF[0][:, 0:n_rows], ACT.Copy).then_inc(S["vec_ok"], 1)
                act.wait_ge(S["alog_in"], 16)
                act.activation(Aneg[:, :, :], alog[:, :, :], ACT.Exp).then_inc(S["aexp_ok"], 1)
                for c in range(NC):
                    act.wait_ge(S["win_mm"], c + 1)
                    act.activation(winT[:, c, :, :].rearrange("p k e -> p (k e)"), (psU, psD)[c][:, :], ACT.Copy)\
                       .then_inc(S["win_ok"], 1)
                act.wait_ge(S["win_mm"], 3)
                act.activation(wzT[:, :], psF[1][:, 0:DI], ACT.Copy).then_inc(S["win_ok"], 1)

            def expert_weights(e):
                act.wait_ge(S["w1_mm"], e + 1)
                act.activation(w1T[:, e, :], psU[:, :], ACT.Copy).then_inc(S["w1_ok"], 1)
                act.wait_ge(S["w2_mm"], e + 1)
                act.activation(w2T[:, e, :, :].rearrange("p j d -> p (j d)"), psD[:, :], ACT.Copy)\
                   .then_inc(S["w2_ok"], 1)

            roots = [0]

            def root(v2, y, v_ok, y_ok, b):
                act.wait_ge(v_ok, b + 1)
                roots[0] += 1
                act.activation(lny[:, :, :], v2[:, :, :], ACT.Ln).then_inc(S["lny_ok"], 1)
                act.wait_ge(S["lny_ok"], roots[0])
                act.activation(y[:, :, :], lny[:, :, :], ACT.Exp, scale=-0.5).then_inc(y_ok, 1)

            def front_root(b):
                root(vv, yy, S["vv_ok"], S["y_ok"], b)

            def tail_root(b):
                root(vv2, yy2, S["vv2_ok"], S["y2_ok"], b)

            def front_res(b):
                act.wait_ge(S["stat_ok"], b + 1)
                if b >= 2:
                    act.wait_ge(S["x1_ok"], b - 1)
                for j in range(TB):
                    t = act.activation(xres[b % 2][:, j, :], xt[b % 2][:, j, :], ACT.Identity,
                                       bias=sc2[:, j:j + 1], scale=sc1[:, j:j + 1])
                t.then_inc(S["xres_ok"], 1)

            def front_hT(b):
                act.wait_ge(S["hT_mm"], b + 1)
                if b == 0:
                    act.wait_ge(S["vec_ok"], 1)
                else:
                    act.wait_ge(S["z_mm"], 2 * b)
                act.activation(hT[:, PADL:], psF[1][:, :], ACT.Identity, bias=col("beta"), scale=col("gamma"))\
                   .then_inc(S["hT_ok"], 1)

            def front_eu(b):
                if b == 0:
                    act.wait_ge(S["nconvb_ok"], 1)
                else:
                    act.wait_ge(S["u_ok"], 2 * b)
                for c in range(NC):
                    act.wait_ge(S["conv_mm"], 2 * b + c + 1)
                    act.activation(eu[:, c, :], psF[c][:, :], ACT.Exp, bias=nconvb[:, c:c + 1], scale=-1.0)\
                       .then_inc(S["eu_ok"], 1)

            def front_ez(b):
                if b:
                    act.wait_ge(S["zs_ok"], 2 * b)
                for i in range(2):
                    act.wait_ge(S["z_mm"], 2 * b + i + 1)
                    act.activation(ez[:, 2 * i:2 * i + 2, :].rearrange("p j d -> p (j d)"), psF[i][:, :], ACT.Exp,
                                   scale=-1.0).then_inc(S["ez_ok"], 1)

            def front_uD(b):
                if b >= 2:
                    act.wait_ge(S["sum_mm"], (b - 2) * NS + 1)
                act.wait_ge(S["u_ok"], 2 * b + 2)
                for c in range(NC):
                    act.activation(uD[b % 2][:, c, :], u[:, c, :], ACT.Copy, scale=col("D", c))\
                       .then_inc(S["uD_ok"], 1)

            def front_softplus(b):
                if b:
                    act.wait_ge(S["nc_ok"], b)
                    act.wait_ge(S["dt_ok"], b)
                for c in range(NC):
                    act.wait_ge(S["dt_mm"], 2 * b + c + 1)
                    act.activation(av[:, c, :], psF[c][:, :], ACT.Abs, bias=col("dt_b", c)).then_inc(S["av_ok"], 1)
                act.wait_ge(S["av_ok"], 2 * b + 2)
                act.activation(zz[:, :, :], av[:, :, :], ACT.Exp, scale=-1.0).then_inc(S["zz_ok"], 1)
                act.wait_ge(S["zz_ok"], b + 1)
                act.activation(ww[:, :, :], zz[:, :, :], ACT.Copy, bias=1.0).then_inc(S["ww_ok"], 1)
                act.wait_ge(S["ww_ok"], b + 1)
                act.activation(lw[:, :, :], ww[:, :, :], ACT.Ln).then_inc(S["lw_ok"], 1)

            def decay(n):
                b, s = divmod(n, NS)
                if s == 0:
                    act.wait_ge(S["dt_ok"], b + 1)
                if n == 0:
                    act.wait_ge(S["aneg_ok"], 1)
                if n >= 2:
                    act.wait_ge(S["h_ok"], 2 * (n - 1))
                for c in range(NC):
                    act.activation(dA[n % 2][:, c, :], dt[b % 2][:, c, :], ACT.Exp, scale=Aneg[:, c, s:s + 1])\
                       .then_inc(S["dA_ok"], 1)

            def copy_C(n):
                act.wait_ge(S["Cb_mm"], n + 1)
                if n >= 2:
                    act.wait_ge(S["hC_ok"], n - 1)
                act.activation(Cb[n % 2][:, :], psC[:, :], ACT.Copy).then_inc(S["Cb_ok"], 1)

            def tail_yzT(b):
                if b:
                    act.wait_ge(S["op_mm"], b)
                for c in range(NC):
                    act.wait_ge(S["yzT_mm"], 2 * b + c + 1)
                    act.activation(yzT[:, c, :], psF[c][:, :], ACT.Copy).then_inc(S["yzT_ok"], 1)

            def tail_xeT(b):
                act.wait_ge(S["xeT_mm"], b + 1)
                if b:
                    act.wait_ge(S["up_mm"], b * E * NF)
                act.activation(xeT[:, :], psF[1][:, :], ACT.Copy).then_inc(S["xeT_ok"], 1)

            def tail_base(b):
                act.wait_ge(S["nr_ok"], b + 1)
                act.wait_ge(S["x1_ok"], b + 1)
                if b >= 2:
                    act.wait_ge(S["res_ok"], b - 1)
                for j in range(TB):
                    t = act.activation(base[b % 2][:, j, :], x1[:, j, :], ACT.Identity, bias=nr[:, 1, j:j + 1],
                                       scale=nr[:, 0, j:j + 1])
                t.then_inc(S["base_ok"], 1)

            def tail_gate(b):
                act.wait_ge(S["mx_ok"], b + 1)
                act.activation(gex[:, :], mx[:, :], ACT.Exp, scale=-1.0).then_inc(S["gex_ok"], 1)

            def tail_hotT(b):
                act.wait_ge(S["hotT_mm"], b + 1)
                if b:
                    act.wait_ge(S["b2_mm"], b)
                act.activation(hotT[:, :], psF[1][0:E, :], ACT.Copy).then_inc(S["hotT_ok"], 1)

            def tail_acc(b):
                act.wait_ge(S["b2_mm"], b + 1)
                if b >= 2:
                    act.wait_ge(stored[b - 2], 16)
                act.activation(acc[b % 2][:, :, :].rearrange("p j d -> p (j d)"), psF[0][:, :], ACT.Copy)\
                   .then_inc(S["acc0_ok"], 1)

            def relu(b, e, j):
                n = (b * E + e) * NF + j
                act.wait_ge(S["up_mm"], n + 1)
                if n >= NF:
                    act.wait_ge(S["down_mm"], b * E + e)
                act.activation(hid[:, j, :], psU[:, :], ACT.Relu, bias=b1c[:, e * NF + j:e * NF + j + 1])\
                   .then_inc(S["hid_ok"], 1)

            def expert_half(b, h):
                for i in range(2 * h, 2 * h + 2):
                    if i < E * NF:
                        relu(b, i // NF, i % NF)

            TAIL_ACT = ((1, tail_yzT), (2, tail_root), (4, tail_base), (4, tail_xeT), (4, tail_gate), (5, tail_hotT),
                        (5, tail_acc))
            FRONT_ACT = ((3, front_root), (5, front_res), (6, front_hT), (7, front_eu), (9, front_ez),
                         (12, front_softplus), (13, front_uD))
            weights_0()
            front_root(0)
            front_res(0)
            front_hT(0)
            front_eu(0)
            front_ez(0)
            front_softplus(0)
            front_uD(0)
            decay(0)
            copy_C(0)
            for b in range(B):
                for s in range(NS):
                    n = b * NS + s
                    if n + 1 < B * NS:
                        decay(n + 1)
                    if b >= 1:
                        for at, step in TAIL_ACT:
                            if s == at:
                                step(b - 1)
                        for h in halves(s):
                            expert_half(b - 1, h)
                    elif s < E:
                        expert_weights(s)
                    if b + 1 < B:
                        for at, step in FRONT_ACT:
                            if s == at:
                                step(b + 1)
                    if n + 1 < B * NS:
                        copy_C(n + 1)
            for step in (tail_yzT, tail_root, tail_base, tail_xeT, tail_gate, tail_hotT, tail_acc):
                step(B - 1)
            for h in range(HALVES):
                expert_half(B - 1, h)

        @block.vector
        def _(dve):
            chain = [0]

            def link(t):
                chain[0] += 1
                t.then_inc(S["dve_chain"], 1)
                dve.wait_ge(S["dve_chain"], chain[0])

            def weights_0():
                dve.memset(hT[:, 0:PADL], 0.0).then_inc(S["pads_ok"], 1)
                for e in range(E):
                    t = dve.memset(firstw[:, :, e:e + 1], float(E - e))
                t.then_inc(S["firstw_ok"], 1)
                dve.wait_ge(S["win_in"], 16)
                dve.wait_ge(S["convw_in"], 16)
                for c in range(NC):
                    for k in range(K):
                        dve.tensor_scalar(win_tap[:, c, k, :], win_raw[:, c, :], convw[:, c, k:k + 1], None, ALU.mult)\
                           .then_inc(S["tap_ok"], 1)
                dve.wait_ge(S["vec_ok"], 1)
                dve.tensor_scalar(nconvb[:, :], vec[:, rows["conv_b"]:rows["conv_b"] + NC], -1.0, None, ALU.mult)\
                   .then_inc(S["nconvb_ok"], 1)
                dve.wait_ge(S["aexp_ok"], 1)
                dve.tensor_scalar(Aneg[:, :, :], Aneg[:, :, :], -1.0, None, ALU.mult).then_inc(S["aneg_ok"], 1)

            def weights_1():
                dve.wait_ge(S["pick_ok"], 1 + 3)
                dve.tensor_copy(pick[:, :, :], pick32[:, :].unsqueeze(2).broadcast_to([3 * BC, BC, P]))\
                   .then_inc(S["pick_ok"], 1)
                dve.wait_ge(S["small_mm"], 1)
                xp = psF[0][:, 0:NC * 64].rearrange("p (c r) -> p c r", c=NC)
                for i in range(3):
                    t = dve.tensor_copy(xpT[:, :, i * BC:(i + 1) * BC], xp[:, :, R:R + BC])
                t.then_inc(S["small_ok"], 1)
                dve.tensor_copy(xpT[:, :, 3 * BC:3 * BC + R], xp[:, :, 0:R]).then_inc(S["small_ok"], 1)
                dve.tensor_copy(dtwT[3 * BC:3 * BC + R, :, :].rearrange("p c d -> p (c d)"), psU[0:R, 0:NC * P])\
                   .then_inc(S["small_ok"], 1)
                dve.tensor_copy(woT[:, :, :].rearrange("p c d -> p (c d)"), psF[0][:, 128:128 + NC * P])\
                   .then_inc(S["small_ok"], 1)

            def gamma_w1():
                dve.wait_ge(S["b1_mm"], 1)
                dve.tensor_tensor(b1c[:, :], psU[:, 0:E * NF], vec[:, rows["b1"]:rows["b1"] + E * NF], ALU.add)\
                   .then_inc(S["b1_ok"], 1)
                for e in range(E):
                    dve.tensor_scalar(w1T[:, e, :], w1T[:, e, :], col("ln_g", e), None, ALU.mult)\
                       .then_inc(S["w1g_ok"], 1)

            def moments(src, st, m, v2, ok):
                for j in range(TB):
                    t = dve.bn_stats(st[:, j, :], src[:, j, :])
                link(t)
                for j in range(TB):
                    t = dve.bn_aggr(m[:, j, :], st[:, j, :])
                link(t)
                link(dve.tensor_scalar(v2[:, 0, :], m[:, :, 1], EPS, None, ALU.add))
                dve.scalar_tensor_tensor(out=v2[:, 1, :], in0=v2[:, 0, :], scalar=EPS, in1=m[:, :, 1],
                                         op0=ALU.mult, op1=ALU.add).then_inc(ok, 1)

            def newton(v2, y, r2):
                link(dve.tensor_tensor(r2[:, :, :], y[:, :, :], y[:, :, :], ALU.mult))
                link(dve.tensor_tensor(r2[:, :, :], r2[:, :, :], v2[:, :, :], ALU.mult))
                link(dve.tensor_scalar(r2[:, :, :], r2[:, :, :], -0.5, 1.5, ALU.mult, ALU.add))
                link(dve.tensor_tensor(r2[:, :, :], r2[:, :, :], y[:, :, :], ALU.mult))

            def front_moments(b):
                dve.wait_ge(x_in[b], 16)
                moments(xt[b % 2], bst, mv, vv, S["vv_ok"])

            def front_norm(b):
                dve.wait_ge(S["y_ok"], b + 1)
                newton(vv, yy, rs)
                if b:
                    dve.wait_ge(S["xres_ok"], b)
                    dve.wait_ge(S["hT_mm"], b)
                dve.scalar_tensor_tensor(out=sc2[:, :], in0=mv[:, :, 0], scalar=-1.0, in1=rs[:, 0, :],
                                         op0=ALU.mult, op1=ALU.mult)
                dve.tensor_scalar(sc1[:, :], rs[:, 0, :], 1.0, None, ALU.add).then_inc(S["stat_ok"], 1)
                for j in range(TB):
                    t = dve.tensor_scalar(xh[:, j, :], xt[b % 2][:, j, :], mv[:, j, 0:1], rs[:, 1, j:j + 1],
                                          ALU.subtract, ALU.mult)
                t.then_inc(S["xh_ok"], 1)

            def front_u(b):
                dve.wait_ge(S["eu_ok"], 2 * b + 2)
                link(dve.tensor_scalar(eu[:, :, :], eu[:, :, :], 1.0, None, ALU.add))
                link(dve.reciprocal(eu[:, :, :], eu[:, :, :]))
                if b:
                    dve.wait_ge(S["uD_ok"], 2 * b)
                    dve.wait_ge(S["xp_mm"], b)
                    dve.wait_ge(S["dtu_ok"], b)
                for c in range(NC):
                    dve.scalar_tensor_tensor(out=u[:, c, :], in0=psF[c][:, :], scalar=col("conv_b", c), in1=eu[:, c, :],
                                             op0=ALU.add, op1=ALU.mult).then_inc(S["u_ok"], 1)

            def front_zs(b):
                dve.wait_ge(S["ez_ok"], 2 * b + 2)
                link(dve.tensor_scalar(ez[:, :, :], ez[:, :, :], 1.0, None, ALU.add))
                link(dve.reciprocal(ez[:, :, :], ez[:, :, :]))
                if b >= 2:
                    dve.wait_ge(S["yz_ok"], b - 1)
                for i in range(2):
                    dve.tensor_tensor(zs[b % 2][:, 2 * i:2 * i + 2, :].rearrange("p j d -> p (j d)"), psF[i][:, :],
                                      ez[:, 2 * i:2 * i + 2, :].rearrange("p j d -> p (j d)"), ALU.mult)\
                       .then_inc(S["zs_ok"], 1)

            def front_parts(b):
                dve.wait_ge(S["xp_mm"], b + 1)
                if b:
                    dve.wait_ge(S["dt_mm"], 2 * b)
                dve.tensor_copy(dtlow[3 * BC:3 * BC + R, :], psF[0][3 * BC:3 * BC + R, :]).then_inc(S["dtlow_ok"], 1)
                if b >= 2:
                    dve.wait_ge(S["Bb_mm"], (b - 1) * NS)
                    dve.wait_ge(S["Cb_mm"], (b - 1) * NS)
                pt = parts[b % 2]
                link(dve.tensor_copy(pt[:, :], psF[0][0:3 * BC, :]))
                link(dve.tensor_tensor(rest[:, :], psF[0][0:3 * BC, :], pt[:, :], ALU.subtract))
                dve.tensor_copy(pt[BC:2 * BC, :], rest[BC:2 * BC, :])
                link(dve.tensor_copy(pt[2 * BC:3 * BC, :], rest[2 * BC:3 * BC, :]))
                link(dve.tensor_tensor(rest[2 * BC:3 * BC, :], rest[2 * BC:3 * BC, :], pt[2 * BC:3 * BC, :],
                                       ALU.subtract))
                dve.tensor_copy(pt[2 * BC:3 * BC, :], rest[2 * BC:3 * BC, :]).then_inc(S["parts_ok"], 1)

            def front_steps(b):
                if b:
                    dve.wait_ge(S["dt_ok"], b)
                for c in range(NC):
                    dve.wait_ge(S["av_ok"], 2 * b + c + 1)
                    dve.tensor_scalar(rv[:, c, :], psF[c][:, :], col("dt_b", c), 0.0, ALU.add, ALU.max)\
                       .then_inc(S["rv_ok"], 1)

            def front_rounding(b):
                dve.wait_ge(S["ww_ok"], b + 1)
                dve.wait_ge(S["lw_ok"], b + 1)
                dve.scalar_tensor_tensor(out=ww[:, :, :].rearrange("p c t -> p (c t)"),
                                         in0=ww[:, :, :].rearrange("p c t -> p (c t)"), scalar=-1.0,
                                         in1=zz[:, :, :].rearrange("p c t -> p (c t)"), op0=ALU.add, op1=ALU.subtract)\
                   .then_inc(S["nc_ok"], 1)

            def inject(n):
                b, s = divmod(n, NS)
                if s == 0:
                    dve.wait_ge(S["dtu_ok"], b + 1)
                dve.wait_ge(S["Bb_mm"], n + 1)
                if n >= 2:
                    dve.wait_ge(S["h_ok"], 2 * (n - 1))
                dve.tensor_tensor(dBu[n % 2][:, :, :], dtu[b % 2][:, :, :],
                                  psB[:, :].unsqueeze(1).broadcast_to([P, NC, L]), ALU.mult).then_inc(S["dBu_ok"], 1)

            def scan(n):
                dve.wait_ge(S["dBu_ok"], n + 1)
                if n >= 2:
                    dve.wait_ge(S["hC_ok"], n - 1)
                for c in range(NC):
                    dve.wait_ge(S["dA_ok"], 2 * n + c + 1)
                    dve.tensor_tensor_scan(hs[n % 2][:, c, :], dA[n % 2][:, c, :], dBu[n % 2][:, c, :], 0.0,
                                           ALU.mult, ALU.add).then_inc(S["h_ok"], 1)

            def tail_yz(b):
                dve.wait_ge(S["sum_mm"], (b + 1) * NS)
                if b:
                    dve.wait_ge(S["yzT_mm"], 2 * b)
                for i in range(2):
                    t = dve.tensor_tensor(yz[:, 2 * i:2 * i + 2, :], psY[:, 2 * i:2 * i + 2, :],
                                          zs[b % 2][:, 2 * i:2 * i + 2, :], ALU.mult)
                t.then_inc(S["yz_ok"], 1)

            def tail_x1(b):
                dve.wait_ge(S["op_mm"], b + 1)
                dve.wait_ge(S["xres_ok"], b + 1)
                if b:
                    dve.wait_ge(S["base_ok"], b)
                dve.tensor_tensor(x1[:, :, :].rearrange("p j d -> p (j d)"), psF[0][:, :],
                                  xres[b % 2][:, :, :].rearrange("p j d -> p (j d)"), ALU.add).then_inc(S["x1_ok"], 1)
                dve.wait_ge(S["x1_ok"], b + 1)
                moments(x1, bst2, mv2, vv2, S["vv2_ok"])

            def tail_norm(b):
                dve.wait_ge(S["y2_ok"], b + 1)
                newton(vv2, yy2, rs2)
                dve.tensor_scalar(nr[:, 0, :], rs2[:, 0, :], 1.0, None, ALU.add)
                dve.scalar_tensor_tensor(out=nr[:, 1, :], in0=mv2[:, :, 0], scalar=-1.0, in1=rs2[:, 0, :],
                                         op0=ALU.mult, op1=ALU.mult).then_inc(S["nr_ok"], 1)
                link(dve.tensor_tensor(nr[:, 2, :], rs2[:, 0, :], rs2[:, 1, :], ALU.mult))
                link(dve.tensor_tensor(nr[:, 2, :], nr[:, 2, :], vv2[:, 1, :], ALU.mult))
                if b:
                    dve.wait_ge(S["xeT_mm"], b)
                for j in range(TB):
                    t = dve.tensor_scalar(xe[:, j, :], x1[:, j, :], mv2[:, j, 0:1], rs2[:, 1, j:j + 1],
                                          ALU.subtract, ALU.mult)
                t.then_inc(S["xe_ok"], 1)

            def tail_choose(b):
                dve.wait_ge(S["aff_mm"], b + 1)
                link(dve.tensor_tensor(aff[:, :, :], psF[0][:, 0:TB * E].rearrange("p (j e) -> p j e", e=E),
                                       nr[:, 2, :].unsqueeze(2).broadcast_to([P, TB, E]), ALU.mult))
                if b:
                    dve.wait_ge(S["gex_ok"], b)
                dve.tensor_reduce(mx[:, :], aff[:, :, :], AX.X, ALU.max).then_inc(S["mx_ok"], 1)
                dve.wait_ge(S["mx_ok"], b + 1)
                link(dve.tensor_tensor(score[:, :, :], aff[:, :, :], mx[:, :].unsqueeze(2).broadcast_to([P, TB, E]),
                                       ALU.is_ge))
                link(dve.tensor_tensor(score[:, :, :], score[:, :, :], firstw[:, :, :], ALU.mult))
                link(dve.tensor_reduce(mx2[:, :], score[:, :, :], AX.X, ALU.max))
                if b:
                    dve.wait_ge(S["hotT_mm"], b)
                    dve.wait_ge(S["mix_ok"], b * E)
                dve.tensor_tensor(hot[:, :, :], score[:, :, :], mx2[:, :].unsqueeze(2).broadcast_to([P, TB, E]),
                                  ALU.is_equal).then_inc(S["hot_ok"], 1)

            def tail_gate(b):
                dve.wait_ge(S["gex_ok"], b + 1)
                link(dve.tensor_scalar(gate[:, :], gex[:, :], 1.0, None, ALU.add))
                link(dve.reciprocal(gate[:, :], gate[:, :]))

            def mix(b, e):
                dve.wait_ge(S["down_mm"], b * E + e + 1)
                if e == 0:
                    dve.wait_ge(S["acc0_ok"], b + 1)
                else:
                    dve.wait_ge(S["mix_ok"], b * E + e)
                if e == 0:
                    dve.wait_ge(S["hot_ok"], b + 1)
                a = acc[b % 2]
                for j in range(TB):
                    t = dve.scalar_tensor_tensor(out=a[:, j, :], in0=psD[:, j * DM:(j + 1) * DM],
                                                 scalar=hot[:, j, e:e + 1], in1=a[:, j, :], op0=ALU.mult, op1=ALU.add)
                t.then_inc(S["mix_ok"], 1)

            def finish(b):
                dve.wait_ge(S["mix_ok"], (b + 1) * E)
                dve.wait_ge(S["base_ok"], b + 1)
                for j in range(TB):
                    t = dve.scalar_tensor_tensor(out=res[b % 2][:, j, :], in0=acc[b % 2][:, j, :],
                                                 scalar=gate[:, j:j + 1], in1=base[b % 2][:, j, :],
                                                 op0=ALU.mult, op1=ALU.add)
                t.then_inc(S["res_ok"], 1)

            TAIL_DVE = ((0, tail_yz), (2, tail_x1), (3, tail_norm), (4, tail_choose), (5, tail_gate))
            FRONT_DVE = ((3, front_moments), (4, front_norm), (8, front_u), (10, front_zs), (11, front_parts),
                         (12, front_steps), (13, front_rounding))
            weights_0()
            front_moments(0)
            front_norm(0)
            weights_1()
            front_u(0)
            front_zs(0)
            front_parts(0)
            front_steps(0)
            front_rounding(0)
            inject(0)
            for b in range(B):
                for s in range(NS):
                    n = b * NS + s
                    if n + 1 < B * NS:
                        inject(n + 1)
                    scan(n)
                    if b >= 1:
                        for at, step in TAIL_DVE:
                            if s == at:
                                step(b - 1)
                        for h in halves(s):
                            if h >= 2 and h % 2 == 0:
                                mix(b - 1, h // 2 - 1)
                        if s == NS - 1:
                            finish(b - 1)
                    elif s == E + 1:
                        gamma_w1()
                    if b + 1 < B:
                        for at, step in FRONT_DVE:
                            if s == at:
                                step(b + 1)
            for step in (tail_yz, tail_x1, tail_norm, tail_choose, tail_gate):
                step(B - 1)
            for e in range(E):
                mix(B - 1, e)
            finish(B - 1)

        @block.gpsimd
        def _(pool):
            pool.memset(ident[:, :], 0.0).then_inc(S["ident_ok"], 1)
            pool.memset(pick32[:, :], 0.0).then_inc(S["pick_ok"], 1)
            pool.wait_ge(S["ident_ok"], 1)
            pool.affine_select(out=ident[:, :], in_=ident[:, :], compare_op=ALU.not_equal, fill=1.0, base=0,
                               pattern=[[-1, P]], channel_multiplier=1).then_inc(S["ident_ok"], 1)
            for i in range(3):
                pool.wait_ge(S["pick_ok"], i + 1)
                pool.affine_select(out=pick32[:, :], in_=pick32[:, :], compare_op=ALU.not_equal, fill=1.0,
                                   base=-BC * i, pattern=[[-1, BC]], channel_multiplier=1).then_inc(S["pick_ok"], 1)

            def front_dt(b):
                pool.wait_ge(S["nc_ok"], b + 1)
                if b:
                    pool.wait_ge(S["dt_ok"], b)
                flat = "p c t -> p (c t)"
                pool.tensor_tensor(sp[:, :, :].rearrange(flat), lw[:, :, :].rearrange(flat),
                                   ww[:, :, :].rearrange(flat), ALU.subtract).then_inc(S["sp_ok"], 1)
                pool.wait_ge(S["sp_ok"], b + 1)
                pool.wait_ge(S["rv_ok"], 2 * b + 2)
                if b >= 2:
                    pool.wait_ge(S["dA_ok"], 2 * (b - 1) * NS)
                pool.tensor_tensor(dt[b % 2][:, :, :].rearrange(flat), sp[:, :, :].rearrange(flat),
                                   rv[:, :, :].rearrange(flat), ALU.add).then_inc(S["dt_ok"], 1)
                pool.wait_ge(S["dt_ok"], b + 1)
                pool.wait_ge(S["u_ok"], 2 * b + 2)
                if b >= 2:
                    pool.wait_ge(S["dBu_ok"], (b - 1) * NS)
                pool.tensor_tensor(dtu[b % 2][:, :, :].rearrange(flat), dt[b % 2][:, :, :].rearrange(flat),
                                   u[:, :, :].rearrange(flat), ALU.mult).then_inc(S["dtu_ok"], 1)

            def read_out(n):
                pool.wait_ge(S["Cb_ok"], n + 1)
                pool.wait_ge(S["h_ok"], 2 * n + 2)
                if n >= 2:
                    pool.wait_ge(S["sum_mm"], n - 1)
                pool.tensor_tensor(hC[n % 2][:, :, :], hs[n % 2][:, :, :],
                                   Cb[n % 2][:, :].unsqueeze(1).broadcast_to([P, NC, L]), ALU.mult)\
                    .then_inc(S["hC_ok"], 1)

            front_dt(0)
            for n in range(B * NS):
                read_out(n)
                if n % NS == 13 and n // NS + 1 < B:
                    front_dt(n // NS + 1)


_INS = ['L0_attn_x', 'L0_attn_ln_gamma', 'L0_attn_ln_beta', 'L0_attn_in_proj_w', 'L0_attn_conv_w', 'L0_attn_conv_b',
        'L0_attn_x_proj_w', 'L0_attn_dt_proj_w', 'L0_attn_dt_proj_b', 'L0_attn_A_log', 'L0_attn_D',
        'L0_attn_out_proj_w', 'L0_ffn_centroids', 'L0_ffn_ln_g', 'L0_ffn_ln_b', 'L0_ffn_w1', 'L0_ffn_b1', 'L0_ffn_w2',
        'L0_ffn_b2']
_OUTS = [((4, 512, 128), 'float32')]


def kernel(**inputs):
    import numpy as _np
    import concourse.bacc as _bacc
    from concourse import mybir as _mybir
    from concourse.bass_utils import run_bass_kernel_spmd as _run

    nc = _bacc.Bacc("TRN2", target_bir_lowering=False, num_devices=1)
    arrays, args = {}, []
    for name in _INS:
        a = _np.ascontiguousarray(inputs[name])
        arrays[f"in_{name}_dram"] = a
        args.append(nc.dram_tensor(f"in_{name}_dram", a.shape, _mybir.dt.from_np(a.dtype), kind="ExternalInput").ap())
    for i, (shape, dtype) in enumerate(_OUTS):
        dt = _mybir.dt.from_np(_np.dtype(dtype))
        args.append(nc.dram_tensor(f"out_{i}_dram", shape, dt, kind="ExternalOutput").ap())
    build(nc, *args)
    r = _run(nc, [arrays], core_ids=[0])
    got = tuple(r.results[0][f"out_{i}_dram"] for i in range(len(_OUTS)))
    return got[0]
```

```python
from contextlib import ExitStack

import concourse.bass as bass
from concourse import mybir

ALU = mybir.AluOpType
ACT = mybir.ActivationFunctionType
AX = mybir.AxisListType
F32 = mybir.dt.float32
BF16 = mybir.dt.bfloat16
EPS = 1e-5
P = 128


def build(nc, x, ln_gamma, ln_beta, in_proj_w, conv_w, conv_b, x_proj_w, dt_proj_w, dt_proj_b, A_log, D,
          out_proj_w, centroids, ln_g, ln_b, w1, b1, w2, b2, out):
    B, L, DM = x.shape
    DI, NS = A_log.shape
    R = dt_proj_w.shape[1]
    K = conv_w.shape[1]
    E, F, _ = w1.shape
    TB = L // P
    NC = DI // P
    NF = F // P
    BC = 2 * NS
    PADL = K - 1
    EXPERTS = 8
    LAG = 2
    AHEAD = 3
    GROUPS = (tuple(range(B - 1)), (B - 1,))
    NG = len(GROUPS)
    NT = [len(g) * TB + E - 1 for g in GROUPS]
    ROUNDS = [len(g) * TB for g in GROUPS]
    FIRST = [sum(NT[:g]) for g in range(NG + 1)]
    assert DM == P and L == 512 and NS == 16

    rows, n_rows = {}, 0
    for name, count in (("gamma", 1), ("beta", 1), ("conv_b", NC), ("dt_b", NC), ("D", NC), ("ln_g", E),
                        ("ln_b", E), ("cent", E)):
        rows[name] = n_rows
        n_rows += count

    ctx = ExitStack()
    with ctx:
        def sb(name, shape, dt=F32):
            return ctx.enter_context(nc.sbuf_tensor(name, shape, dt))

        def ps(name, shape, dt=F32):
            return ctx.enter_context(nc.psum_tensor(name, shape, dt))

        def sem(name):
            return ctx.enter_context(nc.semaphore(name))

        vec_rows = sb("vec_rows", [n_rows, P])
        win_raw = sb("win_raw", [P, 2 * NC, DM])
        xp_raw = sb("xp_raw", [R + BC, DI])
        dtw_raw = sb("dtw_raw", [P, NC, R])
        wo_raw = sb("wo_raw", [P, DI])
        w1_raw = sb("w1_raw", [P, E * NF, DM])
        w2_raw = sb("w2_raw", [P, E, F])
        convw = sb("convw", [P, NC, K])
        alog = sb("alog", [P, NC, NS])
        b2_sb = sb("b2_sb", [E, DM])
        ident = sb("ident", [P, P])
        pick32 = sb("pick32", [3 * BC, BC])
        pick = sb("pick", [3 * BC, BC], BF16)
        vec = sb("vec", [P, n_rows])
        Aneg = sb("Aneg", [P, NC, NS])
        winT = sb("winT", [P, NC, K, P])
        wzT = sb("wzT", [P, DI])
        xpT = sb("xpT", [P, NC, 3 * BC + R])
        dtwT = sb("dtwT", [P, NC, P])
        woT = sb("woT", [P, NC, DM])
        w1T = w1_raw[:, :, :].rearrange("p (e j) d -> p e (j d)", e=E)
        w2T = w2_raw[:, :, :].rearrange("p e (j d) -> p e j d", j=NF)
        lnb_diag = sb("lnb_diag", [P, E, E])
        b1_split = sb("b1_split", [E, 3, F], BF16)
        b1_rows = sb("b1_rows", [3, E, F], BF16)
        ones16 = sb("ones16", [P, P], BF16)
        before32 = sb("before32", [P, P])
        before = sb("before", [P, P], BF16)
        rounds = sb("rounds", [P, E, ROUNDS[0]])
        tile_no = sb("tile_no", [1, NT[0], E])
        one_e = sb("one_e", [P, E])
        firstw = sb("firstw", [P, TB, E])

        xt = [sb(f"xt{i}", [P, TB, DM]) for i in range(2)]
        bst = sb("bst", [P, TB, 6])
        mv = sb("mv", [P, TB, 2])
        vv = sb("vv", [P, 2, TB])
        rs = sb("rs", [P, 2, TB])
        lny = [sb(f"lny{i}", [P, 2, TB]) for i in range(2)]
        yy = sb("yy", [P, 2, TB])
        sc1 = sb("sc1", [P, TB])
        sc2 = sb("sc2", [P, TB])
        xh = sb("xh", [P, TB, DM])
        xres = [sb(f"xres{i}", [P, TB, DM]) for i in range(2)]
        hT = sb("hT", [P, PADL + L])
        room = sb("room", [P, 5, NC, L])
        u, uD, av, ww, lw = (room[:, i] for i in range(5))
        zs = [sb(f"zs{i}", [P, TB, DI]) for i in range(2)]
        parts = [sb(f"parts{i}", [3 * BC, L], BF16) for i in range(2)]
        dtlow = sb("dtlow", [P, L])
        zz = av
        rest = ww[0:3 * BC, 0, :]
        dt = [sb(f"dt{i}", [P, NC, L]) for i in range(2)]
        dtu = [sb(f"dtu{i}", [P, NC, L]) for i in range(2)]
        dA = [sb(f"dA{i}", [P, NC, L]) for i in range(AHEAD)]
        dBu = [sb(f"dBu{i}", [P, NC, L]) for i in range(2)]
        hs = [sb(f"hs{i}", [P, NC, L]) for i in range(AHEAD)]
        hC = [sb(f"hC{i}", [P, NC, L]) for i in range(AHEAD)]
        Cb = [sb(f"Cb{i}", [P, L]) for i in range(AHEAD)]
        yz = sb("yz", [P, TB, DI])
        win_tap = yz[:, :, :].rearrange("p j (a m) -> p (j a m)", m=P).rearrange("p (c k m) -> p c k m", c=NC, k=K)
        yzT = sb("yzT", [P, NC, L])
        x1 = sb("x1", [P, TB, DM])
        bst2 = sb("bst2", [P, TB, 6])
        mv2 = sb("mv2", [P, TB, 2])
        vv2 = sb("vv2", [P, 2, TB])
        rs2 = sb("rs2", [P, 2, TB])
        yy2 = sb("yy2", [P, 2, TB])
        nr = sb("nr", [P, 3, TB])
        xe = [sb(f"xe{b}", [P, TB, DM]) for b in range(B)]
        xeT = sb("xeT", [P, L])
        base = [sb(f"base{b}", [P, TB, DM]) for b in range(B)]
        aff = sb("aff", [P, TB, E])
        score = sb("score", [P, TB, E])
        mx = sb("mx", [P, TB])
        mx2 = sb("mx2", [P, TB])
        gex = sb("gex", [P, TB])
        gate = [sb(f"gate{b}", [P, TB]) for b in range(B)]
        hot = [sb(f"hot{b}", [P, TB, E]) for b in range(B)]
        hotT = sb("hotT", [E, L])
        hot16 = sb("hot16", [P, TB, E], BF16)
        more = sb("more", [P, E, ROUNDS[0]])
        tiles = sb("tiles", [P, E])
        ends = sb("ends", [P, E])
        ends128 = sb("ends128", [P, E])
        start = sb("start", [P, E])
        count = [sb(f"count{b}", [P, E]) for b in range(B)]
        place = sb("place", [P, TB, E])
        rank = [sb(f"rank{b}", [P, TB]) for b in range(B)]
        slotf = sb("slotf", [P, TB])
        slot = [sb(f"slot{b}", [P, TB], mybir.dt.uint32) for b in range(B)]
        past = sb("past", [1, NT[0], E])
        te_f = sb("te_f", [1, NT[0]])
        te = [sb(f"te{g}", [1, NT[g]], mybir.dt.int32) for g in range(NG)]
        rows_room = room[:, :, :, :].rearrange("p i c t -> p (i c t)")
        xs, ys = (rows_room[:, i * NT[0] * DM:(i + 1) * NT[0] * DM].rearrange("p (i d) -> p i d", d=DM)
                  for i in range(2))
        xsT = sb("xsT", [P, P])
        hn = sb("hn", [P, F])
        hh = sb("hh", [P, NF, P])
        b1_sb = hh[0:E, :, :].rearrange("p j s -> p (j s)")
        b1_rest = hn[0:E, :]
        yg = xe
        res = base

        psB = ps("psB", [P, L])
        psC = ps("psC", [P, L])
        psY = ps("psY", [P, TB, DI])
        psF = [ps(f"psF{i}", [P, 512]) for i in range(2)]
        psU = ps("psU", [P, 512])
        psD = ps("psD", [P, 512])

        x_tiles = [nc.dram_tensor(f"x_tiles{g}", [NT[g] * P, DM], F32).ap() for g in range(NG)]
        y_tiles = [nc.dram_tensor(f"y_tiles{g}", [NT[g] * P, DM], F32).ap() for g in range(NG)]
        b1_turn = nc.dram_tensor("b1_turn", [E, 3, F], BF16).ap()
        CHUNKS = [[(lo, min(lo + 4, NT[g])) for lo in range(0, NT[g], 4)] for g in range(NG)]

        S = {}
        for name in """vec_in win_in convw_in xp_in dtw_in wo_in alog_in b2_in w1_in w2_in
                ident_ok pick_ok pads_ok firstw_ok vecT_mm vec_ok tap_ok win_mm win_ok small_mm small_ok
                aexp_ok aneg_ok w1_mm w1_ok w2_mm w2_ok diag_ok b1_mm b1_split_ok b1_turn_in b1_rows_in w1g_ok b1_in
                ones_ok before_ok consts_ok zero_ok tiles_zero rank_ok
                hot16_ok rank_mm slot_ok te_ok xsT_mm xsT_ok up_mm relu_ok hh_mm hh_ok down_mm ys_ok gate_ok
                stat_ok xh_ok xres_ok hT_mm hT_ok conv_mm u_ok uD_ok z_mm zs_ok xp_mm rest_ok parts_ok
                dtlow_ok dt_mm av_ok rv_ok zz_ok ww_ok lw_ok nc_ok tv_ok dt_ok dtu_ok
                Bb_mm dBu_ok Cb_mm Cb_ok dA_ok h_ok hC_ok sum_mm
                yz_ok yzT_mm yzT_ok op_mm x1_ok nr_ok xe_ok base_ok xeT_mm xeT_ok aff_mm mx_ok gex_ok hot_ok
                hotT_mm hotT_ok b2_mm b2_ok res_ok
                vv_ok y_ok vv2_ok y2_ok lny_ok dve_chain""".split():
            S[name] = sem(name)

        x_in = [sem(f"x_in{b}") for b in range(B)]
        stored = [sem(f"stored{b}") for b in range(B)]
        scattered = [sem(f"scattered{g}") for g in range(NG)]
        y_stored = [sem(f"y_stored{g}") for g in range(NG)]
        gathered = [sem(f"gathered{b}") for b in range(B)]
        xs_in = [[sem(f"xs_in{g}_{i}") for i in range(len(CHUNKS[g]))] for g in range(NG)]

        def col(name, i=0):
            return vec[:, rows[name] + i:rows[name] + i + 1]

        FRONT = (("front_moments", 0), ("front_root", 1), ("front_norm", 2), ("front_turn", 3), ("front_conv0", 4),
                 ("front_conv1", 5), ("front_z", 6), ("front_silu", 6), ("front_xproj", 7), ("front_uD", 8),
                 ("front_low", 8), ("front_parts", 9), ("front_dt", 9), ("front_abs", 9), ("front_exp", 10),
                 ("front_rounding", 11), ("front_sub", 11), ("front_log", 11), ("front_add", 12),
                 ("front_dtu", 14), ("front_res", 15))
        TAIL = (("tail_turn", 0), ("tail_proj", 1), ("tail_moments", 2), ("tail_root", 3), ("tail_norm", 4),
                ("tail_xeT", 5), ("tail_base", 6), ("tail_aff", 6), ("tail_choose", 6), ("tail_gate", 7),
                ("tail_rank", 7), ("tail_hot", 7), ("tail_bias", 8))
        TAIL_SOON = (("tail_turn", 0), ("tail_proj", 1), ("tail_moments", 1), ("tail_root", 2), ("tail_norm", 2),
                     ("tail_xeT", 3), ("tail_base", 3), ("tail_aff", 4), ("tail_choose", 4), ("tail_gate", 5),
                     ("tail_rank", 5), ("tail_hot", 6), ("tail_bias", 7))
        LAST = 140
        agenda = [[] for _ in range(LAST + 1)]
        for b in range(1, B):
            for name, at in FRONT:
                agenda[NS * (b - 1) + at].append((name, b))
        routed = []
        for b in range(B):
            begin = NS * (b + 1) + (10 if b < B - 2 else 3 if b < B - 1 else 1)
            for name, at in TAIL if b < B - 2 else TAIL_SOON:
                agenda[begin + at].append((name, b))
                if name == "tail_rank":
                    for g in range(NG):
                        if b == GROUPS[g][-1]:
                            agenda[begin + at].append(("route", g))
                            agenda[begin + at].append(("scatter", g))
                            agenda[begin + at + 1].append(("load_tiles", g))
                            routed.append(begin + at)
        for e in range(E):
            agenda[EXPERTS + e].append(("turn_expert", e))
            agenda[EXPERTS + E + e // 3].append(("b1_shift", e))
            agenda[EXPERTS + E + 4 + e].append(("gamma_w1", e))
        agenda[EXPERTS + E + 3].append(("split_b1", 0))
        at = 0
        done = []
        for g in range(NG):
            at = max(at, routed[g] + 3)
            for m in range(FIRST[g], FIRST[g + 1] + 1):
                agenda[at].append(("tile", (m if m < FIRST[g + 1] else None, m - 1 if m > FIRST[g] else None)))
                at += 1
            done.append(at)
        for g, done in enumerate(done):
            agenda[done].append(("store_tiles", g))
            for i, b in enumerate(GROUPS[g]):
                agenda[done + 2 + i].append(("gather", b))
                agenda[done + 3 + i].append(("finish", b))
                agenda[done + 3 + i].append(("store", b))

        def steps(n, have):
            for name, i in agenda[n]:
                if name in have:
                    have[name](i)

        block = ctx.enter_context(nc.Block())

        @block.sync
        def _(sp_):
            def load_x(b):
                if b >= 2:
                    sp_.wait_ge(S["xh_ok"], b - 1)
                    sp_.wait_ge(S["xres_ok"], b - 1)
                sp_.dma_start(xt[b % 2][:, :, :], x[b].rearrange("(j p) d -> p j d", p=P)).then_inc(x_in[b], 16)

            load_x(0)
            one = [("gamma", ln_gamma), ("beta", ln_beta), ("conv_b", conv_b), ("dt_b", dt_proj_b), ("D", D)]
            for name, v in one:
                n = v.shape[0] // P
                sp_.dma_start(vec_rows[rows[name]:rows[name] + n, :], v.rearrange("(a n) -> a n", n=P))\
                   .then_inc(S["vec_in"], 16)
            for name, v in (("ln_g", ln_g), ("ln_b", ln_b), ("cent", centroids)):
                sp_.dma_start(vec_rows[rows[name]:rows[name] + E, :], v).then_inc(S["vec_in"], 16)
            sp_.dma_start(b1_sb[:, :], b1).then_inc(S["b1_in"], 16)
            load_x(1)
            for e in range(E):
                sp_.dma_start(w1_raw[:, e * NF:(e + 1) * NF, :], w1[e].rearrange("(j p) d -> p j d", p=P))\
                   .then_inc(S["w1_in"], 16)
                sp_.dma_start(w2_raw[:, e, :], w2[e]).then_inc(S["w2_in"], 16)
            sp_.wait_ge(S["zero_ok"], 1)
            for g in range(NG):
                for lo, hi in CHUNKS[g]:
                    sp_.dma_start(x_tiles[g][lo * P:hi * P, :].rearrange("(i p) d -> p i d", p=P), xe[0][:, 0:hi - lo, :])\
                       .then_inc(S["tiles_zero"], 16)
            load_x(2)
            sp_.wait_ge(S["b1_split_ok"], 3)
            sp_.dma_start(b1_turn, b1_split[:, :, :]).then_inc(S["b1_turn_in"], 16)
            sp_.wait_ge(S["b1_turn_in"], 16)
            sp_.dma_start(b1_rows[:, :, :], b1_turn.rearrange("e i f -> i e f")).then_inc(S["b1_rows_in"], 16)
            load_x(3)

            def load_tiles(g):
                sp_.wait_ge(scattered[g], 16 * TB * len(GROUPS[g]))
                if g:
                    sp_.wait_ge(S["xsT_mm"], FIRST[g])
                for (lo, hi), xs_ok in zip(CHUNKS[g], xs_in[g]):
                    sp_.dma_start(xs[:, lo:hi, :], x_tiles[g][lo * P:hi * P, :].rearrange("(i p) d -> p i d", p=P))\
                       .then_inc(xs_ok, 16)

            def store_tiles(g):
                for lo, hi in CHUNKS[g]:
                    sp_.wait_ge(S["ys_ok"], FIRST[g] + hi)
                    sp_.dma_start(y_tiles[g][lo * P:hi * P, :].rearrange("(i p) d -> p i d", p=P), ys[:, lo:hi, :])\
                       .then_inc(y_stored[g], 16)

            have = dict(load_tiles=load_tiles, store_tiles=store_tiles)
            for n in range(LAST + 1):
                steps(n, have)

        @block.tensor
        def _(pe):
            def turn_weights_0():
                pe.wait_ge(S["ident_ok"], 2)
                pe.wait_ge(S["vec_in"], 16 * 8)
                pe.transpose(psF[0][:, 0:n_rows], vec_rows[:, :], ident[0:n_rows, 0:n_rows])\
                  .then_inc(S["vecT_mm"], 1)
                for c in range(NC):
                    pe.wait_ge(S["tap_ok"], K * (c + 1))
                    bank = (psU, psD)[c]
                    for k in range(K):
                        t = pe.transpose(bank[:, k * P:(k + 1) * P], win_tap[:, c, k, :], ident[:, :])
                    t.then_inc(S["win_mm"], 1)
                for c in range(NC):
                    t = pe.transpose(psF[1][:, c * P:(c + 1) * P], win_raw[:, NC + c, :], ident[:, :])
                t.then_inc(S["win_mm"], 1)
                pe.wait_ge(S["xp_in"], 16)
                pe.wait_ge(S["dtw_in"], 16)
                pe.wait_ge(S["wo_in"], 16)
                pe.wait_ge(S["vec_ok"], 1)
                pe.wait_ge(S["win_ok"], 1)
                for c in range(NC):
                    pe.transpose(psF[0][:, c * 64:c * 64 + R + BC], xp_raw[:, c * P:(c + 1) * P],
                                 ident[0:R + BC, 0:R + BC])
                    pe.transpose(psU[0:R, c * P:(c + 1) * P], dtw_raw[:, c, :], ident[:, :])
                for c in range(NC):
                    t = pe.transpose(psF[0][:, 128 + c * P:128 + (c + 1) * P], wo_raw[:, c * P:(c + 1) * P],
                                     ident[:, :])
                t.then_inc(S["small_mm"], 1)

            def turn_expert(e):
                pe.wait_ge(S["w1_in"], 16 * E)
                pe.wait_ge(S["w2_in"], 16 * E)
                if e == 0:
                    pe.wait_ge(S["u_ok"], 2 * 2)
                else:
                    pe.wait_ge(S["w1_ok"], e)
                for j in range(NF):
                    t = pe.transpose(psU[:, j * P:(j + 1) * P], w1_raw[:, e * NF + j, :], ident[:, :])
                t.then_inc(S["w1_mm"], 1)
                if e:
                    pe.wait_ge(S["w2_ok"], e)
                for j in range(NF):
                    t = pe.transpose(psD[:, j * P:(j + 1) * P], w2_raw[:, e, j * P:(j + 1) * P], ident[:, :])
                t.then_inc(S["w2_mm"], 1)

            def b1_shift(e):
                if e == 0:
                    pe.wait_ge(S["w1_ok"], E)
                    pe.wait_ge(S["diag_ok"], 1)
                    pe.wait_ge(S["b1_in"], 16)
                pe.matmul(psU[0:E, :], lnb_diag[:, e, :], w1T[:, e, :], start=(e == 0), stop=False)
                if e == E - 1:
                    pe.matmul(psU[0:E, :], ident[0:E, 0:E], b1_sb[:, :], start=False, stop=True)\
                      .then_inc(S["b1_mm"], 1)

            def front_turn(b):
                if b == 0:
                    pe.wait_ge(S["small_ok"], 4)
                elif b != 2:
                    pe.wait_ge(S["u_ok"], 2 * b)
                else:
                    pe.wait_ge(S["b1_split_ok"], 3)
                pe.wait_ge(S["xh_ok"], b + 1)
                for j in range(TB):
                    t = pe.transpose(psU[:, j * P:(j + 1) * P], xh[:, j, :], ident[:, :])
                t.then_inc(S["hT_mm"], 1)

            def front_conv(b, c):
                pe.wait_ge(S["hT_ok"], b + 1)
                if c == 0:
                    if b == 0:
                        pe.wait_ge(S["win_ok"], 2)
                        pe.wait_ge(S["pads_ok"], 1)
                    elif b != 2:
                        pe.wait_ge(S["u_ok"], 2 * b)
                    else:
                        pe.wait_ge(S["w2_ok"], E)
                bank = (psD, psU)[c]
                for k in range(K):
                    t = pe.matmul(bank[:, :], winT[:, c, k, :], hT[:, k:k + L], start=(k == 0), stop=(k == K - 1))
                t.then_inc(S["conv_mm"], 1)

            def front_z(b):
                for i in range(2):
                    if b == 0:
                        pe.wait_ge(S["small_ok"], 4)
                    else:
                        pe.wait_ge(S["rv_ok"], 2 * b)
                    if b >= 3:
                        pe.wait_ge(S["b2_ok"], b - 2)
                    for j in range(2):
                        t = pe.matmul(psF[i][:, j * DI:(j + 1) * DI],
                                      hT[:, PADL + (2 * i + j) * P:PADL + (2 * i + j + 1) * P], wzT[:, :],
                                      start=True, stop=True)
                    t.then_inc(S["z_mm"], 1)

            def front_xproj(b):
                pe.wait_ge(S["u_ok"], 2 * b + 2)
                pe.wait_ge(S["zs_ok"], 2 * b + 1)
                for c in range(NC):
                    t = pe.matmul(psF[0][0:3 * BC + R, :], xpT[:, c, :], u[:, c, :], start=(c == 0), stop=(c == NC - 1))
                t.then_inc(S["xp_mm"], 1)

            def front_dt(b):
                pe.wait_ge(S["dtlow_ok"], b + 1)
                pe.wait_ge(S["rest_ok"], b + 1)
                pe.wait_ge(S["zs_ok"], 2 * b + 2)
                for c in range(NC):
                    pe.matmul(psF[c][:, :], dtwT[3 * BC:3 * BC + R, c, :], dtlow[3 * BC:3 * BC + R, :],
                              start=True, stop=True).then_inc(S["dt_mm"], 1)

            def spread_B(n):
                b, s = divmod(n, NS)
                pe.wait_ge(S["parts_ok"], b + 1)
                if n:
                    pe.wait_ge(S["dBu_ok"], n)
                pe.matmul(psB[:, :], pick[:, s:s + 1].broadcast_to([3 * BC, P]), parts[b % 2][:, :], start=True, stop=True)\
                  .then_inc(S["Bb_mm"], 1)

            def spread_C(n):
                b, s = divmod(n, NS)
                if n:
                    pe.wait_ge(S["Cb_ok"], n)
                pe.matmul(psC[:, :], pick[:, NS + s:NS + s + 1].broadcast_to([3 * BC, P]), parts[b % 2][:, :], start=True, stop=True)\
                  .then_inc(S["Cb_mm"], 1)

            def add_up(src, first):
                for j in range(TB):
                    for c in range(NC):
                        t = pe.matmul(psY[:, j, c * P:(c + 1) * P], src[:, c, j * P:(j + 1) * P], ident[:, :],
                                      start=first and j % 2 == 0 and c == 0, stop=True, is_transpose=True,
                                      skip_group_check=True)
                return t

            def sum_state(n):
                b, s = divmod(n, NS)
                if s == 0:
                    if b:
                        pe.wait_ge(S["yz_ok"], b)
                    pe.wait_ge(S["uD_ok"], 2 * b + 2)
                    add_up(uD, True)
                pe.wait_ge(S["hC_ok"], n + 1)
                add_up(hC[n % AHEAD], False).then_inc(S["sum_mm"], 1)

            def tail_turn(b):
                pe.wait_ge(S["yz_ok"], b + 1)
                pe.wait_ge(S["rv_ok"], 2 * min(b + 3, B))
                if b:
                    pe.wait_ge(S["b2_ok"], b)
                for c in range(NC):
                    for j in range(TB):
                        t = pe.transpose(psF[c][:, j * P:(j + 1) * P], yz[:, j, c * P:(c + 1) * P], ident[:, :])
                    t.then_inc(S["yzT_mm"], 1)

            def tail_proj(b):
                pe.wait_ge(S["yzT_ok"], 2 * b + 2)
                for j in range(TB):
                    for c in range(NC):
                        t = pe.matmul(psF[0][:, j * DM:(j + 1) * DM], yzT[:, c, j * P:(j + 1) * P], woT[:, c, :],
                                      start=(c == 0), stop=(c == NC - 1))
                t.then_inc(S["op_mm"], 1)

            def tail_xeT(b):
                pe.wait_ge(S["xe_ok"], b + 1)
                for j in range(TB):
                    t = pe.transpose(psF[1][:, j * P:(j + 1) * P], xe[b][:, j, :], ident[:, :])
                t.then_inc(S["xeT_mm"], 1)

            def tail_aff(b):
                pe.wait_ge(S["xeT_ok"], b + 1)
                pe.wait_ge(S["x1_ok"], b + 1)
                for j in range(TB):
                    t = pe.matmul(psF[0][:, j * E:(j + 1) * E], xeT[:, j * P:(j + 1) * P],
                                  vec[:, rows["cent"]:rows["cent"] + E], start=True, stop=True)
                t.then_inc(S["aff_mm"], 1)

            def tail_rank(b):
                pe.wait_ge(S["hot16_ok"], b + 1)
                pe.wait_ge(S["ones_ok"], 1)
                pe.wait_ge(S["before_ok"], 3)
                for j in range(TB + 1):
                    for i in range(min(j, TB)):
                        t = pe.matmul(psF[0][:, j * E:(j + 1) * E], ones16[:, :], hot16[:, i, :],
                                      start=(i == 0), stop=(j == TB and i == TB - 1))
                    if j < TB:
                        pe.matmul(psF[0][:, j * E:(j + 1) * E], before[:, :], hot16[:, j, :],
                                  start=(j == 0), stop=True)
                t.then_inc(S["rank_mm"], 1)

            def tail_hot(b):
                pe.wait_ge(S["hot_ok"], b + 1)
                for j in range(TB):
                    t = pe.transpose(psF[1][0:E, j * P:(j + 1) * P], hot[b][:, j, :], ident[:, :])
                t.then_inc(S["hotT_mm"], 1)

            def tail_bias(b):
                pe.wait_ge(S["hotT_ok"], b + 1)
                pe.wait_ge(S["b2_in"], 16)
                pe.wait_ge(S["rank_ok"], b + 1)
                for j in range(TB):
                    t = pe.matmul(psF[0][:, j * DM:(j + 1) * DM], hotT[:, j * P:(j + 1) * P], b2_sb[:, :],
                                  start=True, stop=True)
                t.then_inc(S["b2_mm"], 1)

            expert = {}

            def take(m):
                g = 0 if m < FIRST[1] else 1
                i = m - FIRST[g]
                if i == 0:
                    pe.wait_ge(S["te_ok"], g + 1)
                if m == 0:
                    pe.wait_ge(S["u_ok"], 2 * B)
                    pe.wait_ge(S["b1_rows_in"], 16)
                    pe.wait_ge(S["w1g_ok"], E)
                    pe.wait_ge(S["ones_ok"], 1)
                for (lo, hi), xs_ok in zip(CHUNKS[g], xs_in[g]):
                    if i == lo:
                        pe.wait_ge(xs_ok, 16)
                if m:
                    pe.wait_ge(S["relu_ok"], m)
                pe.transpose(psU[:, 0:P], xs[:, i, :], ident[:, :]).then_inc(S["xsT_mm"], 1)
                expert[m] = pe.value_load(te[g][0:1, i:i + 1], min_val=0, max_val=E - 1)

            def tile(pair):
                m, d = pair
                if m is not None:
                    take(m)
                if d is not None:
                    pe.wait_ge(S["relu_ok"], d + 1)
                    if d:
                        pe.wait_ge(S["ys_ok"], d)
                    for j in range(NF):
                        t = pe.transpose(psD[:, j * P:(j + 1) * P], hn[:, j * P:(j + 1) * P], ident[:, :])
                    t.then_inc(S["hh_mm"], 1)
                if m is not None:
                    pe.wait_ge(S["xsT_ok"], m + 1)
                    pe.matmul(psU[:, :], ones16[0:3, :], b1_rows[:, bass.ds(expert[m], 1), :],
                              start=True, stop=False)
                    pe.matmul(psU[:, :], xsT[:, :], w1T[:, bass.ds(expert[m], 1), :], start=False, stop=True)\
                      .then_inc(S["up_mm"], 1)
                if d is not None:
                    pe.wait_ge(S["hh_ok"], d + 1)
                    for j in range(NF):
                        t = pe.matmul(psD[:, 0:DM], hh[:, j, :], w2T[:, bass.ds(expert[d], 1), j, :],
                                      start=(j == 0), stop=(j == NF - 1))
                    t.then_inc(S["down_mm"], 1)

            have = dict(tail_turn=tail_turn, tail_proj=tail_proj, tail_xeT=tail_xeT, tail_aff=tail_aff,
                        tail_rank=tail_rank, tail_hot=tail_hot, tail_bias=tail_bias, tile=tile, turn_expert=turn_expert,
                        b1_shift=b1_shift, front_turn=front_turn,
                        front_conv0=lambda b: front_conv(b, 0), front_conv1=lambda b: front_conv(b, 1), front_z=front_z, front_xproj=front_xproj, front_dt=front_dt)
            turn_weights_0()
            front_turn(0)
            front_conv(0, 0)
            front_conv(0, 1)
            front_z(0)
            front_xproj(0)
            front_dt(0)
            spread_B(0)
            spread_C(0)
            for n in range(LAST + 1):
                if n + 1 < B * NS:
                    spread_B(n + 1)
                if LAG <= n < B * NS and n % NS != LAG:
                    sum_state(n - LAG)
                if n + 1 < B * NS:
                    spread_C(n + 1)
                if n == B * NS:
                    for i in range(n - LAG, n):
                        sum_state(i)
                steps(n, have)
                if n < B * NS and n % NS == LAG:
                    sum_state(n - LAG)

        @block.scalar
        def _(act):
            for dst, src, name in (
                    (win_raw[:, :, :], in_proj_w.rearrange("(j p) d -> p j d", p=P), "win_in"),
                    (convw[:, :, :], conv_w.rearrange("(c p) k -> p c k", p=P), "convw_in"),
                    (xp_raw[:, :], x_proj_w, "xp_in"),
                    (dtw_raw[:, :, :], dt_proj_w.rearrange("(c p) r -> p c r", p=P), "dtw_in"),
                    (wo_raw[:, :], out_proj_w, "wo_in"),
                    (alog[:, :, :], A_log.rearrange("(c p) s -> p c s", p=P), "alog_in"),
                    (b2_sb[:, :], b2, "b2_in")):
                act.dma_start(dst, src).then_inc(S[name], 16)

            def weights_0():
                act.preload_act_table_set("natural_log_exp_and_others")
                act.wait_ge(S["vecT_mm"], 1)
                act.activation(vec[:, :], psF[0][:, 0:n_rows], ACT.Copy).then_inc(S["vec_ok"], 1)
                act.wait_ge(S["alog_in"], 16)
                act.activation(Aneg[:, :, :], alog[:, :, :], ACT.Exp).then_inc(S["aexp_ok"], 1)
                for c in range(NC):
                    act.wait_ge(S["win_mm"], c + 1)
                    act.activation(winT[:, c, :, :].rearrange("p k e -> p (k e)"), (psU, psD)[c][:, :], ACT.Copy)\
                       .then_inc(S["win_ok"], 1)
                act.wait_ge(S["win_mm"], 3)
                act.activation(wzT[:, :], psF[1][:, 0:DI], ACT.Copy).then_inc(S["win_ok"], 1)

            def expert_weights(e):
                act.wait_ge(S["w1_mm"], e + 1)
                act.activation(w1T[:, e, :], psU[:, :], ACT.Copy).then_inc(S["w1_ok"], 1)
                act.wait_ge(S["w2_mm"], e + 1)
                act.activation(w2T[:, e, :, :].rearrange("p j d -> p (j d)"), psD[:, :], ACT.Copy)\
                   .then_inc(S["w2_ok"], 1)

            roots = [0]

            def root(v2, ln, y, v_ok, y_ok, b):
                act.wait_ge(v_ok, b + 1)
                roots[0] += 1
                act.activation(ln[:, :, :], v2[:, :, :], ACT.Ln).then_inc(S["lny_ok"], 1)
                act.wait_ge(S["lny_ok"], roots[0])
                act.activation(y[:, :, :], ln[:, :, :], ACT.Exp, scale=-0.5).then_inc(y_ok, 1)

            def front_root(b):
                root(vv, lny[0], yy, S["vv_ok"], S["y_ok"], b)

            def tail_root(b):
                root(vv2, lny[1], yy2, S["vv2_ok"], S["y2_ok"], b)

            def front_res(b):
                act.wait_ge(S["stat_ok"], b + 1)
                if b >= 2:
                    act.wait_ge(S["x1_ok"], b - 1)
                for j in range(TB):
                    t = act.activation(xres[b % 2][:, j, :], xt[b % 2][:, j, :], ACT.Identity,
                                       bias=sc2[:, j:j + 1], scale=sc1[:, j:j + 1])
                t.then_inc(S["xres_ok"], 1)

            def front_hT(b):
                act.wait_ge(S["hT_mm"], b + 1)
                if b == 0:
                    act.wait_ge(S["vec_ok"], 1)
                else:
                    act.wait_ge(S["z_mm"], 2 * b)
                act.activation(hT[:, PADL:], psU[:, :], ACT.Identity, bias=col("beta"), scale=col("gamma"))\
                   .then_inc(S["hT_ok"], 1)

            def front_silu(b):
                act.preload_act_table_set("silu_and_others")
                if b:
                    act.wait_ge(S["dtu_ok"], b)
                for c in range(NC):
                    act.wait_ge(S["conv_mm"], 2 * b + c + 1)
                    act.activation(u[:, c, :], (psD, psU)[c][:, :], ACT.Silu, bias=col("conv_b", c))\
                       .then_inc(S["u_ok"], 1)
                if b >= 2:
                    act.wait_ge(S["yz_ok"], b - 1)
                for i in range(2):
                    act.wait_ge(S["z_mm"], 2 * b + i + 1)
                    act.activation(zs[b % 2][:, 2 * i:2 * i + 2, :].rearrange("p j d -> p (j d)"), psF[i][:, :],
                                   ACT.Silu).then_inc(S["zs_ok"], 1)
                act.preload_act_table_set("natural_log_exp_and_others")

            def front_uD(b):
                if b:
                    act.wait_ge(S["sum_mm"], (b - 1) * NS + 1)
                act.wait_ge(S["u_ok"], 2 * b + 2)
                for c in range(NC):
                    act.activation(uD[:, c, :], u[:, c, :], ACT.Copy, scale=col("D", c))\
                       .then_inc(S["uD_ok"], 1)

            def front_abs(b):
                if b:
                    act.wait_ge(S["tv_ok"], b)
                if b >= 2:
                    act.wait_ge(S["dA_ok"], 2 * (b - 1) * NS)
                for c in range(NC):
                    act.wait_ge(S["dt_mm"], 2 * b + c + 1)
                    act.activation(av[:, c, :], psF[c][:, :], ACT.Abs, bias=col("dt_b", c)).then_inc(S["av_ok"], 1)
                    act.activation(dt[b % 2][:, c, :], psF[c][:, :], ACT.Relu, bias=col("dt_b", c))\
                       .then_inc(S["rv_ok"], 1)

            def front_exp(b):
                if b:
                    act.wait_ge(S["lw_ok"], b)
                act.wait_ge(S["av_ok"], 2 * b + 2)
                act.activation(zz[:, :, :], av[:, :, :], ACT.Exp, scale=-1.0).then_inc(S["zz_ok"], 1)
                act.wait_ge(S["zz_ok"], b + 1)
                act.wait_ge(S["parts_ok"], b + 1)
                act.activation(ww[:, :, :], zz[:, :, :], ACT.Copy, bias=1.0).then_inc(S["ww_ok"], 1)

            def front_log(b):
                if b:
                    act.wait_ge(S["dt_ok"], b)
                act.wait_ge(S["ww_ok"], b + 1)
                act.preload_act_table_set("natural_log")
                act.activation(lw[:, :, :], ww[:, :, :], ACT.Ln).then_inc(S["lw_ok"], 1)
                act.preload_act_table_set("natural_log_exp_and_others")

            def decay(n):
                b, s = divmod(n, NS)
                if s == 0:
                    act.wait_ge(S["dt_ok"], b + 1)
                if n == 0:
                    act.wait_ge(S["aneg_ok"], 1)
                if n >= AHEAD:
                    act.wait_ge(S["h_ok"], 2 * (n - AHEAD + 1))
                for c in range(NC):
                    act.activation(dA[n % AHEAD][:, c, :], dt[b % 2][:, c, :], ACT.Exp, scale=Aneg[:, c, s:s + 1])\
                       .then_inc(S["dA_ok"], 1)

            def copy_C(n):
                act.wait_ge(S["Cb_mm"], n + 1)
                if n >= AHEAD:
                    act.wait_ge(S["hC_ok"], n - AHEAD + 1)
                act.activation(Cb[n % AHEAD][:, :], psC[:, :], ACT.Copy).then_inc(S["Cb_ok"], 1)

            def tail_yzT(b):
                if b:
                    act.wait_ge(S["op_mm"], b)
                for c in range(NC):
                    act.wait_ge(S["yzT_mm"], 2 * b + c + 1)
                    act.activation(yzT[:, c, :], psF[c][:, :], ACT.Copy).then_inc(S["yzT_ok"], 1)

            def tail_xeT(b):
                act.wait_ge(S["xeT_mm"], b + 1)
                if b:
                    act.wait_ge(S["aff_mm"], b)
                act.activation(xeT[:, :], psF[1][:, :], ACT.Copy).then_inc(S["xeT_ok"], 1)

            def tail_base(b):
                act.wait_ge(S["nr_ok"], b + 1)
                act.wait_ge(S["x1_ok"], b + 1)
                for j in range(TB):
                    t = act.activation(base[b][:, j, :], x1[:, j, :], ACT.Identity, bias=nr[:, 1, j:j + 1],
                                       scale=nr[:, 0, j:j + 1])
                t.then_inc(S["base_ok"], 1)

            def tail_gate(b):
                act.wait_ge(S["mx_ok"], b + 1)
                act.activation(gex[:, :], mx[:, :], ACT.Exp, scale=-1.0).then_inc(S["gex_ok"], 1)

            def tail_hotT(b):
                act.wait_ge(S["hotT_mm"], b + 1)
                if b:
                    act.wait_ge(S["b2_mm"], b)
                act.activation(hotT[:, :], psF[1][0:E, :], ACT.Copy).then_inc(S["hotT_ok"], 1)

            def tile(pair):
                m, d = pair
                if m is not None:
                    act.wait_ge(S["xsT_mm"], m + 1)
                    if m:
                        act.wait_ge(S["up_mm"], m)
                    act.activation(xsT[:, :], psU[:, 0:P], ACT.Copy).then_inc(S["xsT_ok"], 1)
                    act.wait_ge(S["up_mm"], m + 1)
                    if m:
                        act.wait_ge(S["hh_mm"], m)
                    act.activation(hn[:, :], psU[:, :], ACT.Relu).then_inc(S["relu_ok"], 1)
                if d is not None:
                    g = 0 if d < FIRST[1] else 1
                    act.wait_ge(S["down_mm"], d + 1)
                    if g and d == FIRST[g]:
                        act.wait_ge(y_stored[g - 1], 16 * len(CHUNKS[g - 1]))
                    act.activation(ys[:, d - FIRST[g], :], psD[:, 0:DM], ACT.Copy).then_inc(S["ys_ok"], 1)

            def store(b):
                act.wait_ge(S["res_ok"], b + 1)
                act.dma_start(out[b].rearrange("(j p) d -> p j d", p=P), res[b][:, :, :]).then_inc(stored[b], 16)

            have = dict(tail_turn=tail_yzT, tail_root=tail_root, tail_xeT=tail_xeT, tail_base=tail_base,
                        tail_gate=tail_gate, tail_hot=tail_hotT, tile=tile, store=store, turn_expert=expert_weights,
                        front_root=front_root, front_res=front_res, front_turn=front_hT,
                        front_silu=front_silu, front_abs=front_abs, front_exp=front_exp,
                        front_log=front_log, front_uD=front_uD)
            weights_0()
            front_root(0)
            front_res(0)
            front_hT(0)
            front_silu(0)
            front_abs(0)
            front_exp(0)
            front_log(0)
            front_uD(0)
            decay(0)
            copy_C(0)
            decay(1)
            for n in range(LAST + 1):
                if n + 1 < B * NS:
                    copy_C(n + 1)
                if n + 2 < B * NS:
                    decay(n + 2)
                steps(n, have)
            for b in range(B):
                act.wait_ge(stored[b], 16)

        @block.vector
        def _(dve):
            chain = [0]

            def link(t):
                chain[0] += 1
                t.then_inc(S["dve_chain"], 1)
                dve.wait_ge(S["dve_chain"], chain[0])

            def weights_0():
                dve.memset(hT[:, 0:PADL], 0.0).then_inc(S["pads_ok"], 1)
                for e in range(E):
                    t = dve.memset(firstw[:, :, e:e + 1], float(E - e))
                t.then_inc(S["firstw_ok"], 1)
                dve.memset(xe[0][:, :, :], 0.0).then_inc(S["zero_ok"], 1)
                dve.memset(one_e[:, :], 1.0)
                for i in range(ROUNDS[0]):
                    dve.memset(rounds[:, :, i:i + 1], float(P * i))
                for i in range(NT[0]):
                    t = dve.memset(tile_no[:, i, :], float(i))
                t.then_inc(S["consts_ok"], 1)
                dve.memset(ones16[:, :], 1.0).then_inc(S["ones_ok"], 1)
                link(dve.memset(lnb_diag[:, :, :], 0.0))
                dve.wait_ge(S["win_in"], 16)
                dve.wait_ge(S["convw_in"], 16)
                for c in range(NC):
                    for k in range(K):
                        dve.tensor_scalar(win_tap[:, c, k, :], win_raw[:, c, :], convw[:, c, k:k + 1], None, ALU.mult)\
                           .then_inc(S["tap_ok"], 1)
                dve.wait_ge(S["vec_ok"], 1)
                dve.tensor_copy(lnb_diag[:, :, :].rearrange("p a b -> p (a b)")[:, 0:E * E:E + 1],
                                vec[:, rows["ln_b"]:rows["ln_b"] + E]).then_inc(S["diag_ok"], 1)
                dve.wait_ge(S["aexp_ok"], 1)
                dve.tensor_scalar(Aneg[:, :, :], Aneg[:, :, :], -1.0, None, ALU.mult).then_inc(S["aneg_ok"], 1)

            def weights_1():
                dve.wait_ge(S["pick_ok"], 1 + 3)
                dve.tensor_copy(pick[:, :], pick32[:, :])\
                   .then_inc(S["pick_ok"], 1)
                dve.wait_ge(S["before_ok"], 2)
                dve.tensor_copy(before[:, :], before32[:, :]).then_inc(S["before_ok"], 1)
                dve.wait_ge(S["small_mm"], 1)
                xp = psF[0][:, 0:NC * 64].rearrange("p (c r) -> p c r", c=NC)
                for i in range(3):
                    t = dve.tensor_copy(xpT[:, :, i * BC:(i + 1) * BC], xp[:, :, R:R + BC])
                t.then_inc(S["small_ok"], 1)
                dve.tensor_copy(xpT[:, :, 3 * BC:3 * BC + R], xp[:, :, 0:R]).then_inc(S["small_ok"], 1)
                dve.tensor_copy(dtwT[3 * BC:3 * BC + R, :, :].rearrange("p c d -> p (c d)"), psU[0:R, 0:NC * P])\
                   .then_inc(S["small_ok"], 1)
                dve.tensor_copy(woT[:, :, :].rearrange("p c d -> p (c d)"), psF[0][:, 128:128 + NC * P])\
                   .then_inc(S["small_ok"], 1)

            def split_b1(_):
                dve.wait_ge(S["b1_mm"], 1)
                dve.tensor_copy(b1_split[:, 0, :], psU[0:E, :]).then_inc(S["b1_split_ok"], 1)
                dve.wait_ge(S["b1_split_ok"], 1)
                link(dve.tensor_tensor(b1_rest[:, :], psU[0:E, :], b1_split[:, 0, :], ALU.subtract))
                dve.tensor_copy(b1_split[:, 1, :], b1_rest[:, :]).then_inc(S["b1_split_ok"], 1)
                dve.wait_ge(S["b1_split_ok"], 2)
                link(dve.tensor_tensor(b1_rest[:, :], b1_rest[:, :], b1_split[:, 1, :], ALU.subtract))
                dve.tensor_copy(b1_split[:, 2, :], b1_rest[:, :]).then_inc(S["b1_split_ok"], 1)

            def gamma_w1(e):
                dve.tensor_scalar(w1T[:, e, :], w1T[:, e, :], col("ln_g", e), None, ALU.mult)\
                   .then_inc(S["w1g_ok"], 1)

            def moments(src, st, m, v2, ok):
                for j in range(TB):
                    t = dve.bn_stats(st[:, j, :], src[:, j, :])
                link(t)
                for j in range(TB):
                    t = dve.bn_aggr(m[:, j, :], st[:, j, :])
                link(t)
                link(dve.tensor_scalar(v2[:, 0, :], m[:, :, 1], EPS, None, ALU.add))
                dve.scalar_tensor_tensor(out=v2[:, 1, :], in0=v2[:, 0, :], scalar=EPS, in1=m[:, :, 1],
                                         op0=ALU.mult, op1=ALU.add).then_inc(ok, 1)

            def newton(v2, y, r2):
                link(dve.tensor_tensor(r2[:, :, :], y[:, :, :], y[:, :, :], ALU.mult))
                link(dve.tensor_tensor(r2[:, :, :], r2[:, :, :], v2[:, :, :], ALU.mult))
                link(dve.tensor_scalar(r2[:, :, :], r2[:, :, :], -0.5, 1.5, ALU.mult, ALU.add))
                link(dve.tensor_tensor(r2[:, :, :], r2[:, :, :], y[:, :, :], ALU.mult))

            def front_moments(b):
                dve.wait_ge(x_in[b], 16)
                moments(xt[b % 2], bst, mv, vv, S["vv_ok"])

            def front_norm(b):
                dve.wait_ge(S["y_ok"], b + 1)
                newton(vv, yy, rs)
                if b:
                    dve.wait_ge(S["xres_ok"], b)
                    dve.wait_ge(S["hT_mm"], b)
                dve.scalar_tensor_tensor(out=sc2[:, :], in0=mv[:, :, 0], scalar=-1.0, in1=rs[:, 0, :],
                                         op0=ALU.mult, op1=ALU.mult)
                dve.tensor_scalar(sc1[:, :], rs[:, 0, :], 1.0, None, ALU.add).then_inc(S["stat_ok"], 1)
                for j in range(TB):
                    t = dve.tensor_scalar(xh[:, j, :], xt[b % 2][:, j, :], mv[:, j, 0:1], rs[:, 1, j:j + 1],
                                          ALU.subtract, ALU.mult)
                t.then_inc(S["xh_ok"], 1)

            def front_low(b):
                dve.wait_ge(S["xp_mm"], b + 1)
                if b:
                    dve.wait_ge(S["lw_ok"], b)
                    dve.wait_ge(S["dt_mm"], 2 * b)
                dve.tensor_copy(dtlow[3 * BC:3 * BC + R, :], psF[0][3 * BC:3 * BC + R, :]).then_inc(S["dtlow_ok"], 1)
                if b >= 2:
                    dve.wait_ge(S["Bb_mm"], (b - 1) * NS)
                    dve.wait_ge(S["Cb_mm"], (b - 1) * NS)
                link(dve.tensor_copy(parts[b % 2][:, :], psF[0][0:3 * BC, :]))
                dve.tensor_tensor(rest[:, :], psF[0][0:3 * BC, :], parts[b % 2][:, :], ALU.subtract)\
                   .then_inc(S["rest_ok"], 1)

            def front_parts(b):
                pt = parts[b % 2]
                dve.wait_ge(S["rest_ok"], b + 1)
                dve.tensor_copy(pt[BC:2 * BC, :], rest[BC:2 * BC, :])
                link(dve.tensor_copy(pt[2 * BC:3 * BC, :], rest[2 * BC:3 * BC, :]))
                link(dve.tensor_tensor(rest[2 * BC:3 * BC, :], rest[2 * BC:3 * BC, :], pt[2 * BC:3 * BC, :],
                                       ALU.subtract))
                dve.tensor_copy(pt[2 * BC:3 * BC, :], rest[2 * BC:3 * BC, :]).then_inc(S["parts_ok"], 1)

            def front_rounding(b):
                dve.wait_ge(S["ww_ok"], b + 1)
                dve.scalar_tensor_tensor(out=zz[:, :, :].rearrange("p c t -> p (c t)"),
                                         in0=ww[:, :, :].rearrange("p c t -> p (c t)"), scalar=-1.0,
                                         in1=zz[:, :, :].rearrange("p c t -> p (c t)"), op0=ALU.add, op1=ALU.subtract)\
                   .then_inc(S["nc_ok"], 1)

            def inject(n):
                b, s = divmod(n, NS)
                if s == 0:
                    dve.wait_ge(S["dtu_ok"], b + 1)
                dve.wait_ge(S["Bb_mm"], n + 1)
                if n >= 2:
                    dve.wait_ge(S["h_ok"], 2 * (n - 1))
                dve.tensor_tensor(dBu[n % 2][:, :, :], dtu[b % 2][:, :, :],
                                  psB[:, :].unsqueeze(1).broadcast_to([P, NC, L]), ALU.mult).then_inc(S["dBu_ok"], 1)

            def scan(n):
                dve.wait_ge(S["dBu_ok"], n + 1)
                if n >= AHEAD:
                    dve.wait_ge(S["hC_ok"], n - AHEAD + 1)
                for c in range(NC):
                    dve.wait_ge(S["dA_ok"], 2 * n + c + 1)
                    dve.tensor_tensor_scan(hs[n % AHEAD][:, c, :], dA[n % AHEAD][:, c, :], dBu[n % 2][:, c, :], 0.0,
                                           ALU.mult, ALU.add).then_inc(S["h_ok"], 1)

            def tail_yz(b):
                dve.wait_ge(S["sum_mm"], (b + 1) * NS)
                if b:
                    dve.wait_ge(S["yzT_mm"], 2 * b)
                for i in range(2):
                    t = dve.tensor_tensor(yz[:, 2 * i:2 * i + 2, :], psY[:, 2 * i:2 * i + 2, :],
                                          zs[b % 2][:, 2 * i:2 * i + 2, :], ALU.mult)
                t.then_inc(S["yz_ok"], 1)

            def tail_x1(b):
                dve.wait_ge(S["op_mm"], b + 1)
                dve.wait_ge(S["xres_ok"], b + 1)
                if b:
                    dve.wait_ge(S["base_ok"], b)
                if b:
                    dve.wait_ge(S["xe_ok"], b)
                dve.tensor_tensor(x1[:, :, :].rearrange("p j d -> p (j d)"), psF[0][:, :],
                                  xres[b % 2][:, :, :].rearrange("p j d -> p (j d)"), ALU.add).then_inc(S["x1_ok"], 1)
                dve.wait_ge(S["x1_ok"], b + 1)
                moments(x1, bst2, mv2, vv2, S["vv2_ok"])

            def tail_norm(b):
                dve.wait_ge(S["y2_ok"], b + 1)
                newton(vv2, yy2, rs2)
                dve.tensor_scalar(nr[:, 0, :], rs2[:, 0, :], 1.0, None, ALU.add)
                dve.scalar_tensor_tensor(out=nr[:, 1, :], in0=mv2[:, :, 0], scalar=-1.0, in1=rs2[:, 0, :],
                                         op0=ALU.mult, op1=ALU.mult).then_inc(S["nr_ok"], 1)
                link(dve.tensor_tensor(nr[:, 2, :], rs2[:, 0, :], rs2[:, 1, :], ALU.mult))
                link(dve.tensor_tensor(nr[:, 2, :], nr[:, 2, :], vv2[:, 1, :], ALU.mult))
                if b == 0:
                    dve.wait_ge(S["tiles_zero"], 16 * sum(len(c) for c in CHUNKS))
                for j in range(TB):
                    t = dve.tensor_scalar(xe[b][:, j, :], x1[:, j, :], mv2[:, j, 0:1], rs2[:, 1, j:j + 1],
                                          ALU.subtract, ALU.mult)
                t.then_inc(S["xe_ok"], 1)

            def tail_choose(b):
                dve.wait_ge(S["aff_mm"], b + 1)
                link(dve.tensor_tensor(aff[:, :, :], psF[0][:, 0:TB * E].rearrange("p (j e) -> p j e", e=E),
                                       nr[:, 2, :].unsqueeze(2).broadcast_to([P, TB, E]), ALU.mult))
                if b:
                    dve.wait_ge(S["gex_ok"], b)
                dve.tensor_reduce(mx[:, :], aff[:, :, :], AX.X, ALU.max).then_inc(S["mx_ok"], 1)
                dve.wait_ge(S["mx_ok"], b + 1)
                link(dve.tensor_tensor(score[:, :, :], aff[:, :, :], mx[:, :].unsqueeze(2).broadcast_to([P, TB, E]),
                                       ALU.is_ge))
                link(dve.tensor_tensor(score[:, :, :], score[:, :, :], firstw[:, :, :], ALU.mult))
                link(dve.tensor_reduce(mx2[:, :], score[:, :, :], AX.X, ALU.max))
                dve.tensor_tensor(hot[b][:, :, :], score[:, :, :], mx2[:, :].unsqueeze(2).broadcast_to([P, TB, E]),
                                  ALU.is_equal).then_inc(S["hot_ok"], 1)
                dve.wait_ge(S["hot_ok"], b + 1)
                if b:
                    dve.wait_ge(S["rank_mm"], b)
                dve.tensor_copy(hot16[:, :, :], hot[b][:, :, :]).then_inc(S["hot16_ok"], 1)

            def tail_gate(b):
                dve.wait_ge(S["gex_ok"], b + 1)
                g = gate[b]
                link(dve.tensor_scalar(g[:, :], gex[:, :], 1.0, None, ALU.add))
                dve.reciprocal(g[:, :], g[:, :]).then_inc(S["gate_ok"], 1)

            def tail_rank(b):
                before_b = not any(b == g[0] for g in GROUPS)
                dve.wait_ge(S["rank_mm"], b + 1)
                ranks = psF[0][:, 0:TB * E].rearrange("p (j e) -> p j e", e=E)
                counts = psF[0][:, TB * E:(TB + 1) * E]
                if before_b:
                    link(dve.tensor_tensor(place[:, :, :], ranks,
                                           count[b - 1][:, :].unsqueeze(1).broadcast_to([P, TB, E]), ALU.add))
                    dve.tensor_tensor(count[b][:, :], counts, count[b - 1][:, :], ALU.add).then_inc(S["rank_ok"], 1)
                    link(dve.tensor_tensor(place[:, :, :], place[:, :, :], hot[b][:, :, :], ALU.mult))
                else:
                    link(dve.tensor_tensor(place[:, :, :], ranks, hot[b][:, :, :], ALU.mult))
                    dve.tensor_copy(count[b][:, :], counts).then_inc(S["rank_ok"], 1)
                link(dve.tensor_reduce(rank[b][:, :], place[:, :, :], AX.X, ALU.add))

            def route(g):
                n_rounds, n_tiles = ROUNDS[g], NT[g]
                dve.wait_ge(S["rank_ok"], GROUPS[g][-1] + 1)
                link(dve.tensor_tensor(more[:, :, 0:n_rounds],
                                       count[GROUPS[g][-1]][:, :].unsqueeze(2).broadcast_to([P, E, n_rounds]),
                                       rounds[:, :, 0:n_rounds], ALU.is_gt))
                link(dve.tensor_reduce(tiles[:, :], more[:, :, 0:n_rounds], AX.X, ALU.add))
                link(dve.tensor_tensor_scan(ends[:, :], one_e[:, :], tiles[:, :], 0.0, ALU.mult, ALU.add))
                link(dve.tensor_scalar(ends128[:, :], ends[:, :], float(P), None, ALU.mult))
                link(dve.scalar_tensor_tensor(out=start[:, :], in0=tiles[:, :], scalar=-float(P), in1=ends128[:, :],
                                              op0=ALU.mult, op1=ALU.add))
                for b in GROUPS[g]:
                    link(dve.tensor_tensor(place[:, :, :], start[:, :].unsqueeze(1).broadcast_to([P, TB, E]),
                                           hot[b][:, :, :], ALU.mult))
                    link(dve.tensor_reduce(slotf[:, :], place[:, :, :], AX.X, ALU.add))
                    dve.tensor_tensor(slot[b][:, :], slotf[:, :], rank[b][:, :], ALU.add).then_inc(S["slot_ok"], 1)
                    dve.wait_ge(S["slot_ok"], b + 1)
                link(dve.tensor_tensor(past[:, 0:n_tiles, :], ends[0:1, :].unsqueeze(1).broadcast_to([1, n_tiles, E]),
                                       tile_no[:, 0:n_tiles, :], ALU.is_le))
                link(dve.tensor_reduce(te_f[:, 0:n_tiles], past[:, 0:n_tiles, :], AX.X, ALU.add))
                dve.tensor_scalar(te[g][:, :], te_f[:, 0:n_tiles], float(E - 1), None, ALU.min).then_inc(S["te_ok"], 1)

            def tail_b2(b):
                dve.wait_ge(S["b2_mm"], b + 1)
                dve.wait_ge(S["base_ok"], b + 1)
                dve.wait_ge(S["gate_ok"], b + 1)
                for j in range(TB):
                    t = dve.scalar_tensor_tensor(out=base[b][:, j, :], in0=psF[0][:, j * DM:(j + 1) * DM],
                                                 scalar=gate[b][:, j:j + 1], in1=base[b][:, j, :],
                                                 op0=ALU.mult, op1=ALU.add)
                t.then_inc(S["b2_ok"], 1)

            def tile(pair):
                d = pair[1]
                if d is not None:
                    dve.wait_ge(S["hh_mm"], d + 1)
                    if d:
                        dve.wait_ge(S["down_mm"], d)
                    dve.tensor_copy(hh[:, :, :].rearrange("p j s -> p (j s)"), psD[:, :]).then_inc(S["hh_ok"], 1)

            def finish(b):
                dve.wait_ge(gathered[b], 16 * TB)
                dve.wait_ge(S["b2_ok"], b + 1)
                for j in range(TB):
                    t = dve.scalar_tensor_tensor(out=res[b][:, j, :], in0=yg[b][:, j, :],
                                                 scalar=gate[b][:, j:j + 1], in1=base[b][:, j, :],
                                                 op0=ALU.mult, op1=ALU.add)
                t.then_inc(S["res_ok"], 1)

            have = dict(tail_moments=tail_x1, tail_norm=tail_norm, tail_choose=tail_choose,
                        tail_gate=tail_gate, tail_rank=tail_rank, route=route, tail_bias=tail_b2, tile=tile,
                        finish=finish, split_b1=split_b1, gamma_w1=gamma_w1,
                        front_moments=front_moments, front_norm=front_norm, front_low=front_low, front_parts=front_parts,
                        front_rounding=front_rounding)
            weights_0()
            front_moments(0)
            front_norm(0)
            weights_1()
            front_low(0)
            front_parts(0)
            front_rounding(0)
            inject(0)
            for n in range(LAST + 1):
                if n + 1 < B * NS:
                    inject(n + 1)
                if NS < n < B * NS and n % NS == LAG:
                    tail_yz(n // NS - 1)
                if n == B * NS:
                    tail_yz(B - 1)
                if n < B * NS:
                    scan(n)
                steps(n, have)

        @block.gpsimd
        def _(pool):
            pool.memset(ident[:, :], 0.0).then_inc(S["ident_ok"], 1)
            pool.memset(pick32[:, :], 0.0).then_inc(S["pick_ok"], 1)
            pool.wait_ge(S["ident_ok"], 1)
            pool.affine_select(out=ident[:, :], in_=ident[:, :], compare_op=ALU.not_equal, fill=1.0, base=0,
                               pattern=[[-1, P]], channel_multiplier=1).then_inc(S["ident_ok"], 1)
            for i in range(3):
                pool.wait_ge(S["pick_ok"], i + 1)
                pool.affine_select(out=pick32[:, :], in_=pick32[:, :], compare_op=ALU.not_equal, fill=1.0,
                                   base=-BC * i, pattern=[[-1, BC]], channel_multiplier=1).then_inc(S["pick_ok"], 1)
            pool.memset(before32[:, :], 1.0).then_inc(S["before_ok"], 1)
            pool.wait_ge(S["before_ok"], 1)
            pool.affine_select(out=before32[:, :], in_=before32[:, :], compare_op=ALU.is_gt, fill=0.0, base=0,
                               pattern=[[1, P]], channel_multiplier=-1).then_inc(S["before_ok"], 1)

            flat = "p c t -> p (c t)"

            def front_sub(b):
                pool.wait_ge(S["nc_ok"], b + 1)
                pool.wait_ge(S["rv_ok"], 2 * b + 2)
                pool.tensor_tensor(dt[b % 2][:, :, :].rearrange(flat), dt[b % 2][:, :, :].rearrange(flat),
                                   zz[:, :, :].rearrange(flat), ALU.subtract).then_inc(S["tv_ok"], 1)

            def front_add(b):
                pool.wait_ge(S["tv_ok"], b + 1)
                pool.wait_ge(S["lw_ok"], b + 1)
                pool.tensor_tensor(dt[b % 2][:, :, :].rearrange(flat), dt[b % 2][:, :, :].rearrange(flat),
                                   lw[:, :, :].rearrange(flat), ALU.add).then_inc(S["dt_ok"], 1)

            def front_dtu(b):
                pool.wait_ge(S["dt_ok"], b + 1)
                pool.wait_ge(S["u_ok"], 2 * b + 2)
                if b >= 2:
                    pool.wait_ge(S["dBu_ok"], (b - 1) * NS)
                pool.tensor_tensor(dtu[b % 2][:, :, :].rearrange(flat), dt[b % 2][:, :, :].rearrange(flat),
                                   u[:, :, :].rearrange(flat), ALU.mult).then_inc(S["dtu_ok"], 1)

            def read_out(n):
                pool.wait_ge(S["Cb_ok"], n + 1)
                pool.wait_ge(S["h_ok"], 2 * n + 2)
                if n >= AHEAD:
                    pool.wait_ge(S["sum_mm"], n - AHEAD + 1)
                pool.tensor_tensor(hC[n % AHEAD][:, :, :], hs[n % AHEAD][:, :, :],
                                   Cb[n % AHEAD][:, :].unsqueeze(1).broadcast_to([P, NC, L]), ALU.mult)\
                    .then_inc(S["hC_ok"], 1)

            def scatter(g):
                if g == 0:
                    pool.wait_ge(S["tiles_zero"], 16 * sum(len(c) for c in CHUNKS))
                for b in GROUPS[g]:
                    pool.wait_ge(S["slot_ok"], b + 1)
                    pool.wait_ge(S["xe_ok"], b + 1)
                    for j in range(TB):
                        pool.indirect_dma_start(
                            out=x_tiles[g], out_offset=bass.IndirectOffsetOnAxis(ap=slot[b][:, j:j + 1], axis=0),
                            in_=xe[b][:, j, :], in_offset=None).then_inc(scattered[g], 16)

            def gather(b):
                g = [b in group for group in GROUPS].index(True)
                pool.wait_ge(y_stored[g], 16 * len(CHUNKS[g]))
                pool.wait_ge(scattered[g], 16 * TB * len(GROUPS[g]))
                for j in range(TB):
                    pool.indirect_dma_start(
                        out=yg[b][:, j, :], out_offset=None, in_=y_tiles[g],
                        in_offset=bass.IndirectOffsetOnAxis(ap=slot[b][:, j:j + 1], axis=0))\
                        .then_inc(gathered[b], 16)

            have = dict(scatter=scatter, gather=gather, front_sub=front_sub, front_add=front_add,
                        front_dtu=front_dtu)
            front_sub(0)
            front_add(0)
            front_dtu(0)
            for n in range(LAST + 1):
                if n < B * NS:
                    read_out(n)
                steps(n, have)


_INS = ['L0_attn_x', 'L0_attn_ln_gamma', 'L0_attn_ln_beta', 'L0_attn_in_proj_w', 'L0_attn_conv_w', 'L0_attn_conv_b',
        'L0_attn_x_proj_w', 'L0_attn_dt_proj_w', 'L0_attn_dt_proj_b', 'L0_attn_A_log', 'L0_attn_D',
        'L0_attn_out_proj_w', 'L0_ffn_centroids', 'L0_ffn_ln_g', 'L0_ffn_ln_b', 'L0_ffn_w1', 'L0_ffn_b1', 'L0_ffn_w2',
        'L0_ffn_b2']
_OUTS = [((4, 512, 128), 'float32')]


def kernel(**inputs):
    import numpy as _np
    import concourse.bacc as _bacc
    from concourse import mybir as _mybir
    from concourse.bass_utils import run_bass_kernel_spmd as _run

    nc = _bacc.Bacc("TRN2", target_bir_lowering=False, num_devices=1)
    arrays, args = {}, []
    for name in _INS:
        a = _np.ascontiguousarray(inputs[name])
        arrays[f"in_{name}_dram"] = a
        args.append(nc.dram_tensor(f"in_{name}_dram", a.shape, _mybir.dt.from_np(a.dtype), kind="ExternalInput").ap())
    for i, (shape, dtype) in enumerate(_OUTS):
        dt = _mybir.dt.from_np(_np.dtype(dtype))
        args.append(nc.dram_tensor(f"out_{i}_dram", shape, dt, kind="ExternalOutput").ap())
    build(nc, *args)
    r = _run(nc, [arrays], core_ids=[0])
    got = tuple(r.results[0][f"out_{i}_dram"] for i in range(len(_OUTS)))
    return got[0]
```

```python
from contextlib import ExitStack

import concourse.bass as bass
from concourse import mybir

ALU = mybir.AluOpType
ACT = mybir.ActivationFunctionType
AX = mybir.AxisListType
F32 = mybir.dt.float32
BF16 = mybir.dt.bfloat16
EPS = 1e-5
P = 128


def build(nc, x, ln_gamma, ln_beta, in_proj_w, conv_w, conv_b, x_proj_w, dt_proj_w, dt_proj_b, A_log, D,
          out_proj_w, centroids, ln_g, ln_b, w1, b1, w2, b2, out):
    B, L, DM = x.shape
    DI, NS = A_log.shape
    R = dt_proj_w.shape[1]
    K = conv_w.shape[1]
    E, F, _ = w1.shape
    TB = L // P
    NC = DI // P
    NF = F // P
    BC = 2 * NS
    PADL = K - 1
    EXPERTS = 8
    SCATTERS = 5
    LOADED = 3
    LAG = 2
    AHEAD = 3
    GROUPS = tuple(range(B - 2)), (B - 2,), (B - 1,)
    NG = len(GROUPS)
    NT = [len(g) * TB + E - 1 for g in GROUPS]
    ROUNDS = [len(g) * TB for g in GROUPS]
    FIRST = [sum(NT[:g]) for g in range(NG + 1)]

    def group_of(m):
        return max(g for g in range(NG) if FIRST[g] <= m)

    assert DM == P and L == 512 and NS == 16

    rows, n_rows = {}, 0
    for name, count in (("gamma", 1), ("beta", 1), ("conv_b", NC), ("dt_b", NC), ("D", NC), ("ln_g", E),
                        ("ln_b", E), ("cent", E)):
        rows[name] = n_rows
        n_rows += count

    ctx = ExitStack()
    with ctx:
        def sb(name, shape, dt=F32):
            return ctx.enter_context(nc.sbuf_tensor(name, shape, dt))

        def ps(name, shape, dt=F32):
            return ctx.enter_context(nc.psum_tensor(name, shape, dt))

        def sem(name):
            return ctx.enter_context(nc.semaphore(name))

        vec_rows = sb("vec_rows", [n_rows, P])
        win_raw = sb("win_raw", [P, 2 * NC, DM])
        xp_raw = sb("xp_raw", [R + BC, DI])
        dtw_raw = sb("dtw_raw", [P, NC, R])
        wo_raw = sb("wo_raw", [P, DI])
        w1_raw = sb("w1_raw", [P, E * NF, DM])
        w2_raw = sb("w2_raw", [P, E, F])
        convw = sb("convw", [P, NC, K])
        alog = sb("alog", [P, NC, NS])
        b2_sb = sb("b2_sb", [E, DM])
        ident = sb("ident", [P, P])
        pick32 = sb("pick32", [3 * BC, BC])
        pick = sb("pick", [3 * BC, BC], BF16)
        vec = sb("vec", [P, n_rows])
        Aneg = sb("Aneg", [P, NC, NS])
        winT = sb("winT", [P, NC, K, P])
        wzT = sb("wzT", [P, DI])
        xpT = sb("xpT", [P, NC, 3 * BC + R])
        dtwT = sb("dtwT", [P, NC, P])
        woT = sb("woT", [P, NC, DM])
        w1T = w1_raw[:, :, :].rearrange("p (e j) d -> p e (j d)", e=E)
        w2T = w2_raw[:, :, :].rearrange("p e (j d) -> p e j d", j=NF)
        lnb_diag = sb("lnb_diag", [P, E, E])
        b1_split = sb("b1_split", [E, 3, F], BF16)
        b1_rows = sb("b1_rows", [3, E, F], BF16)
        ones16 = sb("ones16", [P, P], BF16)
        before32 = sb("before32", [P, P])
        before = sb("before", [P, P], BF16)
        rounds = sb("rounds", [P, E, ROUNDS[0]])
        tile_no = sb("tile_no", [1, NT[0], E])
        one_e = sb("one_e", [P, E])
        firstw = sb("firstw", [P, TB, E])

        xt = [sb(f"xt{i}", [P, TB, DM]) for i in range(2)]
        bst = sb("bst", [P, TB, 6])
        mv = sb("mv", [P, TB, 2])
        vv = sb("vv", [P, 2, TB])
        rs = sb("rs", [P, 2, TB])
        lny = [sb(f"lny{i}", [P, 2, TB]) for i in range(2)]
        yy = sb("yy", [P, 2, TB])
        sc1 = sb("sc1", [P, TB])
        sc2 = sb("sc2", [P, TB])
        xh = sb("xh", [P, TB, DM])
        xres = [sb(f"xres{i}", [P, TB, DM]) for i in range(2)]
        hT = sb("hT", [P, PADL + L])
        room = sb("room", [P, 7, NC, L])
        u, av, ww, lw, uD, dt0, dtu0 = (room[:, i] for i in range(7))
        zs = [sb(f"zs{i}", [P, TB, DI]) for i in range(2)]
        parts = [sb(f"parts{i}", [3 * BC, L], BF16) for i in range(2)]
        dtlow = sb("dtlow", [P, L])
        zz = av
        rest = ww[0:3 * BC, 0, :]
        dt = [dt0, sb("dt1", [P, NC, L])]
        dtu = [dtu0, sb("dtu1", [P, NC, L])]
        dA = [sb(f"dA{i}", [P, NC, L]) for i in range(AHEAD)]
        dBu = [sb(f"dBu{i}", [P, NC, L]) for i in range(2)]
        hs_room = sb("hs_room", [P, AHEAD, NC, L])
        hC_room = sb("hC_room", [P, AHEAD, NC, L])
        hs = [hs_room[:, i] for i in range(AHEAD)]
        hC = [hC_room[:, i] for i in range(AHEAD)]
        Cb = [sb(f"Cb{i}", [P, L]) for i in range(AHEAD)]
        yz = sb("yz", [P, TB, DI])
        win_tap = yz[:, :, :].rearrange("p j (a m) -> p (j a m)", m=P).rearrange("p (c k m) -> p c k m", c=NC, k=K)
        yzT = sb("yzT", [P, NC, L])
        x1 = sb("x1", [P, TB, DM])
        bst2 = sb("bst2", [P, TB, 6])
        mv2 = sb("mv2", [P, TB, 2])
        vv2 = sb("vv2", [P, 2, TB])
        rs2 = sb("rs2", [P, 2, TB])
        yy2 = sb("yy2", [P, 2, TB])
        nr = sb("nr", [P, 3, TB])
        xe = [sb(f"xe{b}", [P, TB, DM]) for b in range(B)]
        xeT = sb("xeT", [P, L])
        base = [sb(f"base{b}", [P, TB, DM]) for b in range(B)]
        aff = sb("aff", [P, TB, E])
        score = sb("score", [P, TB, E])
        mx = sb("mx", [P, TB])
        mx2 = sb("mx2", [P, TB])
        gex = sb("gex", [P, TB])
        gate = [sb(f"gate{b}", [P, TB]) for b in range(B)]
        hot = [sb(f"hot{b}", [P, TB, E]) for b in range(B)]
        hotT = sb("hotT", [E, L])
        hot16 = sb("hot16", [P, TB, E], BF16)
        more = sb("more", [P, E, ROUNDS[0]])
        tiles = sb("tiles", [P, E])
        ends = sb("ends", [P, E])
        ends128 = sb("ends128", [P, E])
        start = sb("start", [P, E])
        count = [sb(f"count{b}", [P, E]) for b in range(B)]
        place = sb("place", [P, TB, E])
        rank = [sb(f"rank{b}", [P, TB]) for b in range(B)]
        slotf = sb("slotf", [P, TB])
        slot = [sb(f"slot{b}", [P, TB], mybir.dt.uint32) for b in range(B)]
        past = sb("past", [1, NT[0], E])
        te_f = sb("te_f", [1, NT[0]])
        te = [sb(f"te{g}", [1, NT[g]], mybir.dt.int32) for g in range(NG)]
        def tile_rows(buffers, at, g):
            flat = buffers[:, :, :, :].rearrange("p i c t -> p (i c t)")
            return flat[:, at:at + NT[g] * DM].rearrange("p (i d) -> p i d", d=DM)

        xs = [tile_rows(room, 0, 0), tile_rows(room, 4 * NC * L, 1), tile_rows(hs_room, 0, 2)]
        ys = [tile_rows(room, 2 * NC * L, 0), tile_rows(room, 4 * NC * L + NT[1] * DM, 1), tile_rows(hC_room, 0, 2)]
        xsT = sb("xsT", [P, P])
        hn = sb("hn", [P, F])
        hh = sb("hh", [P, NF, P])
        b1_sb = hh[0:E, :, :].rearrange("p j s -> p (j s)")
        b1_rest = hn[0:E, :]
        yg = xe
        res = base

        psB = ps("psB", [P, L])
        psC = ps("psC", [P, L])
        psY = ps("psY", [P, TB, DI])
        psF = [ps(f"psF{i}", [P, 512]) for i in range(2)]
        psU = ps("psU", [P, 512])
        psD = ps("psD", [P, 512])

        x_tiles = [nc.dram_tensor(f"x_tiles{g}", [NT[g] * P, DM], F32).ap() for g in range(NG)]
        y_tiles = [nc.dram_tensor(f"y_tiles{g}", [NT[g] * P, DM], F32).ap() for g in range(NG)]
        b1_turn = nc.dram_tensor("b1_turn", [E, 3, F], BF16).ap()
        CHUNKS = [[(lo, min(lo + 4, NT[g])) for lo in range(0, NT[g], 4)] for g in range(NG)]

        S = {}
        for name in """vec_in win_in convw_in xp_in dtw_in wo_in alog_in b2_in w1_in w2_in
                ident_ok pick_ok pads_ok firstw_ok vecT_mm vec_ok tap_ok win_mm win_ok small_mm small_ok
                aexp_ok aneg_ok w1_mm w1_ok w2_mm w2_ok diag_ok b1_mm b1_split_ok b1_turn_in b1_rows_in w1g_ok b1_in
                ones_ok before_ok consts_ok zero_ok tiles_zero rank_ok
                hot16_ok rank_mm slot_ok te_ok xsT_mm xsT_ok up_mm relu_ok hh_mm hh_ok down_mm ys_ok gate_ok
                stat_ok xh_ok xres_ok hT_mm hT_ok conv_mm u_ok uD_ok z_mm zs_ok xp_mm rest_ok parts_ok
                dtlow_ok dt_mm av_ok rv_ok zz_ok ww_ok lw_ok nc_ok tv_ok dt_ok dtu_ok
                Bb_mm dBu_ok Cb_mm Cb_ok dA_ok h_ok hC_ok sum_mm
                yz_ok yzT_mm yzT_ok op_mm x1_ok nr_ok xe_ok base_ok xeT_mm xeT_ok aff_mm mx_ok gex_ok hot_ok
                hotT_mm hotT_ok b2_mm b2_ok res_ok
                vv_ok y_ok vv2_ok y2_ok lny_ok dve_chain""".split():
            S[name] = sem(name)

        x_in = [sem(f"x_in{b}") for b in range(B)]
        stored = [sem(f"stored{b}") for b in range(B)]
        scattered = [sem(f"scattered{g}") for g in range(NG)]
        y_stored = [sem(f"y_stored{g}") for g in range(NG)]
        gathered = [[sem(f"gathered{b}_{j}") for j in range(TB)] for b in range(B)]
        xs_in = [[sem(f"xs_in{g}_{i}") for i in range(len(CHUNKS[g]))] for g in range(NG)]

        def col(name, i=0):
            return vec[:, rows[name] + i:rows[name] + i + 1]

        FRONT = (("front_moments", 0), ("front_root", 0), ("front_norm", 1), ("front_turn", 2), ("front_conv0", 3),
                 ("front_conv1", 4), ("front_conv2", 5), ("front_conv3", 6), ("front_z", 7), ("front_silu", 7),
                 ("front_xproj", 8), ("front_low", 8), ("front_uD", 9), ("front_dt", 9), ("front_parts", 10),
                 ("front_abs", 10), ("front_exp", 11), ("front_rounding", 12), ("front_sub", 12), ("front_log", 12),
                 ("front_add", 12), ("front_dtu", 14), ("front_res", 15))
        TAIL = (("tail_turn", 0), ("tail_proj", 1), ("tail_moments", 2), ("tail_root", 3), ("tail_norm", 3),
                ("tail_xeT", 5), ("tail_base", 6), ("tail_aff", 6), ("tail_choose", 6), ("tail_gate", 7),
                ("tail_rank", 7), ("tail_hot", 7), ("tail_bias", 8))
        TAIL_SOON = (("tail_turn", 0), ("tail_proj", 1), ("tail_moments", 1), ("tail_root", 2), ("tail_norm", 2),
                     ("tail_base", 3), ("tail_xeT", 3), ("tail_aff", 4), ("tail_choose", 4), ("tail_gate", 4),
                     ("tail_rank", 5), ("tail_hot", 5), ("tail_bias", 6))
        LAST = 140
        agenda = [[] for _ in range(LAST + 1)]
        for b in range(1, B):
            for name, at in FRONT:
                agenda[NS * (b - 1) + at].append((name, b))
        routed = []
        for b in range(B):
            begin = NS * (b + 1) + (11 if b < B - 2 else 3 if b < B - 1 else 1)
            for name, at in TAIL if b < B - 3 else TAIL_SOON:
                agenda[begin + at].append((name, b))
                if name == "tail_rank":
                    for g in range(NG):
                        if b == GROUPS[g][-1]:
                            agenda[begin + at].append(("route", g))
                            blocks = [(b2, j) for b2 in GROUPS[g] for j in range(TB)]
                            for i, rows_ in enumerate(blocks):
                                agenda[begin + at + i // SCATTERS].append(("scatter", rows_))
                            routed.append(begin + at + (len(blocks) - 1) // SCATTERS)
                            agenda[routed[g]].append(("load_tiles", g))
        for e in range(E):
            agenda[EXPERTS + e].insert(0, ("turn_expert", e))
            agenda[EXPERTS + E + e // 3].append(("b1_shift", e))
            agenda[EXPERTS + E + 4 + e].append(("gamma_w1", e))
        agenda[EXPERTS + E + 3].append(("split_b1", 0))
        tile_at = {}
        at, last = 0, None
        for m in range(FIRST[NG]):
            g = group_of(m)
            if m == FIRST[g] and routed[g] + LOADED > at:
                if last is not None:
                    tile_at[at] = (None, last, at > NS * B)
                at, last = routed[g] + LOADED, None
            tile_at[at] = (m, last, at > NS * B)
            at, last = at + 1, m
        tile_at[at] = (None, last, True)
        for n, step in tile_at.items():
            agenda[n].append(("tile_products", step))
        for g in range(NG):
            done = 1 + min(n for n, step in tile_at.items() if step[1] == FIRST[g + 1] - 1)
            agenda[done].append(("store_tiles", g))
            for i, b in enumerate(GROUPS[g]):
                at = max(done + 2, routed[-1] + 2) + b
                agenda[at].append(("gather", b))
                agenda[at + 1].append(("finish", b))
                agenda[at + 1].append(("store", b))

        def first_late(d):
            return d == min(down for _, down, late in tile_at.values() if late and down is not None)

        def steps(n, have):
            for name, i in agenda[n]:
                if name in have:
                    have[name](i)

        block = ctx.enter_context(nc.Block())

        @block.sync
        def _(sp_):
            def load_x(b):
                if b >= 2:
                    sp_.wait_ge(S["xh_ok"], b - 1)
                    sp_.wait_ge(S["xres_ok"], b - 1)
                sp_.dma_start(xt[b % 2][:, :, :], x[b].rearrange("(j p) d -> p j d", p=P)).then_inc(x_in[b], 16)

            load_x(0)
            one = [("gamma", ln_gamma), ("beta", ln_beta), ("conv_b", conv_b), ("dt_b", dt_proj_b), ("D", D)]
            for name, v in one:
                n = v.shape[0] // P
                sp_.dma_start(vec_rows[rows[name]:rows[name] + n, :], v.rearrange("(a n) -> a n", n=P))\
                   .then_inc(S["vec_in"], 16)
            for name, v in (("ln_g", ln_g), ("ln_b", ln_b), ("cent", centroids)):
                sp_.dma_start(vec_rows[rows[name]:rows[name] + E, :], v).then_inc(S["vec_in"], 16)
            sp_.dma_start(b1_sb[:, :], b1).then_inc(S["b1_in"], 16)
            load_x(1)
            for e in range(E):
                sp_.dma_start(w1_raw[:, e * NF:(e + 1) * NF, :], w1[e].rearrange("(j p) d -> p j d", p=P))\
                   .then_inc(S["w1_in"], 16)
                sp_.dma_start(w2_raw[:, e, :], w2[e]).then_inc(S["w2_in"], 16)
            sp_.wait_ge(S["zero_ok"], 1)
            for g in range(NG):
                for lo, hi in CHUNKS[g]:
                    sp_.dma_start(x_tiles[g][lo * P:hi * P, :].rearrange("(i p) d -> p i d", p=P),
                                  xe[0][:, 0:hi - lo, :])\
                       .then_inc(S["tiles_zero"], 16)
            load_x(2)
            sp_.wait_ge(S["b1_split_ok"], 3)
            sp_.dma_start(b1_turn, b1_split[:, :, :]).then_inc(S["b1_turn_in"], 16)
            sp_.wait_ge(S["b1_turn_in"], 16)
            sp_.dma_start(b1_rows[:, :, :], b1_turn.rearrange("e i f -> i e f")).then_inc(S["b1_rows_in"], 16)
            load_x(3)

            def load_tiles(g):
                sp_.wait_ge(scattered[g], 16 * TB * len(GROUPS[g]))
                if g == 0:
                    sp_.wait_ge(S["uD_ok"], NC * B)
                    sp_.wait_ge(S["dtu_ok"], B)
                    sp_.wait_ge(S["tv_ok"], B)
                elif g == 1:
                    sp_.wait_ge(S["sum_mm"], (B - 1) * NS + 1)
                    sp_.wait_ge(S["dA_ok"], NC * (B - 1) * NS)
                    sp_.wait_ge(S["dBu_ok"], (B - 1) * NS)
                else:
                    sp_.wait_ge(S["hC_ok"], B * NS)
                for (lo, hi), xs_ok in zip(CHUNKS[g], xs_in[g]):
                    sp_.dma_start(xs[g][:, lo:hi, :], x_tiles[g][lo * P:hi * P, :].rearrange("(i p) d -> p i d", p=P))\
                       .then_inc(xs_ok, 16)

            def store_tiles(g):
                for lo, hi in CHUNKS[g]:
                    sp_.wait_ge(S["ys_ok"], FIRST[g] + hi)
                    sp_.dma_start(y_tiles[g][lo * P:hi * P, :].rearrange("(i p) d -> p i d", p=P), ys[g][:, lo:hi, :])\
                       .then_inc(y_stored[g], 16)

            def store(b):
                for lo, hi in ((0, TB // 2), (TB // 2, TB)):
                    sp_.wait_ge(S["res_ok"], TB * b + hi)
                    sp_.dma_start(out[b].rearrange("(j p) d -> p j d", p=P)[:, lo:hi, :], res[b][:, lo:hi, :])\
                       .then_inc(stored[b], 16)

            have = dict(load_tiles=load_tiles, store_tiles=store_tiles, store=store)
            for n in range(LAST + 1):
                steps(n, have)
            for b in range(B):
                sp_.wait_ge(stored[b], 2 * 16)

        @block.tensor
        def _(pe):
            def turn_weights_0():
                pe.wait_ge(S["ident_ok"], 2)
                for c in range(NC):
                    pe.wait_ge(S["tap_ok"], K * (c + 1))
                    bank = (psU, psD)[c]
                    for k in range(K):
                        t = pe.transpose(bank[:, k * P:(k + 1) * P], win_tap[:, c, k, :], ident[:, :])
                    t.then_inc(S["win_mm"], 1)
                for c in range(NC):
                    t = pe.transpose(psF[1][:, c * P:(c + 1) * P], win_raw[:, NC + c, :], ident[:, :])
                t.then_inc(S["win_mm"], 1)
                pe.wait_ge(S["vec_in"], 16 * 8)
                pe.transpose(psF[0][:, 0:n_rows], vec_rows[:, :], ident[0:n_rows, 0:n_rows])\
                  .then_inc(S["vecT_mm"], 1)
                pe.wait_ge(S["xp_in"], 16)
                pe.wait_ge(S["dtw_in"], 16)
                pe.wait_ge(S["wo_in"], 16)
                pe.wait_ge(S["vec_ok"], 1)
                pe.wait_ge(S["win_ok"], 3)
                for c in range(NC):
                    pe.transpose(psF[0][:, c * 64:c * 64 + R + BC], xp_raw[:, c * P:(c + 1) * P],
                                 ident[0:R + BC, 0:R + BC])
                    pe.transpose(psF[1][0:R, c * P:(c + 1) * P], dtw_raw[:, c, :], ident[:, :])
                for c in range(NC):
                    t = pe.transpose(psF[0][:, 128 + c * P:128 + (c + 1) * P], wo_raw[:, c * P:(c + 1) * P],
                                     ident[:, :])
                t.then_inc(S["small_mm"], 1)

            def turn_expert(e):
                pe.wait_ge(S["w1_in"], 16 * E)
                pe.wait_ge(S["w2_in"], 16 * E)
                if e == 0:
                    pe.wait_ge(S["u_ok"], 2 * 2)
                else:
                    pe.wait_ge(S["w1_ok"], e)
                for j in range(NF):
                    t = pe.transpose(psU[:, j * P:(j + 1) * P], w1_raw[:, e * NF + j, :], ident[:, :])
                t.then_inc(S["w1_mm"], 1)
                if e:
                    pe.wait_ge(S["w2_ok"], e)
                for j in range(NF):
                    t = pe.transpose(psD[:, j * P:(j + 1) * P], w2_raw[:, e, j * P:(j + 1) * P], ident[:, :])
                t.then_inc(S["w2_mm"], 1)

            def b1_shift(e):
                if e == 0:
                    pe.wait_ge(S["w1_ok"], E)
                    pe.wait_ge(S["rv_ok"], 2 * 2)
                    pe.wait_ge(S["diag_ok"], 1)
                    pe.wait_ge(S["b1_in"], 16)
                pe.matmul(psF[1][0:E, :], lnb_diag[:, e, :], w1T[:, e, :], start=(e == 0), stop=False)
                if e == E - 1:
                    pe.matmul(psF[1][0:E, :], ident[0:E, 0:E], b1_sb[:, :], start=False, stop=True)\
                      .then_inc(S["b1_mm"], 1)

            def front_turn(b):
                if b == 0:
                    pe.wait_ge(S["win_ok"], 1)
                elif b != 2:
                    pe.wait_ge(S["u_ok"], 2 * b)
                else:
                    pe.wait_ge(S["w1_ok"], E)
                pe.wait_ge(S["xh_ok"], b + 1)
                for j in range(TB):
                    t = pe.transpose(psU[:, j * P:(j + 1) * P], xh[:, j, :], ident[:, :])
                t.then_inc(S["hT_mm"], 1)

            def front_conv(b, c, half):
                if half == 0:
                    pe.wait_ge(S["hT_ok"], b + 1)
                if c == half == 0:
                    if b == 0:
                        pe.wait_ge(S["win_ok"], 2)
                        pe.wait_ge(S["pads_ok"], 1)
                    elif b != 2:
                        pe.wait_ge(S["u_ok"], 2 * b)
                    else:
                        pe.wait_ge(S["w2_ok"], E)
                for k in range(half * K // 2, (half + 1) * K // 2):
                    t = pe.matmul((psD, psU)[c][:, :], winT[:, c, k, :], hT[:, k:k + L],
                                  start=(k == 0), stop=(k == K - 1))
                if half:
                    t.then_inc(S["conv_mm"], 1)

            def front_z(b):
                for i in range(2):
                    if b == 0:
                        pe.wait_ge(S["small_ok"], 4)
                    else:
                        pe.wait_ge(S["rv_ok"], 2 * b)
                    if b == 2 and i:
                        pe.wait_ge(S["b1_split_ok"], 3)
                    if b >= 3:
                        pe.wait_ge(S["b2_ok"], b - 2)
                    for j in range(2):
                        t = pe.matmul(psF[i][:, j * DI:(j + 1) * DI],
                                      hT[:, PADL + (2 * i + j) * P:PADL + (2 * i + j + 1) * P], wzT[:, :],
                                      start=True, stop=True)
                    t.then_inc(S["z_mm"], 1)

            def front_xproj(b):
                pe.wait_ge(S["u_ok"], 2 * b + 2)
                pe.wait_ge(S["zs_ok"], 2 * b + 1)
                for c in range(NC):
                    t = pe.matmul(psF[0][0:3 * BC + R, :], xpT[:, c, :], u[:, c, :], start=(c == 0), stop=(c == NC - 1))
                t.then_inc(S["xp_mm"], 1)

            def front_dt(b):
                pe.wait_ge(S["dtlow_ok"], b + 1)
                pe.wait_ge(S["zs_ok"], 2 * b + 2)
                for c in (1, 0):
                    if c == 0:
                        pe.wait_ge(S["rest_ok"], b + 1)
                    pe.matmul(psF[c][:, :], dtwT[3 * BC:3 * BC + R, c, :], dtlow[3 * BC:3 * BC + R, :],
                              start=True, stop=True).then_inc(S["dt_mm"], 1)

            def spread_B(n):
                b, s = divmod(n, NS)
                pe.wait_ge(S["parts_ok"], b + 1)
                if n:
                    pe.wait_ge(S["dBu_ok"], n)
                pe.matmul(psB[:, :], pick[:, s:s + 1].broadcast_to([3 * BC, P]), parts[b % 2][:, :],
                          start=True, stop=True).then_inc(S["Bb_mm"], 1)

            def spread_C(n):
                b, s = divmod(n, NS)
                if n:
                    pe.wait_ge(S["Cb_ok"], n)
                pe.matmul(psC[:, :], pick[:, NS + s:NS + s + 1].broadcast_to([3 * BC, P]), parts[b % 2][:, :],
                          start=True, stop=True).then_inc(S["Cb_mm"], 1)

            def add_up(src, first):
                for j in range(TB):
                    for c in range(NC):
                        t = pe.matmul(psY[:, j, c * P:(c + 1) * P], src[:, c, j * P:(j + 1) * P], ident[:, :],
                                      start=first and j % 2 == 0 and c == 0, stop=True, is_transpose=True,
                                      skip_group_check=True)
                return t

            def sum_state(n):
                b, s = divmod(n, NS)
                if s == 0:
                    if b:
                        pe.wait_ge(S["yz_ok"], b)
                    pe.wait_ge(S["uD_ok"], 2 * b + 2)
                    add_up(uD, True)
                pe.wait_ge(S["hC_ok"], n + 1)
                add_up(hC[n % AHEAD], False).then_inc(S["sum_mm"], 1)

            def tail_turn(b):
                pe.wait_ge(S["yz_ok"], b + 1)
                pe.wait_ge(S["rv_ok"], 2 * min(b + 3, B))
                if b:
                    pe.wait_ge(S["b2_ok"], b)
                for c in range(NC):
                    for j in range(TB):
                        t = pe.transpose(psF[c][:, j * P:(j + 1) * P], yz[:, j, c * P:(c + 1) * P], ident[:, :])
                    t.then_inc(S["yzT_mm"], 1)

            def tail_proj(b):
                pe.wait_ge(S["yzT_ok"], 2 * b + 2)
                for j in range(TB):
                    for c in range(NC):
                        t = pe.matmul(psF[0][:, j * DM:(j + 1) * DM], yzT[:, c, j * P:(j + 1) * P], woT[:, c, :],
                                      start=(c == 0), stop=(c == NC - 1))
                t.then_inc(S["op_mm"], 1)

            def tail_xeT(b):
                pe.wait_ge(S["xe_ok"], b + 1)
                for j in range(TB):
                    t = pe.transpose(psF[1][:, j * P:(j + 1) * P], xe[b][:, j, :], ident[:, :])
                t.then_inc(S["xeT_mm"], 1)

            def tail_aff(b):
                pe.wait_ge(S["xeT_ok"], b + 1)
                pe.wait_ge(S["x1_ok"], b + 1)
                for j in range(TB):
                    t = pe.matmul(psF[0][:, j * E:(j + 1) * E], xeT[:, j * P:(j + 1) * P],
                                  vec[:, rows["cent"]:rows["cent"] + E], start=True, stop=True)
                t.then_inc(S["aff_mm"], 1)

            def tail_rank(b):
                pe.wait_ge(S["hot16_ok"], b + 1)
                pe.wait_ge(S["ones_ok"], 1)
                pe.wait_ge(S["before_ok"], 3)
                for j in range(TB + 1):
                    for i in range(min(j, TB)):
                        t = pe.matmul(psF[0][:, j * E:(j + 1) * E], ones16[:, :], hot16[:, i, :],
                                      start=(i == 0), stop=(j == TB and i == TB - 1))
                    if j < TB:
                        pe.matmul(psF[0][:, j * E:(j + 1) * E], before[:, :], hot16[:, j, :],
                                  start=(j == 0), stop=True)
                t.then_inc(S["rank_mm"], 1)

            def tail_hot(b):
                pe.wait_ge(S["hot_ok"], b + 1)
                for j in range(TB):
                    t = pe.transpose(psF[1][0:E, j * P:(j + 1) * P], hot[b][:, j, :], ident[:, :])
                t.then_inc(S["hotT_mm"], 1)

            def tail_bias(b):
                pe.wait_ge(S["hotT_ok"], b + 1)
                pe.wait_ge(S["b2_in"], 16)
                pe.wait_ge(S["rank_ok"], b + 1)
                for j in range(TB):
                    t = pe.matmul(psF[0][:, j * DM:(j + 1) * DM], hotT[:, j * P:(j + 1) * P], b2_sb[:, :],
                                  start=True, stop=True)
                t.then_inc(S["b2_mm"], 1)

            expert = {}

            def take(m, late):
                g = group_of(m)
                i = m - FIRST[g]
                if i == 0:
                    pe.wait_ge(S["te_ok"], g + 1)
                if m == 0:
                    pe.wait_ge(S["u_ok"], 2 * B)
                    pe.wait_ge(S["b1_rows_in"], 16)
                    pe.wait_ge(S["w1g_ok"], E)
                    pe.wait_ge(S["ones_ok"], 1)
                expert[m] = pe.value_load(te[g][0:1, i:i + 1], min_val=0, max_val=E - 1)
                for (lo, hi), xs_ok in zip(CHUNKS[g], xs_in[g]):
                    if i == lo:
                        pe.wait_ge(xs_ok, 16)
                if late:
                    pe.wait_ge(S["Cb_ok"], B * NS)
                    pe.wait_ge(S["xsT_ok"], m)
                elif m:
                    pe.wait_ge(S["relu_ok"], m)
                bank = psC if late else psU
                pe.transpose(bank[:, 0:P], xs[g][:, i, :], ident[:, :]).then_inc(S["xsT_mm"], 1)

            def tile_turn(step):
                m, d, late = step
                if m is not None:
                    take(m, late)
                if d is not None:
                    pe.wait_ge(S["relu_ok"], d + 1)
                    if late:
                        pe.wait_ge(S["hh_ok"], d)
                    if d and (not late or first_late(d)):
                        pe.wait_ge(S["ys_ok"], d)
                    for j in range(NF):
                        t = pe.transpose(psD[:, j * P:(j + 1) * P], hn[:, j * P:(j + 1) * P], ident[:, :])
                    t.then_inc(S["hh_mm"], 1)

            def tile_products(step):
                m, d, late = step
                if m is not None:
                    pe.wait_ge(S["xsT_ok"], m + 1)
                    if late:
                        pe.wait_ge(S["relu_ok"], m)
                    pe.matmul(psU[:, :], ones16[0:3, :], b1_rows[:, bass.ds(expert[m], 1), :],
                              start=True, stop=False)
                    pe.matmul(psU[:, :], xsT[:, :], w1T[:, bass.ds(expert[m], 1), :], start=False, stop=True)\
                      .then_inc(S["up_mm"], 1)
                if d is not None:
                    pe.wait_ge(S["hh_ok"], d + 1)
                    if late:
                        pe.wait_ge(S["dBu_ok"], B * NS)
                        pe.wait_ge(S["ys_ok"], d)
                    bank = psB if late else psD
                    for j in range(NF):
                        t = pe.matmul(bank[:, 0:DM], hh[:, j, :], w2T[:, bass.ds(expert[d], 1), j, :],
                                      start=(j == 0), stop=(j == NF - 1))
                    t.then_inc(S["down_mm"], 1)

            have = dict(tail_turn=tail_turn, tail_proj=tail_proj, tail_xeT=tail_xeT, tail_aff=tail_aff,
                        tail_rank=tail_rank, tail_hot=tail_hot, tail_bias=tail_bias, tile_products=tile_products,
                        turn_expert=turn_expert,
                        b1_shift=b1_shift, front_turn=front_turn,
                        front_conv0=lambda b: front_conv(b, 0, 0), front_conv1=lambda b: front_conv(b, 0, 1),
                        front_conv2=lambda b: front_conv(b, 1, 0), front_conv3=lambda b: front_conv(b, 1, 1),
                        front_z=front_z, front_xproj=front_xproj, front_dt=front_dt)
            turn_weights_0()
            front_turn(0)
            for c in range(NC):
                front_conv(0, c, 0)
                front_conv(0, c, 1)
            front_z(0)
            front_xproj(0)
            front_dt(0)
            spread_B(0)
            spread_C(0)
            for n in range(LAST + 1):
                if n + 1 < B * NS:
                    spread_B(n + 1)
                if n in tile_at:
                    tile_turn(tile_at[n])
                if n + 1 < B * NS:
                    spread_C(n + 1)
                if n == B * NS:
                    for i in range(n - LAG, n):
                        sum_state(i)
                steps(n, have)
                if LAG <= n < B * NS:
                    sum_state(n - LAG)

        @block.scalar
        def _(act):
            for dst, src, name in (
                    (win_raw[:, :, :], in_proj_w.rearrange("(j p) d -> p j d", p=P), "win_in"),
                    (convw[:, :, :], conv_w.rearrange("(c p) k -> p c k", p=P), "convw_in")):
                act.dma_start(dst, src).then_inc(S[name], 16)

            def weights_0():
                act.preload_act_table_set("natural_log_exp_and_others")
                for c in range(NC):
                    act.wait_ge(S["win_mm"], c + 1)
                    act.activation(winT[:, c, :, :].rearrange("p k e -> p (k e)"), (psU, psD)[c][:, :], ACT.Copy)\
                       .then_inc(S["win_ok"], 1)
                act.wait_ge(S["win_mm"], 3)
                act.activation(wzT[:, :], psF[1][:, 0:DI], ACT.Copy).then_inc(S["win_ok"], 1)

            def vectors():
                act.wait_ge(S["vecT_mm"], 1)
                act.activation(vec[:, :], psF[0][:, 0:n_rows], ACT.Copy).then_inc(S["vec_ok"], 1)
                act.wait_ge(S["alog_in"], 16)
                act.activation(Aneg[:, :, :], alog[:, :, :], ACT.Exp).then_inc(S["aexp_ok"], 1)

            def expert_weights(e):
                act.wait_ge(S["w1_mm"], e + 1)
                act.activation(w1T[:, e, :], psU[:, :], ACT.Copy).then_inc(S["w1_ok"], 1)
                act.wait_ge(S["w2_mm"], e + 1)
                act.activation(w2T[:, e, :, :].rearrange("p j d -> p (j d)"), psD[:, :], ACT.Copy)\
                   .then_inc(S["w2_ok"], 1)

            roots = [0]

            def root(v2, ln, y, v_ok, y_ok, b):
                act.wait_ge(v_ok, b + 1)
                roots[0] += 1
                act.activation(ln[:, :, :], v2[:, :, :], ACT.Ln).then_inc(S["lny_ok"], 1)
                act.wait_ge(S["lny_ok"], roots[0])
                act.activation(y[:, :, :], ln[:, :, :], ACT.Exp, scale=-0.5).then_inc(y_ok, 1)

            def front_root(b):
                root(vv, lny[0], yy, S["vv_ok"], S["y_ok"], b)

            def tail_root(b):
                root(vv2, lny[1], yy2, S["vv2_ok"], S["y2_ok"], b)

            def front_res(b):
                act.wait_ge(S["stat_ok"], b + 1)
                if b >= 2:
                    act.wait_ge(S["x1_ok"], b - 1)
                for j in range(TB):
                    t = act.activation(xres[b % 2][:, j, :], xt[b % 2][:, j, :], ACT.Identity,
                                       bias=sc2[:, j:j + 1], scale=sc1[:, j:j + 1])
                t.then_inc(S["xres_ok"], 1)

            def front_hT(b):
                act.wait_ge(S["hT_mm"], b + 1)
                if b == 0:
                    act.wait_ge(S["vec_ok"], 1)
                else:
                    act.wait_ge(S["z_mm"], 2 * b)
                act.activation(hT[:, PADL:], psU[:, :], ACT.Identity, bias=col("beta"), scale=col("gamma"))\
                   .then_inc(S["hT_ok"], 1)

            def front_silu(b):
                act.preload_act_table_set("silu_and_others")
                if b:
                    act.wait_ge(S["dtu_ok"], b)
                for c in range(NC):
                    act.wait_ge(S["conv_mm"], 2 * b + c + 1)
                    act.activation(u[:, c, :], (psD, psU)[c][:, :], ACT.Silu, bias=col("conv_b", c))\
                       .then_inc(S["u_ok"], 1)
                if b >= 2:
                    act.wait_ge(S["yz_ok"], b - 1)
                for i in range(2):
                    act.wait_ge(S["z_mm"], 2 * b + i + 1)
                    act.activation(zs[b % 2][:, 2 * i:2 * i + 2, :].rearrange("p j d -> p (j d)"), psF[i][:, :],
                                   ACT.Silu).then_inc(S["zs_ok"], 1)
                act.preload_act_table_set("natural_log_exp_and_others")

            def front_uD(b):
                if b:
                    act.wait_ge(S["sum_mm"], (b - 1) * NS + 1)
                act.wait_ge(S["u_ok"], 2 * b + 2)
                for c in range(NC):
                    act.activation(uD[:, c, :], u[:, c, :], ACT.Copy, scale=col("D", c))\
                       .then_inc(S["uD_ok"], 1)

            def front_abs(b):
                if b:
                    act.wait_ge(S["tv_ok"], b)
                if b >= 2:
                    act.wait_ge(S["dA_ok"], 2 * (b - 1) * NS)
                for c in (1, 0):
                    act.wait_ge(S["dt_mm"], 2 * b + 2 - c)
                    act.activation(av[:, c, :], psF[c][:, :], ACT.Abs, bias=col("dt_b", c)).then_inc(S["av_ok"], 1)
                    act.activation(dt[b % 2][:, c, :], psF[c][:, :], ACT.Relu, bias=col("dt_b", c))\
                       .then_inc(S["rv_ok"], 1)

            def front_exp(b):
                if b:
                    act.wait_ge(S["lw_ok"], b)
                act.wait_ge(S["av_ok"], 2 * b + 2)
                act.activation(zz[:, :, :], av[:, :, :], ACT.Exp, scale=-1.0).then_inc(S["zz_ok"], 1)
                act.wait_ge(S["zz_ok"], b + 1)
                act.wait_ge(S["parts_ok"], b + 1)
                act.activation(ww[:, :, :], zz[:, :, :], ACT.Copy, bias=1.0).then_inc(S["ww_ok"], 1)

            def front_log(b):
                if b:
                    act.wait_ge(S["dt_ok"], b)
                act.wait_ge(S["ww_ok"], b + 1)
                act.preload_act_table_set("natural_log")
                act.activation(lw[:, :, :], ww[:, :, :], ACT.Ln).then_inc(S["lw_ok"], 1)
                act.preload_act_table_set("natural_log_exp_and_others")

            def decay(n):
                b, s = divmod(n, NS)
                if s == 0:
                    act.wait_ge(S["dt_ok"], b + 1)
                if n == 0:
                    act.wait_ge(S["aneg_ok"], 1)
                if n >= AHEAD:
                    act.wait_ge(S["h_ok"], 2 * (n - AHEAD + 1))
                for c in range(NC):
                    act.activation(dA[n % AHEAD][:, c, :], dt[b % 2][:, c, :], ACT.Exp, scale=Aneg[:, c, s:s + 1])\
                       .then_inc(S["dA_ok"], 1)

            def copy_C(n):
                act.wait_ge(S["Cb_mm"], n + 1)
                if n >= AHEAD:
                    act.wait_ge(S["hC_ok"], n - AHEAD + 1)
                act.activation(Cb[n % AHEAD][:, :], psC[:, :], ACT.Copy).then_inc(S["Cb_ok"], 1)

            def tail_yzT(b):
                if b:
                    act.wait_ge(S["op_mm"], b)
                for c in range(NC):
                    act.wait_ge(S["yzT_mm"], 2 * b + c + 1)
                    act.activation(yzT[:, c, :], psF[c][:, :], ACT.Copy).then_inc(S["yzT_ok"], 1)

            def tail_xeT(b):
                act.wait_ge(S["xeT_mm"], b + 1)
                if b:
                    act.wait_ge(S["aff_mm"], b)
                act.activation(xeT[:, :], psF[1][:, :], ACT.Copy).then_inc(S["xeT_ok"], 1)

            def tail_base(b):
                act.wait_ge(S["nr_ok"], b + 1)
                act.wait_ge(S["x1_ok"], b + 1)
                for j in range(TB):
                    t = act.activation(base[b][:, j, :], x1[:, j, :], ACT.Identity, bias=nr[:, 1, j:j + 1],
                                       scale=nr[:, 0, j:j + 1])
                t.then_inc(S["base_ok"], 1)

            def tail_gate(b):
                act.wait_ge(S["mx_ok"], b + 1)
                act.activation(gex[:, :], mx[:, :], ACT.Exp, scale=-1.0).then_inc(S["gex_ok"], 1)

            def tail_hotT(b):
                act.wait_ge(S["hotT_mm"], b + 1)
                if b:
                    act.wait_ge(S["b2_mm"], b)
                act.activation(hotT[:, :], psF[1][0:E, :], ACT.Copy).then_inc(S["hotT_ok"], 1)

            waiting = []

            def copy_down(d, late):
                g = group_of(d)
                act.wait_ge(S["down_mm"], d + 1)
                if g == 0:
                    act.wait_ge(S["dt_ok"], B)
                elif g == 1 and NG > 2:
                    act.wait_ge(S["dBu_ok"], (B - 1) * NS)
                else:
                    act.wait_ge(S["sum_mm"], B * NS)
                act.activation(ys[g][:, d - FIRST[g], :], (psB if late else psD)[:, 0:DM], ACT.Copy)\
                   .then_inc(S["ys_ok"], 1)

            def tile_turn(step):
                m, d, late = step
                if m is not None:
                    act.wait_ge(S["xsT_mm"], m + 1)
                    if m:
                        act.wait_ge(S["up_mm"], m)
                    act.activation(xsT[:, :], (psC if late else psU)[:, 0:P], ACT.Copy).then_inc(S["xsT_ok"], 1)
                if waiting:
                    copy_down(waiting.pop(), True)
                if d is not None:
                    act.wait_ge(S["hh_mm"], d + 1)
                    act.wait_ge(S["down_mm"], d)
                    act.activation(hh[:, :, :].rearrange("p j s -> p (j s)"), psD[:, :], ACT.Copy)\
                       .then_inc(S["hh_ok"], 1)

            def tile_products(step):
                m, d, late = step
                if m is not None:
                    act.wait_ge(S["up_mm"], m + 1)
                    if m:
                        act.wait_ge(S["hh_mm"], m)
                    act.activation(hn[:, :], psU[:, :], ACT.Relu).then_inc(S["relu_ok"], 1)
                if d is not None and m is not None and late:
                    waiting.append(d)
                elif d is not None:
                    copy_down(d, late)

            have = dict(tail_turn=tail_yzT, tail_root=tail_root, tail_xeT=tail_xeT, tail_base=tail_base,
                        tail_gate=tail_gate, tail_hot=tail_hotT, tile_products=tile_products,
                        turn_expert=expert_weights,
                        front_root=front_root, front_res=front_res, front_turn=front_hT,
                        front_silu=front_silu, front_abs=front_abs, front_exp=front_exp,
                        front_log=front_log, front_uD=front_uD)
            weights_0()
            front_root(0)
            vectors()
            front_hT(0)
            front_silu(0)
            front_abs(0)
            front_exp(0)
            front_log(0)
            decay(0)
            copy_C(0)
            decay(1)
            front_uD(0)
            front_res(0)
            for n in range(LAST + 1):
                if n + 2 < B * NS:
                    decay(n + 2)
                if n in tile_at:
                    tile_turn(tile_at[n])
                if n + 1 < B * NS:
                    copy_C(n + 1)
                steps(n, have)

        @block.vector
        def _(dve):
            chain = [0]

            def link(t):
                chain[0] += 1
                t.then_inc(S["dve_chain"], 1)
                dve.wait_ge(S["dve_chain"], chain[0])

            def weights_0():
                dve.memset(hT[:, 0:PADL], 0.0).then_inc(S["pads_ok"], 1)
                for e in range(E):
                    t = dve.memset(firstw[:, :, e:e + 1], float(E - e))
                t.then_inc(S["firstw_ok"], 1)
                dve.memset(xe[0][:, :, :], 0.0).then_inc(S["zero_ok"], 1)
                dve.memset(one_e[:, :], 1.0)
                for i in range(ROUNDS[0]):
                    dve.memset(rounds[:, :, i:i + 1], float(P * i))
                for i in range(NT[0]):
                    t = dve.memset(tile_no[:, i, :], float(i))
                t.then_inc(S["consts_ok"], 1)
                dve.memset(ones16[:, :], 1.0).then_inc(S["ones_ok"], 1)
                link(dve.memset(lnb_diag[:, :, :], 0.0))
                dve.wait_ge(S["win_in"], 16)
                dve.wait_ge(S["convw_in"], 16)
                for c in range(NC):
                    for k in range(K):
                        dve.tensor_scalar(win_tap[:, c, k, :], win_raw[:, c, :], convw[:, c, k:k + 1], None, ALU.mult)\
                           .then_inc(S["tap_ok"], 1)
            def weights_1():
                dve.wait_ge(S["vec_ok"], 1)
                dve.tensor_copy(lnb_diag[:, :, :].rearrange("p a b -> p (a b)")[:, 0:E * E:E + 1],
                                vec[:, rows["ln_b"]:rows["ln_b"] + E]).then_inc(S["diag_ok"], 1)
                dve.wait_ge(S["aexp_ok"], 1)
                dve.tensor_scalar(Aneg[:, :, :], Aneg[:, :, :], -1.0, None, ALU.mult).then_inc(S["aneg_ok"], 1)
                dve.wait_ge(S["pick_ok"], 1 + 3)
                dve.tensor_copy(pick[:, :], pick32[:, :])\
                   .then_inc(S["pick_ok"], 1)
                dve.wait_ge(S["before_ok"], 2)
                dve.tensor_copy(before[:, :], before32[:, :]).then_inc(S["before_ok"], 1)
                dve.wait_ge(S["small_mm"], 1)
                xp = psF[0][:, 0:NC * 64].rearrange("p (c r) -> p c r", c=NC)
                for i in range(3):
                    t = dve.tensor_copy(xpT[:, :, i * BC:(i + 1) * BC], xp[:, :, R:R + BC])
                t.then_inc(S["small_ok"], 1)
                dve.tensor_copy(xpT[:, :, 3 * BC:3 * BC + R], xp[:, :, 0:R]).then_inc(S["small_ok"], 1)
                dve.tensor_copy(dtwT[3 * BC:3 * BC + R, :, :].rearrange("p c d -> p (c d)"), psF[1][0:R, 0:NC * P])\
                   .then_inc(S["small_ok"], 1)
                dve.tensor_copy(woT[:, :, :].rearrange("p c d -> p (c d)"), psF[0][:, 128:128 + NC * P])\
                   .then_inc(S["small_ok"], 1)

            def split_b1(_):
                dve.wait_ge(S["b1_mm"], 1)
                dve.tensor_copy(b1_split[:, 0, :], psF[1][0:E, :]).then_inc(S["b1_split_ok"], 1)
                dve.wait_ge(S["b1_split_ok"], 1)
                link(dve.tensor_tensor(b1_rest[:, :], psF[1][0:E, :], b1_split[:, 0, :], ALU.subtract))
                dve.tensor_copy(b1_split[:, 1, :], b1_rest[:, :]).then_inc(S["b1_split_ok"], 1)
                dve.wait_ge(S["b1_split_ok"], 2)
                link(dve.tensor_tensor(b1_rest[:, :], b1_rest[:, :], b1_split[:, 1, :], ALU.subtract))
                dve.tensor_copy(b1_split[:, 2, :], b1_rest[:, :]).then_inc(S["b1_split_ok"], 1)

            def gamma_w1(e):
                dve.tensor_scalar(w1T[:, e, :], w1T[:, e, :], col("ln_g", e), None, ALU.mult)\
                   .then_inc(S["w1g_ok"], 1)

            def moments(src, st, m, v2, ok):
                for j in range(TB):
                    t = dve.bn_stats(st[:, j, :], src[:, j, :])
                link(t)
                for j in range(TB):
                    t = dve.bn_aggr(m[:, j, :], st[:, j, :])
                link(t)
                link(dve.tensor_scalar(v2[:, 0, :], m[:, :, 1], EPS, None, ALU.add))
                dve.scalar_tensor_tensor(out=v2[:, 1, :], in0=v2[:, 0, :], scalar=EPS, in1=m[:, :, 1],
                                         op0=ALU.mult, op1=ALU.add).then_inc(ok, 1)

            def newton(v2, y, r2):
                link(dve.tensor_tensor(r2[:, :, :], y[:, :, :], y[:, :, :], ALU.mult))
                link(dve.tensor_tensor(r2[:, :, :], r2[:, :, :], v2[:, :, :], ALU.mult))
                link(dve.tensor_scalar(r2[:, :, :], r2[:, :, :], -0.5, 1.5, ALU.mult, ALU.add))
                link(dve.tensor_tensor(r2[:, :, :], r2[:, :, :], y[:, :, :], ALU.mult))

            def front_moments(b):
                dve.wait_ge(x_in[b], 16)
                moments(xt[b % 2], bst, mv, vv, S["vv_ok"])

            def front_norm(b):
                dve.wait_ge(S["y_ok"], b + 1)
                newton(vv, yy, rs)
                if b:
                    dve.wait_ge(S["xres_ok"], b)
                    dve.wait_ge(S["hT_mm"], b)
                dve.scalar_tensor_tensor(out=sc2[:, :], in0=mv[:, :, 0], scalar=-1.0, in1=rs[:, 0, :],
                                         op0=ALU.mult, op1=ALU.mult)
                dve.tensor_scalar(sc1[:, :], rs[:, 0, :], 1.0, None, ALU.add).then_inc(S["stat_ok"], 1)
                for j in range(TB):
                    t = dve.tensor_scalar(xh[:, j, :], xt[b % 2][:, j, :], mv[:, j, 0:1], rs[:, 1, j:j + 1],
                                          ALU.subtract, ALU.mult)
                t.then_inc(S["xh_ok"], 1)

            def front_low(b):
                dve.wait_ge(S["xp_mm"], b + 1)
                if b:
                    dve.wait_ge(S["lw_ok"], b)
                    dve.wait_ge(S["dt_mm"], 2 * b)
                dve.tensor_copy(dtlow[3 * BC:3 * BC + R, :], psF[0][3 * BC:3 * BC + R, :]).then_inc(S["dtlow_ok"], 1)
                if b >= 2:
                    dve.wait_ge(S["Bb_mm"], (b - 1) * NS)
                    dve.wait_ge(S["Cb_mm"], (b - 1) * NS)
                link(dve.tensor_copy(parts[b % 2][:, :], psF[0][0:3 * BC, :]))
                dve.tensor_tensor(rest[:, :], psF[0][0:3 * BC, :], parts[b % 2][:, :], ALU.subtract)\
                   .then_inc(S["rest_ok"], 1)

            def front_parts(b):
                pt = parts[b % 2]
                dve.wait_ge(S["rest_ok"], b + 1)
                dve.tensor_copy(pt[BC:2 * BC, :], rest[BC:2 * BC, :])
                link(dve.tensor_copy(pt[2 * BC:3 * BC, :], rest[2 * BC:3 * BC, :]))
                link(dve.tensor_tensor(rest[2 * BC:3 * BC, :], rest[2 * BC:3 * BC, :], pt[2 * BC:3 * BC, :],
                                       ALU.subtract))
                dve.tensor_copy(pt[2 * BC:3 * BC, :], rest[2 * BC:3 * BC, :]).then_inc(S["parts_ok"], 1)

            def front_rounding(b):
                dve.wait_ge(S["ww_ok"], b + 1)
                dve.scalar_tensor_tensor(out=zz[:, :, :].rearrange("p c t -> p (c t)"),
                                         in0=ww[:, :, :].rearrange("p c t -> p (c t)"), scalar=-1.0,
                                         in1=zz[:, :, :].rearrange("p c t -> p (c t)"), op0=ALU.add, op1=ALU.subtract)\
                   .then_inc(S["nc_ok"], 1)

            def first_steps():
                dve.wait_ge(S["nc_ok"], 1)
                dve.wait_ge(S["rv_ok"], 2)
                dve.tensor_tensor(dt[0][:, :, :], dt[0][:, :, :], zz[:, :, :], ALU.subtract).then_inc(S["tv_ok"], 1)
                dve.wait_ge(S["tv_ok"], 1)
                dve.wait_ge(S["lw_ok"], 1)
                dve.tensor_tensor(dt[0][:, :, :], dt[0][:, :, :], lw[:, :, :], ALU.add).then_inc(S["dt_ok"], 1)

            def front_dtu(b):
                dve.wait_ge(S["dt_ok"], b + 1)
                dve.wait_ge(S["u_ok"], 2 * b + 2)
                if b >= 2:
                    dve.wait_ge(S["dBu_ok"], (b - 1) * NS)
                dve.tensor_tensor(dtu[b % 2][:, :, :], dt[b % 2][:, :, :], u[:, :, :], ALU.mult)\
                   .then_inc(S["dtu_ok"], 1)

            def inject(n):
                b, s = divmod(n, NS)
                if s == 0:
                    dve.wait_ge(S["dtu_ok"], b + 1)
                dve.wait_ge(S["Bb_mm"], n + 1)
                if n >= 2:
                    dve.wait_ge(S["h_ok"], 2 * (n - 1))
                dve.tensor_tensor(dBu[n % 2][:, :, :], dtu[b % 2][:, :, :],
                                  psB[:, :].unsqueeze(1).broadcast_to([P, NC, L]), ALU.mult).then_inc(S["dBu_ok"], 1)

            def scan(n):
                dve.wait_ge(S["dBu_ok"], n + 1)
                if n >= AHEAD:
                    dve.wait_ge(S["hC_ok"], n - AHEAD + 1)
                for c in range(NC):
                    dve.wait_ge(S["dA_ok"], 2 * n + c + 1)
                    dve.tensor_tensor_scan(hs[n % AHEAD][:, c, :], dA[n % AHEAD][:, c, :], dBu[n % 2][:, c, :], 0.0,
                                           ALU.mult, ALU.add).then_inc(S["h_ok"], 1)

            def tail_yz(b):
                dve.wait_ge(S["sum_mm"], (b + 1) * NS)
                if b:
                    dve.wait_ge(S["yzT_mm"], 2 * b)
                for i in range(2):
                    t = dve.tensor_tensor(yz[:, 2 * i:2 * i + 2, :], psY[:, 2 * i:2 * i + 2, :],
                                          zs[b % 2][:, 2 * i:2 * i + 2, :], ALU.mult)
                t.then_inc(S["yz_ok"], 1)

            def tail_x1(b):
                dve.wait_ge(S["op_mm"], b + 1)
                dve.wait_ge(S["xres_ok"], b + 1)
                if b:
                    dve.wait_ge(S["base_ok"], b)
                if b:
                    dve.wait_ge(S["xe_ok"], b)
                dve.tensor_tensor(x1[:, :, :].rearrange("p j d -> p (j d)"), psF[0][:, :],
                                  xres[b % 2][:, :, :].rearrange("p j d -> p (j d)"), ALU.add).then_inc(S["x1_ok"], 1)
                dve.wait_ge(S["x1_ok"], b + 1)
                moments(x1, bst2, mv2, vv2, S["vv2_ok"])

            def tail_norm(b):
                dve.wait_ge(S["y2_ok"], b + 1)
                newton(vv2, yy2, rs2)
                dve.tensor_scalar(nr[:, 0, :], rs2[:, 0, :], 1.0, None, ALU.add)
                dve.scalar_tensor_tensor(out=nr[:, 1, :], in0=mv2[:, :, 0], scalar=-1.0, in1=rs2[:, 0, :],
                                         op0=ALU.mult, op1=ALU.mult).then_inc(S["nr_ok"], 1)
                link(dve.tensor_tensor(nr[:, 2, :], rs2[:, 0, :], rs2[:, 1, :], ALU.mult))
                link(dve.tensor_tensor(nr[:, 2, :], nr[:, 2, :], vv2[:, 1, :], ALU.mult))
                if b == 0:
                    dve.wait_ge(S["tiles_zero"], 16 * sum(len(c) for c in CHUNKS))
                for j in range(TB):
                    t = dve.tensor_scalar(xe[b][:, j, :], x1[:, j, :], mv2[:, j, 0:1], rs2[:, 1, j:j + 1],
                                          ALU.subtract, ALU.mult)
                t.then_inc(S["xe_ok"], 1)

            def tail_choose(b):
                dve.wait_ge(S["aff_mm"], b + 1)
                link(dve.tensor_tensor(aff[:, :, :], psF[0][:, 0:TB * E].rearrange("p (j e) -> p j e", e=E),
                                       nr[:, 2, :].unsqueeze(2).broadcast_to([P, TB, E]), ALU.mult))
                if b:
                    dve.wait_ge(S["gex_ok"], b)
                dve.tensor_reduce(mx[:, :], aff[:, :, :], AX.X, ALU.max).then_inc(S["mx_ok"], 1)
                dve.wait_ge(S["mx_ok"], b + 1)
                link(dve.tensor_tensor(score[:, :, :], aff[:, :, :], mx[:, :].unsqueeze(2).broadcast_to([P, TB, E]),
                                       ALU.is_ge))
                link(dve.tensor_tensor(score[:, :, :], score[:, :, :], firstw[:, :, :], ALU.mult))
                link(dve.tensor_reduce(mx2[:, :], score[:, :, :], AX.X, ALU.max))
                dve.tensor_tensor(hot[b][:, :, :], score[:, :, :], mx2[:, :].unsqueeze(2).broadcast_to([P, TB, E]),
                                  ALU.is_equal).then_inc(S["hot_ok"], 1)
                dve.wait_ge(S["hot_ok"], b + 1)
                if b:
                    dve.wait_ge(S["rank_mm"], b)
                dve.tensor_copy(hot16[:, :, :], hot[b][:, :, :]).then_inc(S["hot16_ok"], 1)

            def tail_gate(b):
                dve.wait_ge(S["gex_ok"], b + 1)
                g = gate[b]
                link(dve.tensor_scalar(g[:, :], gex[:, :], 1.0, None, ALU.add))
                dve.reciprocal(g[:, :], g[:, :]).then_inc(S["gate_ok"], 1)

            def tail_rank(b):
                before_b = not any(b == g[0] for g in GROUPS)
                dve.wait_ge(S["rank_mm"], b + 1)
                ranks = psF[0][:, 0:TB * E].rearrange("p (j e) -> p j e", e=E)
                counts = psF[0][:, TB * E:(TB + 1) * E]
                if before_b:
                    link(dve.tensor_tensor(place[:, :, :], ranks,
                                           count[b - 1][:, :].unsqueeze(1).broadcast_to([P, TB, E]), ALU.add))
                    dve.tensor_tensor(count[b][:, :], counts, count[b - 1][:, :], ALU.add).then_inc(S["rank_ok"], 1)
                    link(dve.tensor_tensor(place[:, :, :], place[:, :, :], hot[b][:, :, :], ALU.mult))
                else:
                    link(dve.tensor_tensor(place[:, :, :], ranks, hot[b][:, :, :], ALU.mult))
                    dve.tensor_copy(count[b][:, :], counts).then_inc(S["rank_ok"], 1)
                link(dve.tensor_reduce(rank[b][:, :], place[:, :, :], AX.X, ALU.add))

            def route(g):
                n_rounds, n_tiles = ROUNDS[g], NT[g]
                dve.wait_ge(S["rank_ok"], GROUPS[g][-1] + 1)
                link(dve.tensor_tensor(more[:, :, 0:n_rounds],
                                       count[GROUPS[g][-1]][:, :].unsqueeze(2).broadcast_to([P, E, n_rounds]),
                                       rounds[:, :, 0:n_rounds], ALU.is_gt))
                link(dve.tensor_reduce(tiles[:, :], more[:, :, 0:n_rounds], AX.X, ALU.add))
                link(dve.tensor_tensor_scan(ends[:, :], one_e[:, :], tiles[:, :], 0.0, ALU.mult, ALU.add))
                link(dve.tensor_scalar(ends128[:, :], ends[:, :], float(P), None, ALU.mult))
                link(dve.scalar_tensor_tensor(out=start[:, :], in0=tiles[:, :], scalar=-float(P), in1=ends128[:, :],
                                              op0=ALU.mult, op1=ALU.add))
                for b in GROUPS[g]:
                    link(dve.tensor_tensor(place[:, :, :], start[:, :].unsqueeze(1).broadcast_to([P, TB, E]),
                                           hot[b][:, :, :], ALU.mult))
                    link(dve.tensor_reduce(slotf[:, :], place[:, :, :], AX.X, ALU.add))
                    dve.tensor_tensor(slot[b][:, :], slotf[:, :], rank[b][:, :], ALU.add).then_inc(S["slot_ok"], 1)
                    dve.wait_ge(S["slot_ok"], b + 1)
                link(dve.tensor_tensor(past[:, 0:n_tiles, :], ends[0:1, :].unsqueeze(1).broadcast_to([1, n_tiles, E]),
                                       tile_no[:, 0:n_tiles, :], ALU.is_le))
                link(dve.tensor_reduce(te_f[:, 0:n_tiles], past[:, 0:n_tiles, :], AX.X, ALU.add))
                dve.tensor_scalar(te[g][:, :], te_f[:, 0:n_tiles], float(E - 1), None, ALU.min).then_inc(S["te_ok"], 1)

            def tail_b2(b):
                dve.wait_ge(S["b2_mm"], b + 1)
                dve.wait_ge(S["base_ok"], b + 1)
                dve.wait_ge(S["gate_ok"], b + 1)
                for j in range(TB):
                    t = dve.scalar_tensor_tensor(out=base[b][:, j, :], in0=psF[0][:, j * DM:(j + 1) * DM],
                                                 scalar=gate[b][:, j:j + 1], in1=base[b][:, j, :],
                                                 op0=ALU.mult, op1=ALU.add)
                t.then_inc(S["b2_ok"], 1)

            def finish(b):
                dve.wait_ge(S["b2_ok"], b + 1)
                for j in range(TB):
                    dve.wait_ge(gathered[b][j], 16)
                    dve.scalar_tensor_tensor(out=res[b][:, j, :], in0=yg[b][:, j, :], scalar=gate[b][:, j:j + 1],
                                             in1=base[b][:, j, :], op0=ALU.mult, op1=ALU.add)\
                       .then_inc(S["res_ok"], 1)

            have = dict(tail_moments=tail_x1, tail_norm=tail_norm, tail_choose=tail_choose,
                        tail_gate=tail_gate, tail_rank=tail_rank, route=route, tail_bias=tail_b2,
                        finish=finish, split_b1=split_b1, gamma_w1=gamma_w1,
                        front_moments=front_moments, front_norm=front_norm, front_low=front_low,
                        front_parts=front_parts,
                        front_rounding=front_rounding, front_dtu=front_dtu)
            weights_0()
            front_moments(0)
            front_norm(0)
            weights_1()
            front_low(0)
            front_parts(0)
            front_rounding(0)
            first_steps()
            front_dtu(0)
            inject(0)
            for n in range(LAST + 1):
                if n + 1 < B * NS:
                    inject(n + 1)
                if NS < n < B * NS and n % NS == LAG:
                    tail_yz(n // NS - 1)
                if n == B * NS:
                    tail_yz(B - 1)
                if n < B * NS:
                    scan(n)
                steps(n, have)

        @block.gpsimd
        def _(pool):
            pool.memset(ident[:, :], 0.0).then_inc(S["ident_ok"], 1)
            pool.memset(pick32[:, :], 0.0).then_inc(S["pick_ok"], 1)
            pool.wait_ge(S["ident_ok"], 1)
            pool.affine_select(out=ident[:, :], in_=ident[:, :], compare_op=ALU.not_equal, fill=1.0, base=0,
                               pattern=[[-1, P]], channel_multiplier=1).then_inc(S["ident_ok"], 1)
            for i in range(3):
                pool.wait_ge(S["pick_ok"], i + 1)
                pool.affine_select(out=pick32[:, :], in_=pick32[:, :], compare_op=ALU.not_equal, fill=1.0,
                                   base=-BC * i, pattern=[[-1, BC]], channel_multiplier=1).then_inc(S["pick_ok"], 1)
            for dst, src, name in (
                    (alog[:, :, :], A_log.rearrange("(c p) s -> p c s", p=P), "alog_in"),
                    (xp_raw[:, :], x_proj_w, "xp_in"),
                    (dtw_raw[:, :, :], dt_proj_w.rearrange("(c p) r -> p c r", p=P), "dtw_in"),
                    (wo_raw[:, :], out_proj_w, "wo_in"),
                    (b2_sb[:, :], b2, "b2_in")):
                pool.dma_start(dst, src).then_inc(S[name], 16)
            pool.memset(before32[:, :], 1.0).then_inc(S["before_ok"], 1)
            pool.wait_ge(S["before_ok"], 1)
            pool.affine_select(out=before32[:, :], in_=before32[:, :], compare_op=ALU.is_gt, fill=0.0, base=0,
                               pattern=[[1, P]], channel_multiplier=-1).then_inc(S["before_ok"], 1)

            flat = "p c t -> p (c t)"

            def front_sub(b):
                pool.wait_ge(S["nc_ok"], b + 1)
                pool.wait_ge(S["rv_ok"], 2 * b + 2)
                pool.tensor_tensor(dt[b % 2][:, :, :].rearrange(flat), dt[b % 2][:, :, :].rearrange(flat),
                                   zz[:, :, :].rearrange(flat), ALU.subtract).then_inc(S["tv_ok"], 1)

            def front_add(b):
                pool.wait_ge(S["tv_ok"], b + 1)
                pool.wait_ge(S["lw_ok"], b + 1)
                pool.tensor_tensor(dt[b % 2][:, :, :].rearrange(flat), dt[b % 2][:, :, :].rearrange(flat),
                                   lw[:, :, :].rearrange(flat), ALU.add).then_inc(S["dt_ok"], 1)

            def read_out(n):
                pool.wait_ge(S["Cb_ok"], n + 1)
                pool.wait_ge(S["h_ok"], 2 * n + 2)
                if n >= AHEAD:
                    pool.wait_ge(S["sum_mm"], n - AHEAD + 1)
                pool.tensor_tensor(hC[n % AHEAD][:, :, :], hs[n % AHEAD][:, :, :],
                                   Cb[n % AHEAD][:, :].unsqueeze(1).broadcast_to([P, NC, L]), ALU.mult)\
                    .then_inc(S["hC_ok"], 1)

            def scatter(block_of_rows):
                b, j = block_of_rows
                g = [b in group for group in GROUPS].index(True)
                if b == 0 and j == 0:
                    pool.wait_ge(S["tiles_zero"], 16 * sum(len(c) for c in CHUNKS))
                if j == 0:
                    pool.wait_ge(S["slot_ok"], b + 1)
                    pool.wait_ge(S["xe_ok"], b + 1)
                pool.indirect_dma_start(
                    out=x_tiles[g], out_offset=bass.IndirectOffsetOnAxis(ap=slot[b][:, j:j + 1], axis=0),
                    in_=xe[b][:, j, :], in_offset=None).then_inc(scattered[g], 16)

            def gather(b):
                g = [b in group for group in GROUPS].index(True)
                pool.wait_ge(y_stored[g], 16 * len(CHUNKS[g]))
                pool.wait_ge(scattered[g], 16 * TB * len(GROUPS[g]))
                for j in range(TB):
                    pool.indirect_dma_start(
                        out=yg[b][:, j, :], out_offset=None, in_=y_tiles[g],
                        in_offset=bass.IndirectOffsetOnAxis(ap=slot[b][:, j:j + 1], axis=0))\
                        .then_inc(gathered[b][j], 16)

            have = dict(scatter=scatter, gather=gather, front_sub=front_sub, front_add=front_add)
            for n in range(LAST + 1):
                if n < B * NS:
                    read_out(n)
                steps(n, have)


_INS = ['L0_attn_x', 'L0_attn_ln_gamma', 'L0_attn_ln_beta', 'L0_attn_in_proj_w', 'L0_attn_conv_w', 'L0_attn_conv_b',
        'L0_attn_x_proj_w', 'L0_attn_dt_proj_w', 'L0_attn_dt_proj_b', 'L0_attn_A_log', 'L0_attn_D',
        'L0_attn_out_proj_w', 'L0_ffn_centroids', 'L0_ffn_ln_g', 'L0_ffn_ln_b', 'L0_ffn_w1', 'L0_ffn_b1', 'L0_ffn_w2',
        'L0_ffn_b2']
_OUTS = [((4, 512, 128), 'float32')]


def kernel(**inputs):
    import numpy as _np
    import concourse.bacc as _bacc
    from concourse import mybir as _mybir
    from concourse.bass_utils import run_bass_kernel_spmd as _run

    nc = _bacc.Bacc("TRN2", target_bir_lowering=False, num_devices=1)
    arrays, args = {}, []
    for name in _INS:
        a = _np.ascontiguousarray(inputs[name])
        arrays[f"in_{name}_dram"] = a
        args.append(nc.dram_tensor(f"in_{name}_dram", a.shape, _mybir.dt.from_np(a.dtype), kind="ExternalInput").ap())
    for i, (shape, dtype) in enumerate(_OUTS):
        dt = _mybir.dt.from_np(_np.dtype(dtype))
        args.append(nc.dram_tensor(f"out_{i}_dram", shape, dt, kind="ExternalOutput").ap())
    build(nc, *args)
    r = _run(nc, [arrays], core_ids=[0])
    got = tuple(r.results[0][f"out_{i}_dram"] for i in range(len(_OUTS)))
    return got[0]
```
